# Optimizing a Trainium2 kernel written in Bass

```python
import numpy as np
import jax
import jax.numpy as jnp

def _softmax(x, axis=-1):
    return jax.nn.softmax(x, axis=axis)

def _gelu(x):
    return jax.nn.gelu(x, approximate=True)

def _silu(x):
    return jax.nn.silu(x)

def _sigmoid(x):
    return jax.nn.sigmoid(x)

def _layernorm(x, axis=-1, eps=1e-05):
    m = jnp.mean(x, axis=axis, keepdims=True)
    v = jnp.var(x, axis=axis, keepdims=True)
    return (x - m) / jnp.sqrt(v + eps)

def _scatter_add(tgt, idx, src, axis=0):
    return tgt.at[idx].add(src)

def _segment_sum(src, seg, n):
    return jax.ops.segment_sum(src, seg, n)
kernel_name = 'mk_decoder_preln_d4_seqx_r4_cb49b8'

def setup_inputs(seed: int=0):
    np.random.seed(seed)
    _w = jnp.asarray

    def _rec_inputs():
        import jax
        import jax.numpy as jnp
        _rk = jax.random.key(seed)
        x = 7.22e-05 + 1 * jax.random.normal(jax.random.fold_in(_rk, 1), (16, 112, 256), jnp.float32)
        _lenS = 112 - jax.random.randint(jax.random.fold_in(_rk, 7), (16,), 0, max(1, 112 // 4) + 1, jnp.int32)
        _lenS2 = 375 - jax.random.randint(jax.random.fold_in(_rk, 8), (16,), 0, max(1, 375 // 4) + 1, jnp.int32)
        _ctx_1024P = jax.random.normal(jax.random.fold_in(_rk, 11), (16, 16, 256), jnp.float32)
        _ctx_1024c = jax.random.dirichlet(jax.random.fold_in(_rk, 511), 0.3 * jnp.ones((16,), jnp.float32), (16, 375))
        _ctx_1024t = jnp.einsum('bsk,bkd->bsd', _ctx_1024c, _ctx_1024P)
        _ctx_1024t = _ctx_1024t * jax.lax.rsqrt(jnp.mean(jnp.square(_ctx_1024t)) + 1e-12) * 0.953939
        ctx_1024 = 4.13588e-05 + 0.999923 * (_ctx_1024t + 0.3 * jax.random.normal(jax.random.fold_in(_rk, 611), (16, 375, 256), jnp.float32))
        fside_BxS2_0 = 0.0132156 + 1.00766 * jax.random.normal(jax.random.fold_in(_rk, 13), (16, 375), jnp.float32)
        _validS = jnp.arange(112)[None, :] < _lenS[:, None]
        _validS2 = jnp.arange(375)[None, :] < _lenS2[:, None]
        _causal = jnp.tril(jnp.ones((112, 112), dtype=bool))
        mask_BxS2_if1 = jnp.where(jnp.ones((16, 375), dtype=bool), 1, 0).astype(jnp.int32)
        mask_BxS2_bk0 = jnp.logical_not(jnp.broadcast_to(_validS2[:, :], (16, 375)))
        return (x, ctx_1024, fside_BxS2_0, mask_BxS2_if1, mask_BxS2_bk0)
    x, ctx_1024, fside_BxS2_0, mask_BxS2_if1, mask_BxS2_bk0 = _rec_inputs()

    def _L0_attn_setup():
        import jax, jax.numpy as jnp
        import numpy as np
        DIM = 256
        DIM_HEADS = 64
        key = jax.random.key(seed)
        k1, k2, k3 = jax.random.split(key, 3)
        x = jax.random.normal(k1, (1, 512, DIM), dtype=jnp.float32)
        w_qkv = jax.random.normal(k2, (DIM_HEADS * 3, DIM), dtype=jnp.float32) * 0.02
        w_out = jax.random.normal(k3, (DIM, DIM_HEADS), dtype=jnp.float32) * 0.02
        return {'x': x, 'w_qkv': w_qkv, 'w_out': w_out}
    _L0_attn_all = _L0_attn_setup()
    _L0_attn_in = {k: v for k, v in _L0_attn_all.items() if k in ('w_qkv', 'w_out')}
    del _L0_attn_all

    def _L0_xattn_setup():
        import jax, jax.numpy as jnp
        import numpy as np
        HEADS = 16
        DIM_HEAD = 64
        QUERY_DIM = 256
        CONTEXT_DIM = 256
        INNER = HEADS * DIM_HEAD
        key = jax.random.key(seed)
        k1, k2, k3, k4, k5, k6, k7 = jax.random.split(key, 7)
        B, N, M = (4, 512, 512)
        s = 0.02
        return {'x': jax.random.normal(k1, (B, N, QUERY_DIM), jnp.float32), 'context': jax.random.normal(k2, (B, M, CONTEXT_DIM), jnp.float32), 'Wq': jax.random.normal(k3, (INNER, QUERY_DIM), jnp.float32) * s, 'Wk': jax.random.normal(k4, (INNER, CONTEXT_DIM), jnp.float32) * s, 'Wv': jax.random.normal(k5, (INNER, CONTEXT_DIM), jnp.float32) * s, 'Wo': jax.random.normal(k6, (QUERY_DIM, INNER), jnp.float32) * s, 'bo': jax.random.normal(k7, (QUERY_DIM,), jnp.float32) * s}
    _L0_xattn_all = _L0_xattn_setup()
    _L0_xattn_in = {k: v for k, v in _L0_xattn_all.items() if k in ('Wq', 'Wk', 'Wv', 'Wo', 'bo')}
    del _L0_xattn_all

    def _L0_ffn_setup():
        import jax, jax.numpy as jnp
        import numpy as np
        DIM = 256
        HID = 512
        OUT = 256
        NE = 8
        TOPK = 2

        def _xavier(key, shape):
            fan_in, fan_out = (shape[-2], shape[-1])
            lim = jnp.sqrt(6.0 / (fan_in + fan_out))
            return jax.random.uniform(key, shape, jnp.float32, -lim, lim)
        key = jax.random.key(seed)
        ks = jax.random.split(key, 8)
        X = jax.random.normal(ks[0], (4, 256, DIM), jnp.float32)
        W1 = _xavier(ks[1], (NE, DIM, HID))
        W3 = _xavier(ks[2], (NE, DIM, HID))
        W2 = _xavier(ks[3], (NE, HID, OUT))
        b1 = jnp.zeros((NE, HID), jnp.float32)
        b3 = jnp.zeros((NE, HID), jnp.float32)
        b2 = jnp.zeros((NE, OUT), jnp.float32)
        Wg = _xavier(ks[4], (DIM, NE))
        bg = jnp.zeros((NE,), jnp.float32)
        Wf = _xavier(ks[5], (OUT, OUT))
        bf = jnp.zeros((OUT,), jnp.float32)
        return {'X': X, 'W1': W1, 'b1': b1, 'W3': W3, 'b3': b3, 'W2': W2, 'b2': b2, 'Wg': Wg, 'bg': bg, 'Wf': Wf, 'bf': bf}
    _L0_ffn_all = _L0_ffn_setup()
    _L0_ffn_in = {k: v for k, v in _L0_ffn_all.items() if k in ('W1', 'b1', 'W3', 'b3', 'W2', 'b2', 'Wg', 'bg', 'Wf', 'bf')}
    del _L0_ffn_all

    def _L1_attn_setup():
        import jax, jax.numpy as jnp
        import numpy as np
        import math
        _OFFSETS = sorted(set(range(0, 33)) | {48, 64, 96, 128, 192, 64, 96, 128, 192, 256, 384})
        B, N, D, H, FFN = (1, 512, 256, 16, 704)
        EPS = 1e-06

        def _rmsnorm(x, scale):
            rms = jnp.sqrt(jnp.mean(x * x, axis=-1, keepdims=True) + EPS)
            return scale * (x / rms)
        key = jax.random.key(seed)
        ks = jax.random.split(key, 8)
        s = 0.02
        alphas = jnp.linspace(0.2, 2.0, H)
        delta_vals = jnp.array([math.log(1.0 + max(d, 0.2)) for d in _OFFSETS], dtype=jnp.float32)
        pos_bias = -delta_vals[:, None] * alphas[None, :]
        return {'x': jax.random.normal(ks[0], (B, N, D), jnp.float32), 'norm1_scale': jnp.ones((D,), jnp.float32), 'norm2_scale': jnp.ones((D,), jnp.float32), 'w_qkv': jax.random.normal(ks[1], (D, 3 * D), jnp.float32) * s, 'w_out': jax.random.normal(ks[2], (D, D), jnp.float32) * s, 'w_gate': jax.random.normal(ks[3], (D, D), jnp.float32) * s, 'b_gate': jnp.full((D,), 2.0, jnp.float32), 'pos_bias': pos_bias, 'w_ffn_gate': jax.random.normal(ks[4], (D, FFN), jnp.float32) * s, 'w_ffn_up': jax.random.normal(ks[5], (D, FFN), jnp.float32) * s, 'w_ffn_down': jax.random.normal(ks[6], (FFN, D), jnp.float32) * s, 'offsets': jnp.array(_OFFSETS, dtype=jnp.int32)}
    _L1_attn_all = _L1_attn_setup()
    _L1_attn_in = {k: v for k, v in _L1_attn_all.items() if k in ('norm1_scale', 'norm2_scale', 'w_qkv', 'w_out', 'w_gate', 'b_gate', 'pos_bias', 'w_ffn_gate', 'w_ffn_up', 'w_ffn_down', 'offsets')}
    del _L1_attn_all

    def _L1_xattn_setup():
        import jax, jax.numpy as jnp
        import numpy as np
        B, S, D = (4, 512, 256)
        KEY_DIM, VALUE_DIM = (256, 256)
        BETA = 1.0 / np.sqrt(D)
        key = jax.random.key(seed)
        ks = jax.random.split(key, 9)
        inv = 1.0 / np.sqrt(D)
        return {'query': jax.random.normal(ks[0], (B, S, D), dtype=jnp.float32), 'key': jax.random.normal(ks[1], (B, S, D), dtype=jnp.float32), 'value': jax.random.normal(ks[2], (B, S, D), dtype=jnp.float32), 'Wq': jax.random.normal(ks[3], (D, KEY_DIM), dtype=jnp.float32) * inv, 'bq': jnp.zeros((KEY_DIM,), dtype=jnp.float32), 'Wk': jax.random.normal(ks[4], (D, KEY_DIM), dtype=jnp.float32) * inv, 'bk': jnp.zeros((KEY_DIM,), dtype=jnp.float32), 'Wv': jax.random.normal(ks[5], (D, VALUE_DIM), dtype=jnp.float32) * inv, 'bv': jnp.zeros((VALUE_DIM,), dtype=jnp.float32)}
    _L1_xattn_all = _L1_xattn_setup()
    _L1_xattn_in = {k: v for k, v in _L1_xattn_all.items() if k in ('Wq', 'bq', 'Wk', 'bk', 'Wv', 'bv')}
    del _L1_xattn_all

    def _L1_ffn_setup():
        import math
        import jax, jax.numpy as jnp
        import numpy as np
        B, L, D, F_FF, E = (4, 512, 256, 1024, 8)
        TOP_K = 1
        CAPACITY_FACTOR = 1.25
        key = jax.random.key(seed)
        ks = jax.random.split(key, 4)
        h = jax.random.normal(ks[0], (B, L, D), dtype=jnp.float32)
        gate_w = jax.random.normal(ks[1], (E, D), dtype=jnp.float32) * 0.02
        gate_b = jnp.zeros((E,), dtype=jnp.float32)
        w1 = jax.random.normal(ks[2], (E, D, F_FF), dtype=jnp.float32) * 0.02
        b1 = jnp.zeros((E, F_FF), dtype=jnp.float32)
        w2 = jax.random.normal(ks[3], (E, F_FF, D), dtype=jnp.float32) * 0.02
        b2 = jnp.zeros((E, D), dtype=jnp.float32)
        return {'h': h, 'gate_w': gate_w, 'gate_b': gate_b, 'w1': w1, 'b1': b1, 'w2': w2, 'b2': b2}
    _L1_ffn_all = _L1_ffn_setup()
    _L1_ffn_in = {k: v for k, v in _L1_ffn_all.items() if k in ('gate_w', 'gate_b', 'w1', 'b1', 'w2', 'b2')}
    del _L1_ffn_all

    def _L2_attn_setup():
        import math
        import jax, jax.numpy as jnp
        import numpy as np
        HEADS = 16
        REL_WINDOW = 128
        key = jax.random.key(seed)
        k1, k2, k3, k4, k5 = jax.random.split(key, 5)
        b, s, d = (2, 512, 256)
        hd = d // HEADS
        R = 2 * REL_WINDOW + 1
        return {'x': jax.random.normal(k1, (b, s, d), dtype=jnp.float32), 'Wqkv': jax.random.normal(k2, (3 * d, d), dtype=jnp.float32) * (1.0 / math.sqrt(d)), 'bqkv': jax.random.normal(k3, (3 * d,), dtype=jnp.float32) * 0.02, 'Wr': jax.random.normal(k4, (R, hd), dtype=jnp.float32) * (1.0 / math.sqrt(hd)), 'br': jax.random.normal(k5, (R,), dtype=jnp.float32) * 0.02}
    _L2_attn_all = _L2_attn_setup()
    _L2_attn_in = {k: v for k, v in _L2_attn_all.items() if k in ('Wqkv', 'bqkv', 'Wr', 'br')}
    del _L2_attn_all

    def _L2_xattn_setup():
        import jax, jax.numpy as jnp
        import numpy as np
        D_MODEL = 256
        N_HEADS = 16
        HEAD_DIM = D_MODEL // N_HEADS
        key = jax.random.key(seed)
        ks = jax.random.split(key, 10)
        B, LQ, LKV = (4, 256, 512)
        inv = 1.0 / np.sqrt(D_MODEL)
        inp = {'query': jax.random.normal(ks[0], (B, LQ, D_MODEL), dtype=jnp.float32), 'key_value': jax.random.normal(ks[1], (B, LKV, D_MODEL), dtype=jnp.float32), 'attention_mask': jnp.ones((B, LKV), dtype=jnp.int32), 'Wq': jax.random.normal(ks[2], (D_MODEL, D_MODEL), dtype=jnp.float32) * inv, 'bq': jnp.zeros((D_MODEL,), dtype=jnp.float32), 'Wk': jax.random.normal(ks[3], (D_MODEL, D_MODEL), dtype=jnp.float32) * inv, 'bk': jnp.zeros((D_MODEL,), dtype=jnp.float32), 'Wv': jax.random.normal(ks[4], (D_MODEL, D_MODEL), dtype=jnp.float32) * inv, 'bv': jnp.zeros((D_MODEL,), dtype=jnp.float32), 'Wo': jax.random.normal(ks[5], (D_MODEL, D_MODEL), dtype=jnp.float32) * inv, 'bo': jnp.zeros((D_MODEL,), dtype=jnp.float32)}
        return inp
    _L2_xattn_all = _L2_xattn_setup()
    _L2_xattn_in = {k: v for k, v in _L2_xattn_all.items() if k in ('Wq', 'bq', 'Wk', 'bk', 'Wv', 'bv', 'Wo', 'bo')}
    del _L2_xattn_all

    def _L2_ffn_setup():
        import jax, jax.numpy as jnp
        import numpy as np
        B, S, D, H, E = (4, 512, 256, 512, 8)
        key = jax.random.key(seed)
        ks = jax.random.split(key, 8)
        scale = 0.02
        return {'x': jax.random.normal(ks[0], (B, S, D), dtype=jnp.float32), 'Wr': jax.random.normal(ks[1], (D, E), dtype=jnp.float32) * scale, 'br': jnp.zeros((E,), dtype=jnp.float32), 'W1': jax.random.normal(ks[2], (E, D, H), dtype=jnp.float32) * scale, 'b1': jnp.zeros((E, H), dtype=jnp.float32), 'W2': jax.random.normal(ks[3], (E, H, D), dtype=jnp.float32) * scale, 'b2': jnp.zeros((E, D), dtype=jnp.float32)}
    _L2_ffn_all = _L2_ffn_setup()
    _L2_ffn_in = {k: v for k, v in _L2_ffn_all.items() if k in ('Wr', 'br', 'W1', 'b1', 'W2', 'b2')}
    del _L2_ffn_all

    def _L3_attn_setup():
        import jax, jax.numpy as jnp
        import numpy as np
        B, T, D = (4, 512, 256)
        key = jax.random.key(seed)
        kx, kq, kk, kv = jax.random.split(key, 4)
        scale = 1.0 / np.sqrt(D)
        return {'x': jax.random.normal(kx, (B, T, D), dtype=jnp.float32), 'Wq': jax.random.normal(kq, (D, D), dtype=jnp.float32) * scale, 'Wk': jax.random.normal(kk, (D, D), dtype=jnp.float32) * scale, 'Wv': jax.random.normal(kv, (D, D), dtype=jnp.float32) * scale}
    _L3_attn_all = _L3_attn_setup()
    _L3_attn_in = {k: v for k, v in _L3_attn_all.items() if k in ('Wq', 'Wk', 'Wv')}
    del _L3_attn_all

    def _L3_xattn_setup():
        import jax, jax.numpy as jnp
        import numpy as np
        EMBED_DIM = 256
        NUM_HEADS = 16
        HEAD_DIM = EMBED_DIM // NUM_HEADS
        B, SQ, SK = (2, 512, 512)
        key = jax.random.key(seed)
        ks = jax.random.split(key, 10)
        s = 1.0 / np.sqrt(EMBED_DIM)
        return {'tgt': jax.random.normal(ks[0], (B, SQ, EMBED_DIM), jnp.float32), 'mem': jax.random.normal(ks[1], (B, SK, EMBED_DIM), jnp.float32), 'attn_bias': jax.random.normal(ks[2], (B, SK), jnp.float32), 'memory_key_padding_mask': jax.random.randint(ks[3], (B, SK), 0, 2).astype(bool), 'Wq_w': jax.random.normal(ks[4], (EMBED_DIM, EMBED_DIM), jnp.float32) * s, 'Wq_b': jnp.zeros((EMBED_DIM,), jnp.float32), 'Wkv_w': jax.random.normal(ks[5], (2 * EMBED_DIM, EMBED_DIM), jnp.float32) * s, 'Wkv_b': jnp.zeros((2 * EMBED_DIM,), jnp.float32), 'out_w': jax.random.normal(ks[6], (EMBED_DIM, EMBED_DIM), jnp.float32) * s, 'out_b': jnp.zeros((EMBED_DIM,), jnp.float32)}
    _L3_xattn_all = _L3_xattn_setup()
    _L3_xattn_in = {k: v for k, v in _L3_xattn_all.items() if k in ('Wq_w', 'Wq_b', 'Wkv_w', 'Wkv_b', 'out_w', 'out_b')}
    del _L3_xattn_all

    def _L3_ffn_setup():
        import jax, jax.numpy as jnp
        import numpy as np
        HIDDEN = 256
        INTER = 512
        NUM_EXPERTS = 8
        TOPK = 2
        STD = 0.02
        key = jax.random.key(seed)
        k1, k2, k3, k4 = jax.random.split(key, 4)
        return {'hidden_states': jax.random.normal(k1, (1, 512, HIDDEN), dtype=jnp.float32), 'w1': jax.random.normal(k2, (NUM_EXPERTS, 2 * INTER, HIDDEN), dtype=jnp.float32) * STD, 'w2': jax.random.normal(k3, (NUM_EXPERTS, HIDDEN, INTER), dtype=jnp.float32) * STD, 'router_w': jax.random.normal(k4, (NUM_EXPERTS, HIDDEN), dtype=jnp.float32) * STD}
    _L3_ffn_all = _L3_ffn_setup()
    _L3_ffn_in = {k: v for k, v in _L3_ffn_all.items() if k in ('w1', 'w2', 'router_w')}
    del _L3_ffn_all
    return {'x': x, 'ctx_1024': ctx_1024, 'fside_BxS2_0': fside_BxS2_0, 'mask_BxS2_if1': mask_BxS2_if1, 'mask_BxS2_bk0': mask_BxS2_bk0, 'L0_attn_w_qkv': _L0_attn_in['w_qkv'], 'L0_attn_w_out': _L0_attn_in['w_out'], 'L0_xattn_Wq': _L0_xattn_in['Wq'], 'L0_xattn_Wk': _L0_xattn_in['Wk'], 'L0_xattn_Wv': _L0_xattn_in['Wv'], 'L0_xattn_Wo': _L0_xattn_in['Wo'], 'L0_xattn_bo': _L0_xattn_in['bo'], 'L0_ffn_W1': _L0_ffn_in['W1'], 'L0_ffn_b1': _L0_ffn_in['b1'], 'L0_ffn_W3': _L0_ffn_in['W3'], 'L0_ffn_b3': _L0_ffn_in['b3'], 'L0_ffn_W2': _L0_ffn_in['W2'], 'L0_ffn_b2': _L0_ffn_in['b2'], 'L0_ffn_Wg': _L0_ffn_in['Wg'], 'L0_ffn_bg': _L0_ffn_in['bg'], 'L0_ffn_Wf': _L0_ffn_in['Wf'], 'L0_ffn_bf': _L0_ffn_in['bf'], 'L1_attn_norm1_scale': _L1_attn_in['norm1_scale'], 'L1_attn_norm2_scale': _L1_attn_in['norm2_scale'], 'L1_attn_w_qkv': _L1_attn_in['w_qkv'], 'L1_attn_w_out': _L1_attn_in['w_out'], 'L1_attn_w_gate': _L1_attn_in['w_gate'], 'L1_attn_b_gate': _L1_attn_in['b_gate'], 'L1_attn_pos_bias': _L1_attn_in['pos_bias'], 'L1_attn_w_ffn_gate': _L1_attn_in['w_ffn_gate'], 'L1_attn_w_ffn_up': _L1_attn_in['w_ffn_up'], 'L1_attn_w_ffn_down': _L1_attn_in['w_ffn_down'], 'L1_attn_offsets': _L1_attn_in['offsets'], 'L1_xattn_Wq': _L1_xattn_in['Wq'], 'L1_xattn_bq': _L1_xattn_in['bq'], 'L1_xattn_Wk': _L1_xattn_in['Wk'], 'L1_xattn_bk': _L1_xattn_in['bk'], 'L1_xattn_Wv': _L1_xattn_in['Wv'], 'L1_xattn_bv': _L1_xattn_in['bv'], 'L1_ffn_gate_w': _L1_ffn_in['gate_w'], 'L1_ffn_gate_b': _L1_ffn_in['gate_b'], 'L1_ffn_w1': _L1_ffn_in['w1'], 'L1_ffn_b1': _L1_ffn_in['b1'], 'L1_ffn_w2': _L1_ffn_in['w2'], 'L1_ffn_b2': _L1_ffn_in['b2'], 'L2_attn_Wqkv': _L2_attn_in['Wqkv'], 'L2_attn_bqkv': _L2_attn_in['bqkv'], 'L2_attn_Wr': _L2_attn_in['Wr'], 'L2_attn_br': _L2_attn_in['br'], 'L2_xattn_Wq': _L2_xattn_in['Wq'], 'L2_xattn_bq': _L2_xattn_in['bq'], 'L2_xattn_Wk': _L2_xattn_in['Wk'], 'L2_xattn_bk': _L2_xattn_in['bk'], 'L2_xattn_Wv': _L2_xattn_in['Wv'], 'L2_xattn_bv': _L2_xattn_in['bv'], 'L2_xattn_Wo': _L2_xattn_in['Wo'], 'L2_xattn_bo': _L2_xattn_in['bo'], 'L2_ffn_Wr': _L2_ffn_in['Wr'], 'L2_ffn_br': _L2_ffn_in['br'], 'L2_ffn_W1': _L2_ffn_in['W1'], 'L2_ffn_b1': _L2_ffn_in['b1'], 'L2_ffn_W2': _L2_ffn_in['W2'], 'L2_ffn_b2': _L2_ffn_in['b2'], 'L3_attn_Wq': _L3_attn_in['Wq'], 'L3_attn_Wk': _L3_attn_in['Wk'], 'L3_attn_Wv': _L3_attn_in['Wv'], 'L3_xattn_Wq_w': _L3_xattn_in['Wq_w'], 'L3_xattn_Wq_b': _L3_xattn_in['Wq_b'], 'L3_xattn_Wkv_w': _L3_xattn_in['Wkv_w'], 'L3_xattn_Wkv_b': _L3_xattn_in['Wkv_b'], 'L3_xattn_out_w': _L3_xattn_in['out_w'], 'L3_xattn_out_b': _L3_xattn_in['out_b'], 'L3_ffn_w1': _L3_ffn_in['w1'], 'L3_ffn_w2': _L3_ffn_in['w2'], 'L3_ffn_router_w': _L3_ffn_in['router_w']}

def reference(x, ctx_1024, fside_BxS2_0, mask_BxS2_if1, mask_BxS2_bk0, L0_attn_w_qkv, L0_attn_w_out, L0_xattn_Wq, L0_xattn_Wk, L0_xattn_Wv, L0_xattn_Wo, L0_xattn_bo, L0_ffn_W1, L0_ffn_b1, L0_ffn_W3, L0_ffn_b3, L0_ffn_W2, L0_ffn_b2, L0_ffn_Wg, L0_ffn_bg, L0_ffn_Wf, L0_ffn_bf, L1_attn_norm1_scale, L1_attn_norm2_scale, L1_attn_w_qkv, L1_attn_w_out, L1_attn_w_gate, L1_attn_b_gate, L1_attn_pos_bias, L1_attn_w_ffn_gate, L1_attn_w_ffn_up, L1_attn_w_ffn_down, L1_attn_offsets, L1_xattn_Wq, L1_xattn_bq, L1_xattn_Wk, L1_xattn_bk, L1_xattn_Wv, L1_xattn_bv, L1_ffn_gate_w, L1_ffn_gate_b, L1_ffn_w1, L1_ffn_b1, L1_ffn_w2, L1_ffn_b2, L2_attn_Wqkv, L2_attn_bqkv, L2_attn_Wr, L2_attn_br, L2_xattn_Wq, L2_xattn_bq, L2_xattn_Wk, L2_xattn_bk, L2_xattn_Wv, L2_xattn_bv, L2_xattn_Wo, L2_xattn_bo, L2_ffn_Wr, L2_ffn_br, L2_ffn_W1, L2_ffn_b1, L2_ffn_W2, L2_ffn_b2, L3_attn_Wq, L3_attn_Wk, L3_attn_Wv, L3_xattn_Wq_w, L3_xattn_Wq_b, L3_xattn_Wkv_w, L3_xattn_Wkv_b, L3_xattn_out_w, L3_xattn_out_b, L3_ffn_w1, L3_ffn_w2, L3_ffn_router_w):
    import jax
    import jax.numpy as jnp

    def _L0_attn_ref(x, w_qkv, w_out):
        import jax, jax.numpy as jnp
        import numpy as np
        DIM = 256
        DIM_HEADS = 64
        b, n, _ = x.shape
        h = DIM_HEADS
        qkv = jnp.einsum('bnc,fc->bnf', x, w_qkv)
        q, k, v = jnp.split(qkv, 3, axis=-1)
        q = q.transpose(0, 2, 1)[..., None]
        k = k.transpose(0, 2, 1)[..., None]
        v = v.transpose(0, 2, 1)[..., None]
        scale = 1.0 / jnp.sqrt(jnp.float32(h))
        dots = jnp.einsum('bhid,bhjd->bhij', q, k) * scale
        causal = jnp.tril(jnp.ones((n, n), dtype=bool))
        dots = jnp.where(causal, dots, -jnp.inf)
        attn = jax.nn.softmax(dots, axis=-1)
        out = jnp.einsum('bhij,bhjd->bhid', attn, v)
        out = out[..., 0].transpose(0, 2, 1)
        return jnp.einsum('bnh,ch->bnc', out, w_out)

    def _L0_xattn_ref(x, context, Wq, Wk, Wv, Wo, bo):
        import jax, jax.numpy as jnp
        import numpy as np
        HEADS = 16
        DIM_HEAD = 64
        QUERY_DIM = 256
        CONTEXT_DIM = 256
        INNER = HEADS * DIM_HEAD
        B, N, _ = x.shape
        M = context.shape[1]
        scale = DIM_HEAD ** (-0.5)
        q = jnp.einsum('bnd,ed->bne', x, Wq)
        k = jnp.einsum('bmd,ed->bme', context, Wk)
        v = jnp.einsum('bmd,ed->bme', context, Wv)
        q = q.reshape(B, N, HEADS, DIM_HEAD).transpose(0, 2, 1, 3)
        k = k.reshape(B, M, HEADS, DIM_HEAD).transpose(0, 2, 1, 3)
        v = v.reshape(B, M, HEADS, DIM_HEAD).transpose(0, 2, 1, 3)
        sim = jnp.einsum('bhid,bhjd->bhij', q, k) * scale
        attn = jax.nn.softmax(sim, axis=-1)
        out = jnp.einsum('bhij,bhjd->bhid', attn, v)
        out = out.transpose(0, 2, 1, 3).reshape(B, N, INNER)
        return jnp.einsum('bne,oe->bno', out, Wo) + bo

    def _L0_ffn_ref(X, W1, b1, W3, b3, W2, b2, Wg, bg, Wf, bf):
        import jax, jax.numpy as jnp
        import numpy as np
        DIM = 256
        HID = 512
        OUT = 256
        NE = 8
        TOPK = 2

        def _xavier(key, shape):
            fan_in, fan_out = (shape[-2], shape[-1])
            lim = jnp.sqrt(6.0 / (fan_in + fan_out))
            return jax.random.uniform(key, shape, jnp.float32, -lim, lim)
        gating = jax.nn.softmax(X @ Wg + bg, axis=-1)
        top_k_indices = jnp.argsort(gating, axis=-1)[..., -TOPK:]
        h1 = jnp.einsum('bsd,edh->bseh', X, W1) + b1
        h3 = jnp.einsum('bsd,edh->bseh', X, W3) + b3
        h = jax.nn.silu(h1 * h3)
        expert_outputs = jnp.einsum('bseh,eho->bseo', h, W2) + b2
        topk_out = jnp.take_along_axis(expert_outputs, top_k_indices[..., None], axis=2)
        topk_w = jnp.take_along_axis(gating, top_k_indices, axis=-1)
        mixed = jnp.sum(topk_w[..., None] * topk_out, axis=2)
        return mixed @ Wf + bf

    def _L1_attn_ref(x, norm1_scale, norm2_scale, w_qkv, w_out, w_gate, b_gate, pos_bias, w_ffn_gate, w_ffn_up, w_ffn_down, offsets):
        import jax, jax.numpy as jnp
        import numpy as np
        import math
        _OFFSETS = sorted(set(range(0, 33)) | {48, 64, 96, 128, 192, 64, 96, 128, 192, 256, 384})
        B, N, D, H, FFN = (1, 512, 256, 16, 704)
        EPS = 1e-06

        def _rmsnorm(x, scale):
            rms = jnp.sqrt(jnp.mean(x * x, axis=-1, keepdims=True) + EPS)
            return scale * (x / rms)
        Bx, Nx, Dx = x.shape
        HD = Dx // H
        xn = _rmsnorm(x, norm1_scale)
        qkv = xn @ w_qkv
        q, k, v = jnp.split(qkv, 3, axis=-1)
        to_heads = lambda t: t.reshape(Bx, Nx, H, HD).transpose(0, 2, 1, 3)
        q, k, v = (to_heads(q), to_heads(k), to_heads(v))
        t_idx = jnp.arange(Nx)
        src = jnp.clip(t_idx[:, None] - offsets[None, :], 0, None)
        Kg = k[:, :, src, :]
        Vg = v[:, :, src, :]
        scale = HD ** (-0.5)
        scores = jnp.einsum('bhnd,bhnod->bhno', q, Kg) * scale
        scores = scores + pos_bias.T[None, :, None, :]
        invalid = t_idx[:, None] < offsets[None, :]
        scores = jnp.where(invalid[None, None], -jnp.inf, scores)
        alpha = jax.nn.softmax(scores, axis=-1)
        out = jnp.einsum('bhno,bhnod->bhnd', alpha, Vg)
        out = out.transpose(0, 2, 1, 3).reshape(Bx, Nx, Dx)
        gate = jax.nn.sigmoid(xn @ w_gate + b_gate)
        x = x + out * gate @ w_out
        xn2 = _rmsnorm(x, norm2_scale)
        x = x + jax.nn.silu(xn2 @ w_ffn_gate) * (xn2 @ w_ffn_up) @ w_ffn_down
        return x

    def _L1_xattn_ref(query, key, value, Wq, bq, Wk, bk, Wv, bv):
        import jax, jax.numpy as jnp
        import numpy as np
        B, S, D = (4, 512, 256)
        KEY_DIM, VALUE_DIM = (256, 256)
        BETA = 1.0 / np.sqrt(D)
        q = query @ Wq + bq
        k = key @ Wk + bk
        v = value @ Wv + bv
        scores = jnp.einsum('bik,bjk->bij', q, k)
        A = jax.nn.softmax(BETA * scores, axis=-1)
        return jnp.einsum('bij,bjk->bik', A, v)

    def _L1_ffn_ref(h, gate_w, gate_b, w1, b1, w2, b2):
        import math
        import jax, jax.numpy as jnp
        import numpy as np
        B, L, D, F_FF, E = (4, 512, 256, 1024, 8)
        TOP_K = 1
        CAPACITY_FACTOR = 1.25
        Bh, Lh, Dh = h.shape
        T = Bh * Lh
        capacity = max(1, math.ceil(CAPACITY_FACTOR * (T * TOP_K / E)))
        x = h.reshape(T, Dh)
        logits = x @ gate_w.T + gate_b
        probs = jax.nn.softmax(logits, axis=-1)
        idx = jnp.argmax(probs, axis=-1)
        top_prob = jnp.max(probs, axis=-1)
        one_hot = jax.nn.one_hot(idx, E, dtype=jnp.int32)
        pos = jnp.take_along_axis(jnp.cumsum(one_hot, axis=0), idx[:, None], axis=1)[:, 0] - 1
        keep = pos < capacity
        safe_pos = jnp.where(keep, pos, 0)
        buf = jnp.zeros((E, capacity, Dh), dtype=x.dtype)
        buf = buf.at[idx, safe_pos].add(x * keep[:, None].astype(x.dtype))
        hdn = jax.nn.relu(jnp.einsum('ecd,edf->ecf', buf, w1) + b1[:, None, :])
        eout = jnp.einsum('ecf,efd->ecd', hdn, w2) + b2[:, None, :]
        gathered = eout[idx, safe_pos]
        out = gathered * (top_prob * keep.astype(x.dtype))[:, None]
        return out.reshape(Bh, Lh, Dh)

    def _L2_attn_ref(x, Wqkv, bqkv, Wr, br):
        import math
        import jax, jax.numpy as jnp
        import numpy as np
        HEADS = 16
        REL_WINDOW = 128
        b, s, d = x.shape
        h = HEADS
        hd = d // h
        w = REL_WINDOW
        scale = math.sqrt(d / h)
        qkv = (x @ Wqkv.T + bqkv).reshape(b, s, h, 3 * hd)
        q, k, v = jnp.split(qkv, 3, axis=-1)
        q = q.transpose(0, 2, 1, 3)
        k = k.transpose(0, 2, 1, 3)
        v = v.transpose(0, 2, 1, 3)
        content = jnp.einsum('bhik,bhjk->bhij', q, k) / scale
        idx = jnp.arange(s)
        offsets = jnp.clip(idx[None, :] - idx[:, None], -w, w) + w
        rp = jnp.einsum('bhik,rk->bhir', q, Wr) + br
        pos = jnp.take_along_axis(rp, jnp.broadcast_to(offsets, (b, h, s, s)), axis=-1)
        attn = jax.nn.softmax(content + pos, axis=-1)
        out = jnp.einsum('bhij,bhjk->bhik', attn, v)
        return out.transpose(0, 2, 1, 3).reshape(b, s, d)

    def _L2_xattn_ref(query, key_value, attention_mask, Wq, bq, Wk, bk, Wv, bv, Wo, bo):
        import jax, jax.numpy as jnp
        import numpy as np
        D_MODEL = 256
        N_HEADS = 16
        HEAD_DIM = D_MODEL // N_HEADS
        B, LQ, _ = query.shape
        LKV = key_value.shape[1]
        scale = HEAD_DIM ** (-0.5)
        q = (query @ Wq + bq).reshape(B, LQ, N_HEADS, HEAD_DIM).transpose(0, 2, 1, 3)
        k = (key_value @ Wk + bk).reshape(B, LKV, N_HEADS, HEAD_DIM).transpose(0, 2, 1, 3)
        v = (key_value @ Wv + bv).reshape(B, LKV, N_HEADS, HEAD_DIM).transpose(0, 2, 1, 3)
        scores = jnp.einsum('bhqd,bhkd->bhqk', q, k) * scale
        mask = (attention_mask != 0)[:, None, None, :]
        scores = jnp.where(mask, scores, -jnp.inf)
        attn = jax.nn.softmax(scores, axis=-1)
        context = jnp.einsum('bhqk,bhkd->bhqd', attn, v)
        context = context.transpose(0, 2, 1, 3).reshape(B, LQ, D_MODEL)
        return context @ Wo + bo

    def _L2_ffn_ref(x, Wr, br, W1, b1, W2, b2):
        import jax, jax.numpy as jnp
        import numpy as np
        B, S, D, H, E = (4, 512, 256, 512, 8)
        d = x.shape[-1]
        tokens = x.reshape(-1, d)
        logits = tokens @ Wr + br
        probs = jax.nn.softmax(logits, axis=-1)
        expert = jnp.argmax(probs, axis=-1)
        max_prob = jnp.take_along_axis(probs, expert[:, None], axis=-1)
        h = jax.nn.relu(jnp.einsum('td,edh->teh', tokens, W1) + b1[None])
        y = jnp.einsum('teh,ehd->ted', h, W2) + b2[None]
        out = jnp.take_along_axis(y, expert[:, None, None], axis=1)[:, 0, :]
        return (out * max_prob).reshape(x.shape)

    def _L3_attn_ref(x, Wq, Wk, Wv):
        import jax, jax.numpy as jnp
        import numpy as np
        B, T, D = (4, 512, 256)
        q = jnp.einsum('btd,od->bto', x, Wq)
        k = jnp.einsum('btd,od->bto', x, Wk)
        v = jnp.einsum('btd,od->bto', x, Wv)
        scores = jnp.einsum('bqd,bkd->bqk', q, k)
        inv_sqrt_d = 1.0 / np.sqrt(k.shape[-1]).astype(np.float32)
        weights = jax.nn.softmax(scores * inv_sqrt_d, axis=-1)
        return jnp.einsum('bqk,bkd->bqd', weights, v)

    def _L3_xattn_ref(tgt, mem, attn_bias, memory_key_padding_mask, Wq_w, Wq_b, Wkv_w, Wkv_b, out_w, out_b):
        import jax, jax.numpy as jnp
        import numpy as np
        EMBED_DIM = 256
        NUM_HEADS = 16
        HEAD_DIM = EMBED_DIM // NUM_HEADS
        B, SQ, SK = (2, 512, 512)
        b, sq, _ = tgt.shape
        sk = mem.shape[1]
        q = (tgt @ Wq_w.T + Wq_b).reshape(b, sq, NUM_HEADS, HEAD_DIM)
        kv = (mem @ Wkv_w.T + Wkv_b).reshape(b, sk, 2, NUM_HEADS, HEAD_DIM)
        k, v = (kv[:, :, 0], kv[:, :, 1])
        scale = 1.0 / np.sqrt(HEAD_DIM)
        scores = jnp.einsum('bthd,bshd->bhts', q, k * scale)
        scores = scores + attn_bias[:, None, None, :]
        pad = jnp.where(memory_key_padding_mask, 0.0, -jnp.inf).astype(scores.dtype)
        scores = scores + pad[:, None, None, :]
        attn = jax.nn.softmax(scores, axis=-1)
        ctx = jnp.einsum('bhts,bshd->bthd', attn, v)
        out = ctx.reshape(b, sq, EMBED_DIM) @ out_w.T + out_b
        return out

    def _L3_ffn_ref(hidden_states, w1, w2, router_w):
        import jax, jax.numpy as jnp
        import numpy as np
        HIDDEN = 256
        INTER = 512
        NUM_EXPERTS = 8
        TOPK = 2
        STD = 0.02
        orig_shape = hidden_states.shape
        dtype = hidden_states.dtype
        x = hidden_states.reshape(-1, orig_shape[-1])
        E = w1.shape[0]
        gating = x @ router_w.T
        probs = jax.nn.softmax(gating.astype(jnp.float32), axis=-1)
        topk_w, sel = jax.lax.top_k(probs, TOPK)
        topk_w = topk_w.astype(dtype)
        combine = (jax.nn.one_hot(sel, E, dtype=dtype) * topk_w[..., None]).sum(axis=1)
        h = jnp.einsum('td,eid->tei', x, w1)
        gate = jax.nn.silu(h[..., :INTER])
        y = h[..., INTER:] * gate
        out = jnp.einsum('tei,ehi,te->th', y, w2, combine)
        return out.reshape(orig_shape)
    x = x + _L0_attn_ref(_layernorm(x, axis=-1), L0_attn_w_qkv, L0_attn_w_out)
    x = x + _L0_xattn_ref(_layernorm(x, axis=-1), ctx_1024, L0_xattn_Wq, L0_xattn_Wk, L0_xattn_Wv, L0_xattn_Wo, L0_xattn_bo)
    x = x + _L0_ffn_ref(_layernorm(x, axis=-1), L0_ffn_W1, L0_ffn_b1, L0_ffn_W3, L0_ffn_b3, L0_ffn_W2, L0_ffn_b2, L0_ffn_Wg, L0_ffn_bg, L0_ffn_Wf, L0_ffn_bf)
    x = x + _L1_attn_ref(_layernorm(x, axis=-1), L1_attn_norm1_scale, L1_attn_norm2_scale, L1_attn_w_qkv, L1_attn_w_out, L1_attn_w_gate, L1_attn_b_gate, L1_attn_pos_bias, L1_attn_w_ffn_gate, L1_attn_w_ffn_up, L1_attn_w_ffn_down, L1_attn_offsets)
    x = x + _L1_xattn_ref(_layernorm(x, axis=-1), ctx_1024, ctx_1024, L1_xattn_Wq, L1_xattn_bq, L1_xattn_Wk, L1_xattn_bk, L1_xattn_Wv, L1_xattn_bv)
    x = x + _L1_ffn_ref(_layernorm(x, axis=-1), L1_ffn_gate_w, L1_ffn_gate_b, L1_ffn_w1, L1_ffn_b1, L1_ffn_w2, L1_ffn_b2)
    x = x + _L2_attn_ref(_layernorm(x, axis=-1), L2_attn_Wqkv, L2_attn_bqkv, L2_attn_Wr, L2_attn_br)
    x = x + _L2_xattn_ref(_layernorm(x, axis=-1), ctx_1024, mask_BxS2_if1, L2_xattn_Wq, L2_xattn_bq, L2_xattn_Wk, L2_xattn_bk, L2_xattn_Wv, L2_xattn_bv, L2_xattn_Wo, L2_xattn_bo)
    x = x + _L2_ffn_ref(_layernorm(x, axis=-1), L2_ffn_Wr, L2_ffn_br, L2_ffn_W1, L2_ffn_b1, L2_ffn_W2, L2_ffn_b2)
    x = x + _L3_attn_ref(_layernorm(x, axis=-1), L3_attn_Wq, L3_attn_Wk, L3_attn_Wv)
    x = x + _L3_xattn_ref(_layernorm(x, axis=-1), ctx_1024, fside_BxS2_0, mask_BxS2_bk0, L3_xattn_Wq_w, L3_xattn_Wq_b, L3_xattn_Wkv_w, L3_xattn_Wkv_b, L3_xattn_out_w, L3_xattn_out_b)
    x = x + _L3_ffn_ref(_layernorm(x, axis=-1), L3_ffn_w1, L3_ffn_w2, L3_ffn_router_w)
    return x

_drawn_inputs = setup_inputs


def setup_inputs(seed=0):
    import zlib

    import numpy as np

    out = dict(_drawn_inputs(seed))
    spreads = {'L0_ffn_b1': (0.0, 0.295),
     'L0_ffn_b3': (0.0, 0.298),
     'L0_ffn_b2': (0.0, 0.1),
     'L0_ffn_bg': (0.0, 0.1),
     'L0_ffn_bf': (0.0, 0.1),
     'L1_attn_norm1_scale': (1.0, 0.6),
     'L1_attn_norm2_scale': (1.0, 0.6),
     'L1_attn_b_gate': (2.0, 0.6),
     'L1_xattn_bq': (0.0, 0.716),
     'L1_xattn_bk': (0.0, 0.8),
     'L1_xattn_bv': (0.0, 0.1),
     'L1_ffn_gate_b': (0.0, 0.8),
     'L1_ffn_b1': (0.0, 0.8),
     'L1_ffn_b2': (0.0, 0.8),
     'L2_xattn_bq': (0.0, 0.745),
     'L2_xattn_bk': (0.0, 0.8),
     'L2_xattn_bv': (0.0, 0.1),
     'L2_xattn_bo': (0.0, 0.1),
     'L2_ffn_br': (0.0, 0.8),
     'L2_ffn_b1': (0.0, 0.8),
     'L2_ffn_b2': (0.0, 0.8),
     'L3_xattn_Wq_b': (0.0, 0.741),
     'L3_xattn_Wkv_b': (0.0, 0.1),
     'L3_xattn_out_b': (0.0, 0.1)}
    factors = {'L0_attn_w_qkv': 4.079,
     'L0_attn_w_out': 4.012,
     'L0_xattn_Wq': 7.274,
     'L0_xattn_Wk': 6.958,
     'L1_attn_w_qkv': 3.139,
     'L1_attn_w_out': 3.145,
     'L1_attn_w_gate': 8.0,
     'L1_attn_pos_bias': 4.029,
     'L1_attn_w_ffn_gate': 3.976,
     'L1_attn_w_ffn_up': 3.921,
     'L1_attn_w_ffn_down': 3.936,
     'L1_ffn_gate_w': 3.775,
     'L1_ffn_w1': 5.174,
     'L1_ffn_w2': 4.103,
     'L2_attn_bqkv': 5.208,
     'L2_attn_br': 8.0,
     'L2_ffn_Wr': 4.871,
     'L2_ffn_W1': 7.724,
     'L2_ffn_W2': 6.236,
     'L3_ffn_w1': 8.0,
     'L3_ffn_w2': 8.0,
     'L3_ffn_router_w': 8.0}
    for name, (base, spread) in spreads.items():
        noise = np.random.default_rng([zlib.crc32(name.encode()), seed]).standard_normal(out[name].shape)
        drawn = base * np.exp(spread * noise) if base else spread * noise
        out[name] = jnp.asarray(drawn.astype(out[name].dtype))
    for name, factor in factors.items():
        out[name] = (out[name] * factor).astype(out[name].dtype)
    return out
```

```python
from contextlib import ExitStack

import concourse.bass as bass
from concourse import mybir

F32 = mybir.dt.float32
I32 = mybir.dt.int32
U8 = mybir.dt.uint8
ACT = mybir.ActivationFunctionType
ALU = mybir.AluOpType
AX_X = mybir.AxisListType.X

NB = 16
T = 112
D = 256
KD = D // 128
SK = 375
KC = 125
NKC = SK // KC
NE = 8
NPAIR = NB // 2
RELS = 2 * T - 1
REL_WINDOW = 128
MASKED = -1.0e30
LN_EPS = 1e-5
RMS_EPS = 1e-6
CAPACITY = -(-(5 * NB * T) // (4 * NE))


def wait(eng, sem, value):
    if isinstance(value, int) and value <= 0:
        return
    eng.wait_ge(sem, value)


def reuse(b, n, per, ring, uses=None):
    uses = per if uses is None else uses
    if n >= ring:
        return b * per + n - ring + 1
    last = n + (uses - 1 - n) // ring * ring
    return (b - 1) * per + last + 1


def over_batches(eng, body):
    for u in range(2):
        body(u, u, 0)
    with eng.Fori(1, NPAIR) as i:
        for u in range(2):
            body(i * 2 + u, u, i)


class Phase:

    def __init__(self, nc, name):
        self.nc, self.name, self.ctx, self.sems = nc, name, ExitStack(), []

    def __enter__(self):
        return self

    def sb(self, name, shape, dt=F32):
        return self.ctx.enter_context(self.nc.sbuf_tensor(f"{self.name}_{name}", shape, dt))

    def ps(self, name, shape):
        return self.ctx.enter_context(self.nc.psum_tensor(f"{self.name}_{name}", shape, F32))

    def sem(self, name):
        s = self.ctx.enter_context(self.nc.semaphore(f"{self.name}_{name}"))
        self.sems.append(s)
        return s

    def __exit__(self, *exc):
        if exc[0] is None:
            for s in self.sems:
                self.nc.gpsimd.sem_clear(s)
            self.nc.all_engine_barrier()
        self.ctx.close()


def batch(t, b):
    return t[0:T, bass.ds(b, 1), :].rearrange("p b d -> p (b d)")


def column(t, b):
    return t[0:T, bass.ds(b, 1)]


def row_bcast(ap, n):
    return ap.rearrange("(a n) -> a n", a=1).broadcast_to([n, ap.shape[0]])



class Norm:
    def __init__(self, p, x, kind):
        self.x, self.kind = x, kind
        self.st = p.sb("bn", [T, NB, 6])
        self.w = p.sb("bnw", [T, 6, NB])
        self.mean = p.sb("mean", [T, NB])
        self.var = p.sb("var", [T, NB])
        self.rstd = p.sb("rstd", [T, NB])
        self.rms = p.sb("rms", [T, NB])
        self.std = p.sb("std", [T, 2, NB])
        self.rows_done = p.sem("bn_rows")
        self.steps = p.sem("bn_steps")
        self.to_sqrt = p.sem("to_sqrt")
        self.sqrt_done = p.sem("sqrt_done")

    def vector(self, v):
        with v.Fori(0, NB) as b:
            v.bn_stats(self.st[:, bass.ds(b, 1), :].rearrange("p b s -> p (b s)"), batch(self.x, b)).then_inc(self.rows_done, 1)
        v.wait_ge(self.rows_done, NB)
        me, qe, mo, qo = (self.st[:, :, k] for k in (1, 2, 4, 5))
        s, d, q, d2, ve, ms = (self.w[:, k, :] for k in range(6))
        n = 0

        def chain(ins):
            nonlocal n
            n += 1
            ins.then_inc(self.steps, 1)
            v.wait_ge(self.steps, n)

        v.tensor_tensor(s, me, mo, ALU.add).then_inc(self.steps, 1)
        v.tensor_tensor(d, me, mo, ALU.subtract).then_inc(self.steps, 1)
        n += 2
        chain(v.tensor_tensor(q, qe, qo, ALU.add))
        chain(v.scalar_tensor_tensor(d2, d, 0.25, d, ALU.mult, ALU.mult))
        v.tensor_scalar(self.mean[:], s, 0.5, None, ALU.mult).then_inc(self.steps, 1)
        n += 1
        chain(v.scalar_tensor_tensor(self.var[:], q, 1.0 / D, d2, ALU.mult, ALU.add))
        if self.kind != "rms":
            v.tensor_scalar(ve, self.var[:], LN_EPS, None, ALU.add).then_inc(self.to_sqrt, 1)
            v.wait_ge(self.sqrt_done, 1)
            chain(v.reciprocal(self.rstd[:], self.std[:, 0, :]))
        if self.kind == "ln_rms":
            chain(v.tensor_tensor(ms, self.var[:], self.rstd[:], ALU.mult))
            chain(v.tensor_tensor(ms, ms, self.rstd[:], ALU.mult))
        if self.kind == "rms":
            chain(v.tensor_tensor(ms, self.mean[:], self.mean[:], ALU.mult))
            chain(v.tensor_tensor(ms, ms, self.var[:], ALU.add))
        if self.kind != "ln":
            k = 2 if self.kind == "ln_rms" else 1
            v.tensor_scalar(ve, ms, RMS_EPS, None, ALU.add).then_inc(self.to_sqrt, 1)
            v.wait_ge(self.sqrt_done, k)
            chain(v.reciprocal(self.rms[:], self.std[:, 1, :]))

    def scalar(self, a):
        which = {"ln": (0,), "ln_rms": (0, 1), "rms": (1,)}[self.kind]
        for n, k in enumerate(which):
            a.wait_ge(self.to_sqrt, n + 1)
            a.activation(self.std[:, k, :], self.w[:, 4, :], ACT.Sqrt).then_inc(self.sqrt_done, 1)

    def rows(self, v, b, out, done, h=None, h_done=None, scale_row=None):
        if self.kind == "ln":
            v.tensor_scalar(out, batch(self.x, b), column(self.mean, b), column(self.rstd, b),
                            ALU.subtract, ALU.mult).then_inc(done, 1)
            return
        if self.kind == "ln_rms":
            v.tensor_scalar(batch(h, b), batch(self.x, b), column(self.mean, b), column(self.rstd, b),
                            ALU.subtract, ALU.mult).then_inc(h_done, 1)
            v.wait_ge(h_done, b + 1)
        v.scalar_tensor_tensor(out, batch(h, b), column(self.rms, b), scale_row,
                               ALU.mult, ALU.mult).then_inc(done, 1)



def attention(nc, name, x, K, *, heads, dh, dv, wq, wk, wv, scale, ctxT=None, bq=None, bk=None, bv=None,
              wo=None, bo=None, maskrow=None, addend=None, pos_dram=None, gate=None, norm="ln",
              norm_scale=None, y=None):
    cross = ctxT is not None
    G = wq.shape[1] // 128
    S = SK if cross else T
    kc, nkc = (KC, NKC) if cross else (T, 1)
    DV = heads * dv
    per_group = max(1, 128 // max(32, dh))
    slot = 128 // per_group
    rows = min(dh, 128) + (1 if maskrow is not None else 0)
    HU = 1 if cross or heads == 1 else 4
    if HU == 1:
        units = [[h] for h in range(heads)]
    else:
        units = [[per_group * g + j for g in range(heads // per_group)] for j in range(per_group)]
    NU = len(units)
    has_add = addend is not None or pos_dram is not None
    QPB = min(G, 4)
    NQ = G // QPB
    VW = min(DV, 512)
    NV = DV // VW
    jobs = [("x", 0)] + [("q", n) for n in range(NQ)]
    jobs += [("k", g) for g in range(G)] if cross else [("k", 0)]
    jobs += [("v", c * NV + n) for c in range(nkc) for n in range(NV)]
    jobs += [("g", 0)] if gate else []
    NPP = len(jobs)
    NBLK = DV // 128
    NTT = -(-NBLK // 4) if wo is not None else 0
    NT = NU + (NTT + 1 if wo is not None else 0)
    dest = x if y is None else y
    norm_p = 4
    ident, ones, indcol = K["ident"], K["ones"], K["indcol"]

    with Phase(nc, name) as p:
        wq_sb = p.sb("wq", [128, KD, G * 128])
        wk_sb = p.sb("wk", [128, KD, G * 128])
        wv_sb = p.sb("wv", [128, KD, DV])
        wo_sb = p.sb("wo", [128, NBLK, D]) if wo is not None else None
        bq_sb = p.sb("bq", [128, G]) if bq is not None else None
        bk_sb = p.sb("bk", [128, G]) if bk is not None else None
        bv_sb = p.sb("bv", [T, DV]) if bv is not None else None
        bo_sb = p.sb("bo", [1, D]) if bo is not None else None
        gw_sb = p.sb("gw", [128, KD, D]) if gate else None
        gb_sb = p.sb("gb", [1, D]) if gate else None
        gate_sb = p.sb("gate", [T, 2, D]) if gate else None
        gate_w = p.sb("gate_w", [T, 2, D]) if gate else None
        ns_sb = p.sb("ns", [T, D]) if norm_scale is not None else None
        ctx_sb = p.sb("ctx", [128, 2, KD, SK]) if cross else None
        pos_sb = p.sb("pos", [T, 2, heads, T]) if pos_dram is not None else None
        xn = p.sb("xn", [T, 2, D])
        xnT = p.sb("xnT", [128, 2, KD, T])
        qT = p.sb("qT", [128, 2, G, T])
        kT = p.sb("kT", [128, 2, G, S])
        vs = p.sb("v", [kc, 2, nkc, DV])
        logit = p.sb("logit", [T, 2, HU, S]) if has_add else None
        probs = p.sb("probs", [T, 4, HU, S])
        pT = p.sb("pT", [kc, 2, HU * nkc, T])
        nmax = p.sb("nmax", [T, 2, NU, HU])
        den = p.sb("den", [T, 2, NU, HU])
        rden = p.sb("rden", [T, 2, NU, HU])
        o_sb = p.sb("o", [T, 2, DV])
        oT = p.sb("oT", [128, NBLK, T]) if wo is not None else None

        pp = p.ps("pp", [128, 2, 512])
        sc = p.ps("sc", [128, 2, 512])
        tr = p.ps("tr", [128, 2, 512])
        po = p.ps("po", [128, 2, 512])

        st = Norm(p, x, norm)
        loaded = p.sem("loaded")
        n_loads = 0
        scaled = p.sem("scaled")
        ctx_in = [p.sem(f"ctx_in{u}") for u in range(2)]
        pos_in = [p.sem(f"pos_in{u}") for u in range(2)]
        xn_ready = p.sem("xn_ready")
        h_done = p.sem("h_done")
        pp_ready = p.sem("pp_ready")
        pp_empty = p.sem("pp_empty")
        s_ready = p.sem("s_ready")
        l_ready = p.sem("l_ready")
        m_ready = p.sem("m_ready")
        e_ready = p.sem("e_ready")
        t_ready = p.sem("t_ready")
        t_empty = p.sem("t_empty")
        pv_done = p.sem("pv_done")
        rden_ready = p.sem("rden_ready")
        o_norm = p.sem("o_norm")
        o_bias = p.sem("o_bias")
        o_ready = p.sem("o_ready")
        g_steps = p.sem("g_steps")
        x_done = p.sem("x_done")

        loads = [(wq_sb[:], wq.rearrange("(k p) n -> p k n", p=128)),
                 (wk_sb[:], wk.rearrange("(k p) n -> p k n", p=128)),
                 (wv_sb[:], wv.rearrange("(k p) n -> p k n", p=128))]
        if bq is not None:
            loads.append((bq_sb[:], bq))
        if bk is not None:
            loads.append((bk_sb[:], bk))
        if bv is not None:
            loads.append((bv_sb[:], row_bcast(bv, T)))
        if wo is not None:
            loads.append((wo_sb[:], wo.rearrange("(k p) n -> p k n", p=128)))
        if bo is not None:
            loads.append((bo_sb[:], bo.rearrange("(a n) -> a n", a=1)))
        if gate:
            loads.append((gw_sb[:], gate[0].rearrange("(k p) n -> p k n", p=128)))
            loads.append((gb_sb[:], gate[1].rearrange("(a n) -> a n", a=1)))
        if norm_scale is not None:
            loads.append((ns_sb[:], row_bcast(norm_scale, T)))
        n_loads = len(loads)
        n_scaled = 2 if bq is not None else 1

        def o_cols(u, h):
            if DV > 512:
                return po[0:T, h * dv // 512, h * dv % 512:h * dv % 512 + dv]
            return po[0:T, u, h * dv:(h + 1) * dv]

        def o_all(u):
            return po[0:T, :, :].rearrange("p a n -> p (a n)") if DV > 512 else po[0:T, u, 0:DV]

        with nc.Block() as block:

            @block.sync
            def _(sp):
                for dst, src in loads:
                    sp.dma_start(dst, src).then_inc(loaded, 16)
                if not cross and pos_dram is None:
                    return

                def body(b, u, i):
                    if cross:
                        wait(sp, pp_ready, (b - 1) * NPP)
                        sp.dma_start(ctx_sb[:, u, :, :], ctxT[bass.ds(b, 1)].rearrange("b (k p) s -> p (b k) s", p=128)).then_inc(ctx_in[u], 16)
                    if pos_dram is not None:
                        wait(sp, l_ready, (b - 1) * NU)
                        sp.dma_start(pos_sb[:, u, :, :], pos_dram(b)).then_inc(pos_in[u], 16)

                over_batches(sp, body)

            @block.tensor
            def _(pe):
                pe.wait_ge(loaded, 16 * n_loads)
                pe.wait_ge(scaled, n_scaled)

                def project(b, u, i):
                    for j, (kind, n) in enumerate(jobs):
                        bank = pp[:, j % 2, :]
                        wait(pe, pp_empty, reuse(b, j, NPP, 2))
                        kv_src = ctx_sb[:, u] if cross else xnT[:, u]
                        if kind == "x":
                            pe.wait_ge(xn_ready, b + 1)
                            for k in range(KD):
                                last = pe.transpose(bank[:, k * T:(k + 1) * T], xn[:, u, k * 128:(k + 1) * 128], ident[0:T, 0:T])
                        if kind == "q":
                            if n == 0:
                                pe.wait_ge(pp_empty, b * NPP + 1)
                            for q in range(QPB):
                                for k in range(KD):
                                    g = n * QPB + q
                                    last = pe.matmul(bank[:, q * T:(q + 1) * T], wq_sb[:, k, g * 128:(g + 1) * 128],
                                                     xnT[:, u, k, :], start=k == 0, stop=k == KD - 1)
                        if kind == "k":
                            if cross and n == 0:
                                pe.wait_ge(ctx_in[u], i * 16 + 16)
                            for q in range(1 if cross else G):
                                g = n + q
                                for k in range(KD):
                                    last = pe.matmul(bank[:, q * S:(q + 1) * S], wk_sb[:, k, g * 128:(g + 1) * 128],
                                                     kv_src[:, k, :], start=k == 0, stop=k == KD - 1 and maskrow is None)
                                if maskrow is not None:
                                    last = pe.matmul(bank[:, q * S:(q + 1) * S], K["indrow"][0:1, :],
                                                     maskrow[0:1, bass.ds(b * SK, SK)], start=False, stop=True)
                        if kind == "v":
                            c, m = n // NV, n % NV
                            for k in range(KD):
                                last = pe.matmul(bank[0:kc, 0:VW], kv_src[:, k, c * kc:(c + 1) * kc],
                                                 wv_sb[:, k, m * VW:(m + 1) * VW], start=k == 0, stop=k == KD - 1)
                        if kind == "g":
                            for k in range(KD):
                                pe.matmul(bank[0:T, 0:D], xnT[:, u, k, :], gw_sb[:, k, :], start=k == 0, stop=False)
                            last = pe.matmul(bank[0:T, 0:D], ones[0:1, 0:T], gb_sb[0:1, :], start=False, stop=True)
                        last.then_inc(pp_ready, 1)

                def scores(b, u, n):
                    if n == 0:
                        pe.wait_ge(pp_empty, (b + 1) * NPP)
                    wait(pe, e_ready, reuse(b, n, NU, 2))
                    for c, h in enumerate(units[n]):
                        out = sc[0:T, n % 2, c * S:(c + 1) * S]
                        if dh > 128:
                            for g in range(G):
                                last = pe.matmul(out, qT[:, u, g, :], kT[:, u, g, :], start=g == 0, stop=g == G - 1)
                        else:
                            g, r = h // per_group, h % per_group * slot
                            last = pe.matmul(out, qT[r:r + rows, u, g, :], kT[r:r + rows, u, g, :], start=True, stop=True)
                    last.then_inc(s_ready, 1)

                def turn(b, u, n):
                    pe.wait_ge(e_ready, b * NU + n + 1)
                    wait(pe, t_empty, reuse(b, n, NT, 2))
                    for c in range(HU):
                        for m in range(nkc):
                            s = c * nkc + m
                            last = pe.transpose(tr[0:kc, n % 2, s * T:(s + 1) * T],
                                                probs[:, n % 4, c, m * kc:(m + 1) * kc], ident[0:T, 0:T])
                    last.then_inc(t_ready, 1)

                def values(b, u, n):
                    pe.wait_ge(t_empty, b * NT + n + 1)
                    if n == 0:
                        wait(pe, o_norm, b if DV > 512 else b - 1)
                    for c, h in enumerate(units[n]):
                        for m in range(nkc):
                            last = pe.matmul(o_cols(u, h), pT[:, n % 2, c * nkc + m, :],
                                             vs[:, u, m, h * dv:(h + 1) * dv], start=m == 0, stop=m == nkc - 1)
                    last.then_inc(pv_done, 1)

                def tail(b, u):
                    if wo is None:
                        return
                    pe.wait_ge(o_ready, b + 1)
                    for n in range(NTT):
                        s = NU + n
                        wait(pe, t_empty, reuse(b, s, NT, 2))
                        for q in range(min(4, NBLK - 4 * n)):
                            k = 4 * n + q
                            last = pe.transpose(tr[:, s % 2, q * T:(q + 1) * T], o_sb[:, u, k * 128:(k + 1) * 128],
                                                ident[0:T, 0:T])
                        last.then_inc(t_ready, 1)
                    s = NU + NTT
                    pe.wait_ge(t_empty, b * NT + s)
                    for k in range(NBLK):
                        last = pe.matmul(tr[0:T, s % 2, 0:D], oT[:, k, :], wo_sb[:, k, :], start=k == 0,
                                         stop=k == NBLK - 1 and bo is None)
                    if bo is not None:
                        last = pe.matmul(tr[0:T, s % 2, 0:D], ones[0:1, 0:T], bo_sb[0:1, :], start=False, stop=True)
                    last.then_inc(t_ready, 1)

                def body(b, u, i):
                    project(b, u, i)
                    if not (isinstance(b, int) and b == 0):
                        tail(b - 1, 1 - u)
                    for n in range(NU + 3):
                        if n < NU:
                            scores(b, u, n)
                        if 0 <= n - 3:
                            values(b, u, n - 3)
                        if 0 <= n - 2 < NU:
                            turn(b, u, n - 2)

                over_batches(pe, body)
                tail(NB - 1, 1)

            @block.scalar
            def _(a):
                st.scalar(a)
                a.wait_ge(loaded, 16 * n_loads)
                if bq is not None:
                    a.wait_ge(scaled, n_scaled)

                def body(b, u, i):
                    for j, (kind, n) in enumerate(jobs):
                        bank = pp[:, j % 2, :]
                        a.wait_ge(pp_ready, b * NPP + j + 1)
                        if kind == "x":
                            last = a.activation(xnT[:, u, :, :].rearrange("p k t -> p (k t)"), bank[:, 0:KD * T], ACT.Copy)
                        if kind == "q":
                            if bq is None:
                                last = a.activation(qT[:, u, n * QPB:(n + 1) * QPB, :].rearrange("p g t -> p (g t)"), bank[:, 0:QPB * T], ACT.Copy)
                            else:
                                for q in range(QPB):
                                    g = n * QPB + q
                                    last = a.activation(qT[:, u, g, :], bank[:, q * T:(q + 1) * T], ACT.Identity, bias=bq_sb[:, g:g + 1])
                        if kind == "k":
                            for q in range(1 if cross else G):
                                g = n + q
                                if bk is None:
                                    last = a.activation(kT[:, u, g, :], bank[:, q * S:(q + 1) * S], ACT.Copy)
                                else:
                                    last = a.activation(kT[:, u, g, :], bank[:, q * S:(q + 1) * S], ACT.Identity, bias=bk_sb[:, g:g + 1])
                        if kind == "v":
                            c, m = n // NV, n % NV
                            last = a.activation(vs[:, u, c, m * VW:(m + 1) * VW], bank[0:kc, 0:VW], ACT.Copy)
                        if kind == "g":
                            last = a.activation(gate_w[:, u, :], bank[0:T, 0:D], ACT.Exp, scale=-1.0)
                        last.then_inc(pp_empty, 1)
                    for n in range(NU):
                        a.wait_ge(m_ready, b * NU + n + 1)
                        wait(a, t_ready, reuse(b, n, NT, 4, NU))
                        for c in range(HU):
                            src = logit[:, n % 2, c, :] if has_add else sc[0:T, n % 2, c * S:(c + 1) * S]
                            last = a.activation(probs[:, n % 4, c, :], src, ACT.Exp, bias=nmax[:, u, n, c:c + 1],
                                                accum_out=den[:, u, n, c:c + 1])
                        last.then_inc(e_ready, 1)

                over_batches(a, body)

            @block.vector
            def _(v):
                st.vector(v)
                v.wait_ge(loaded, 16 * n_loads)
                v.tensor_scalar(wq_sb[:], wq_sb[:], scale, None, ALU.mult).then_inc(scaled, 1)
                if bq is not None:
                    if maskrow is not None:
                        v.scalar_tensor_tensor(bq_sb[:], bq_sb[:], scale, indcol[:, 0:1].broadcast_to([128, G]),
                                               ALU.mult, ALU.add).then_inc(scaled, 1)
                    else:
                        v.tensor_scalar(bq_sb[:], bq_sb[:], scale, None, ALU.mult).then_inc(scaled, 1)

                def maxima(b, u, i, n):
                    v.wait_ge(s_ready, b * NU + n + 1)
                    src = sc[0:T, n % 2, 0:HU * S].rearrange("p (c s) -> p c s", c=HU)
                    if has_add:
                        wait(v, e_ready, reuse(b, n, NU, 2))
                        if pos_dram is not None:
                            if n == 0:
                                v.wait_ge(pos_in[u], i * 16 + 16)
                            add = pos_sb[:, u]
                        else:
                            add = addend[:]
                        add = add.rearrange("p (g j) s -> p j g s", j=per_group)[:, n, :, :]
                        v.tensor_tensor(logit[:, n % 2, :, :], src, add, ALU.add).then_inc(l_ready, 1)
                        v.wait_ge(l_ready, b * NU + n + 1)
                        src = logit[:, n % 2, :, :]
                    v.tensor_reduce(nmax[:, u, n, :], src, AX_X, ALU.max, negate=True).then_inc(m_ready, 1)

                def copy_turned(b, u, n):
                    v.wait_ge(t_ready, b * NT + n + 1)
                    wait(v, pv_done, reuse(b, n, NU, 2))
                    v.tensor_copy(pT[:, n % 2, :, :].rearrange("p c t -> p (c t)"), tr[0:kc, n % 2, 0:HU * nkc * T]).then_inc(t_empty, 1)

                def tail(b, u):
                    v.wait_ge(pv_done, (b + 1) * NU)
                    v.reciprocal(rden[:, u], den[:, u]).then_inc(rden_ready, 1)
                    v.wait_ge(rden_ready, b + 1)
                    o3 = o_sb[:, u, :].rearrange("p (h d) -> p h d", d=dv)
                    p3 = o_all(u).rearrange("p (h d) -> p h d", d=dv)
                    if HU == 1:
                        rd = rden[:, u].rearrange("p n c -> p (n c)").unsqueeze(2).broadcast_to([T, heads, dv])
                        v.tensor_tensor(o3, p3, rd, ALU.mult).then_inc(o_norm, 1)
                    else:
                        for n in range(NU):
                            rd = rden[:, u, n, :].unsqueeze(2).broadcast_to([T, HU, dv])
                            last = v.tensor_tensor(o3.rearrange("p (c n) d -> p n c d", n=NU)[:, n],
                                                   p3.rearrange("p (c n) d -> p n c d", n=NU)[:, n], rd, ALU.mult)
                        last.then_inc(o_norm, 1)
                    v.wait_ge(o_norm, b + 1)
                    if bv is not None:
                        v.tensor_tensor(o_sb[:, u, :], o_sb[:, u, :], bv_sb[:], ALU.add).then_inc(o_bias, 1)
                        v.wait_ge(o_bias, b + 1)
                    if gate:
                        v.tensor_scalar(gate_w[:, u, :], gate_w[:, u, :], 1.0, None, ALU.add).then_inc(g_steps, 1)
                        v.wait_ge(g_steps, b * 2 + 1)
                        v.reciprocal(gate_sb[:, u, :], gate_w[:, u, :]).then_inc(g_steps, 1)
                        v.wait_ge(g_steps, b * 2 + 2)
                        v.tensor_tensor(o_sb[:, u, :], o_sb[:, u, :], gate_sb[:, u, :], ALU.mult).then_inc(o_ready, 1)
                    elif wo is not None:
                        v.sem_inc(o_ready, 1)
                    if wo is None:
                        v.tensor_tensor(batch(dest, b), batch(dest, b), o_sb[:, u, :], ALU.add).then_inc(x_done, 1)
                        return
                    for n in range(NTT):
                        s = NU + n
                        v.wait_ge(t_ready, b * NT + s + 1)
                        blocks = min(4, NBLK - 4 * n)
                        v.tensor_copy(oT[:, 4 * n:4 * n + blocks, :].rearrange("p k t -> p (k t)"), tr[:, s % 2, 0:blocks * T]).then_inc(t_empty, 1)
                    s = NU + NTT
                    v.wait_ge(t_ready, b * NT + s + 1)
                    v.tensor_tensor(batch(dest, b), batch(dest, b), tr[0:T, s % 2, 0:D], ALU.add).then_inc(t_empty, 1)

                def body(b, u, i):
                    wait(v, pp_ready, (b - 2) * NPP + 1)
                    st.rows(v, b, xn[:, u, :], xn_ready, h=y, h_done=h_done, scale_row=ns_sb[:] if ns_sb is not None else None)
                    if not (isinstance(b, int) and b == 0):
                        tail(b - 1, 1 - u)
                    for n in range(NU + 2):
                        if n < NU:
                            maxima(b, u, i, n)
                        if 0 <= n - 2:
                            copy_turned(b, u, n - 2)

                over_batches(v, body)
                tail(NB - 1, 1)



HD0 = 64
ROWS = 8
NG0 = T // ROWS


def channel_attention(nc, x, K, wqkv, woutT):
    name = "l0a"
    ident = K["ident"]
    with Phase(nc, name + "o") as outer:
        qkv = outer.sb("qkv", [128, 3, NPAIR, T])
        num = outer.sb("num", [128, NPAIR, T])
        den = outer.sb("den", [128, NPAIR, T])
        nmx = outer.sb("nmx", [128, NPAIR, T])

        with Phase(nc, name + "p") as p:
            w = p.sb("w", [128, KD, 3 * HD0])
            xn = p.sb("xn", [T, 2, D])
            xnT = p.sb("xnT", [128, 2, KD, T])
            ptx = p.ps("ptx", [128, 2, 512])
            pqk = p.ps("pqk", [128, 2, 512])
            st = Norm(p, x, "ln")
            loaded, xn_ready, tx_ready = p.sem("loaded"), p.sem("xn_ready"), p.sem("tx_ready")
            xT_ready, qk_ready, qk_out = p.sem("xT_ready"), p.sem("qk_ready"), p.sem("qk_out")
            with nc.Block() as block:

                @block.sync
                def _(sp):
                    sp.dma_start(w[:], wqkv.rearrange("(k p) n -> p k n", p=128)).then_inc(loaded, 16)

                @block.vector
                def _(v):
                    st.vector(v)

                    def body(b, u, i):
                        wait(v, tx_ready, b - 1)
                        st.rows(v, b, xn[:, u, :], xn_ready)
                        v.wait_ge(tx_ready, b + 1)
                        wait(v, qk_ready, b - 1)
                        v.tensor_copy(xnT[:, u].rearrange("p k t -> p (k t)"), ptx[:, u, 0:KD * T]).then_inc(xT_ready, 1)

                    over_batches(v, body)

                @block.tensor
                def _(pe):
                    pe.wait_ge(loaded, 16)

                    def body(b, u, i):
                        pe.wait_ge(xn_ready, b + 1)
                        wait(pe, xT_ready, b - 1)
                        for k in range(KD):
                            last = pe.transpose(ptx[:, u, k * T:(k + 1) * T], xn[:, u, k * 128:(k + 1) * 128], ident[0:T, 0:T])
                        last.then_inc(tx_ready, 1)
                        pe.wait_ge(xT_ready, b + 1)
                        wait(pe, qk_out, b - 1)
                        for c in range(3):
                            for k in range(KD):
                                last = pe.matmul(pqk[64 * u:64 * u + 64, u, c * T:(c + 1) * T], w[:, k, c * HD0:(c + 1) * HD0],
                                                 xnT[:, u, k, :], start=k == 0, stop=k == KD - 1)
                        last.then_inc(qk_ready, 1)

                    over_batches(pe, body)

                @block.scalar
                def _(a):
                    st.scalar(a)

                    def body(b, u, i):
                        a.wait_ge(qk_ready, b + 1)
                        half = slice(64 * u, 64 * u + 64)
                        for c in range(3):
                            dst = qkv[half, c, bass.ds(i, 1), :].rearrange("p i t -> p (i t)")
                            last = a.activation(dst, pqk[half, u, c * T:(c + 1) * T], ACT.Copy, scale=HD0 ** -0.5 if c == 0 else 1.0)
                        last.then_inc(qk_out, 1)

                    over_batches(a, body)

        with Phase(nc, name + "s") as p:
            cmax, cmin = p.sb("cmax", [128, NPAIR, T]), p.sb("cmin", [128, NPAIR, T])
            ex = p.sb("ex", [128, NG0, ROWS, T])
            scans, max_ready = p.sem("scans"), p.sem("max_ready")
            e_ready, slot_free, prod = p.sem("e_ready"), p.sem("slot_free"), p.sem("prod")
            with nc.Block() as block:

                @block.vector
                def _(v):
                    for i in range(NPAIR):
                        k = qkv[:, 1, i, :]
                        v.tensor_tensor_scan(cmax[:, i, :], k, k, -3.0e38, ALU.max, ALU.max).then_inc(scans, 1)
                        v.tensor_tensor_scan(cmin[:, i, :], k, k, 3.0e38, ALU.min, ALU.min).then_inc(scans, 1)
                    v.wait_ge(scans, 2 * NPAIR)
                    v.tensor_tensor(cmax[:], cmax[:], qkv[:, 0], ALU.mult).then_inc(scans, 1)
                    v.tensor_tensor(cmin[:], cmin[:], qkv[:, 0], ALU.mult).then_inc(scans, 1)
                    v.wait_ge(scans, 2 * NPAIR + 2)
                    v.tensor_tensor(cmax[:], cmax[:], cmin[:], ALU.max).then_inc(scans, 1)
                    v.wait_ge(scans, 2 * NPAIR + 3)
                    v.tensor_scalar(nmx[:], cmax[:], -1.0, None, ALU.mult).then_inc(max_ready, 1)
                    v.memset(ex[:].rearrange("p g r t -> p (g r t)"), 0.0).then_inc(slot_free, NG0)
                    with v.Fori(0, NPAIR) as i:
                        for g in range(NG0):
                            v.wait_ge(e_ready, i * NG0 + g + 1)
                            L = (g + 1) * ROWS
                            e = ex[:, g, :, 0:L]
                            vrow = qkv[:, 2, bass.ds(i, 1), 0:L].broadcast_to([128, ROWS, L])
                            v.tensor_tensor(e, e, vrow, ALU.mult).then_inc(prod, 1)
                            v.wait_ge(prod, i * NG0 + g + 1)
                            v.tensor_reduce(num[:, bass.ds(i, 1), g * ROWS:L].rearrange("p i t -> p (i t)"), e, AX_X, ALU.add).then_inc(slot_free, 1)

                @block.scalar
                def _(a):
                    a.wait_ge(max_ready, 1)
                    with a.Fori(0, NPAIR) as i:
                        for g in range(NG0):
                            a.wait_ge(slot_free, i * NG0 + g + 1)
                            for r in range(ROWS):
                                n = g * ROWS + r

                                def at(t, lo, hi):
                                    return t[:, bass.ds(i, 1), lo:hi].rearrange("p i t -> p (i t)")
                                last = a.activation(ex[:, g, r, 0:n + 1], at(qkv[:, 1], 0, n + 1), ACT.Exp, bias=at(nmx, n, n + 1),
                                                    scale=at(qkv[:, 0], n, n + 1), accum_out=at(den, n, n + 1))
                            last.then_inc(e_ready, 1)

        with Phase(nc, name + "y") as p:
            w = p.sb("w", [128, D])
            o_st = p.sb("o_st", [128, T])
            py = p.ps("py", [128, 2, 512])
            loaded, recip, o_ready, y_ready, x_done = (p.sem(s) for s in ("loaded", "recip", "o_ready", "y_ready", "x_done"))
            with nc.Block() as block:

                @block.sync
                def _(sp):
                    for u in range(2):
                        sp.dma_start(w[64 * u:64 * u + 64, :], woutT).then_inc(loaded, 16)

                @block.vector
                def _(v):
                    v.reciprocal(den[:], den[:]).then_inc(recip, 1)
                    v.wait_ge(recip, 1)

                    def body(b, u, i):
                        half = slice(64 * u, 64 * u + 64)
                        wait(v, y_ready, b - 1)
                        v.tensor_tensor(o_st[half, :], num[half, bass.ds(i, 1), :].rearrange("p i t -> p (i t)"),
                                        den[half, bass.ds(i, 1), :].rearrange("p i t -> p (i t)"), ALU.mult).then_inc(o_ready, 1)
                        v.wait_ge(y_ready, b + 1)
                        v.tensor_tensor(batch(x, b), batch(x, b), py[0:T, u, 0:D], ALU.add).then_inc(x_done, 1)

                    over_batches(v, body)

                @block.tensor
                def _(pe):
                    pe.wait_ge(loaded, 32)

                    def body(b, u, i):
                        half = slice(64 * u, 64 * u + 64)
                        pe.wait_ge(o_ready, b + 1)
                        wait(pe, x_done, b - 1)
                        pe.matmul(py[0:T, u, 0:D], o_st[half, :], w[half, :], start=True, stop=True).then_inc(y_ready, 1)

                    over_batches(pe, body)



def offset_bias(nc, bias, K, pos_biasT, offsets, scratch):
    H, NO = pos_biasT.shape
    with Phase(nc, "l1b") as p:
        pb, off, offf = p.sb("pb", [H, NO]), p.sb("off", [H, NO], I32), p.sb("offf", [H, NO])
        diff = p.sb("diff", [H, T], I32)
        difff = p.sb("difff", [H, T])
        a = p.sb("a", [H, T, NO])
        mx, sm, row = p.sb("mx", [H, T]), p.sb("sm", [H, T]), p.sb("row", [H, RELS])
        loaded, iota_done, steps, to_act, act_done, row_ready, stored, back = (
            p.sem(s) for s in ("loaded", "iota_done", "steps", "to_act", "act_done", "row_ready", "stored", "back"))
        with nc.Block() as block:

            @block.sync
            def _(sp):
                sp.dma_start(pb[:], pos_biasT).then_inc(loaded, 16)
                sp.dma_start(off[:], offsets.rearrange("(a n) -> a n", a=1).broadcast_to([H, NO])).then_inc(loaded, 16)
                sp.wait_ge(row_ready, 2)
                sp.dma_start(scratch, row[:].unsqueeze(1).broadcast_to([H, T, RELS])).then_inc(stored, 16)
                sp.wait_ge(stored, 16)
                sp.dma_start(bias[:], skewed(scratch, 0, H)).then_inc(back, 16)
                sp.wait_ge(back, 16)

            @block.gpsimd
            def _(g):
                g.iota(diff[:], pattern=[[-1, T]], base=T - 1, channel_multiplier=0).then_inc(iota_done, 1)

            @block.vector
            def _(v):
                n = 0

                def chain(ins):
                    nonlocal n
                    n += 1
                    ins.then_inc(steps, 1)
                    v.wait_ge(steps, n)

                v.memset(row[:], MASKED).then_inc(row_ready, 1)
                v.wait_ge(loaded, 32)
                v.wait_ge(iota_done, 1)
                chain(v.tensor_copy(offf[:], off[:]))
                chain(v.tensor_copy(difff[:], diff[:]))
                wide = [H, T, NO]
                chain(v.tensor_tensor(a[:], difff[:].unsqueeze(2).broadcast_to(wide), offf[:].unsqueeze(1).broadcast_to(wide), ALU.not_equal))
                chain(v.tensor_scalar(a[:], a[:], MASKED, None, ALU.mult))
                chain(v.tensor_tensor(a[:], a[:], pb[:].unsqueeze(1).broadcast_to(wide), ALU.add))
                chain(v.tensor_reduce(mx[:], a[:], AX_X, ALU.max))
                chain(v.tensor_tensor(a[:], a[:], mx[:].unsqueeze(2).broadcast_to(wide), ALU.subtract))
                v.sem_inc(to_act, 1)
                v.wait_ge(act_done, 1)
                v.tensor_reduce(sm[:], a[:], AX_X, ALU.add).then_inc(to_act, 1)
                v.wait_ge(act_done, 2)
                v.wait_ge(row_ready, 1)
                v.tensor_tensor(row[:, 0:T], sm[:], mx[:], ALU.add).then_inc(row_ready, 1)

            @block.scalar
            def _(s):
                s.wait_ge(to_act, 1)
                s.activation(a[:], a[:], ACT.Exp).then_inc(act_done, 1)
                s.wait_ge(to_act, 2)
                s.activation(sm[:], sm[:], ACT.Ln).then_inc(act_done, 1)


def skewed(scratch, b, H):
    flat = scratch.rearrange("h t r -> h (t r)")
    part = flat[bass.ds(b * H, H), T - 1:T - 1 + T * (RELS - 1)]
    return part.rearrange("h (t r) -> t h r", r=RELS - 1)[:, :, 0:T]



def relative_positions(nc, x, K, wq, bq, wrT, br, scratch):
    H, G = 16, 4
    ident, indcol = K["ident"], K["indcol"]
    with Phase(nc, "l2p") as p:
        w = p.sb("w", [128, KD, G * 128])
        wr = p.sb("wr", [128, RELS])
        bq_sb = p.sb("bq", [128, G])
        xn, xnT, qT = p.sb("xn", [T, 2, D]), p.sb("xnT", [128, 2, KD, T]), p.sb("qT", [128, 2, G, T])
        rp = p.sb("rp", [T, 2, H, RELS])
        pp, pr = p.ps("pp", [128, 2, 512]), p.ps("pr", [128, 4, 512])
        st = Norm(p, x, "ln")
        loaded, bq_ready, xn_ready, pp_ready, pp_empty, r_ready, r_out = (
            p.sem(s) for s in ("loaded", "bq_ready", "xn_ready", "pp_ready", "pp_empty", "r_ready", "r_out"))
        stored = [p.sem(f"stored{u}") for u in range(2)]
        lo = REL_WINDOW - (T - 1)
        NR = H // 2
        pairs = [(j, g) for j in range(4) for g in (0, 2)]
        with nc.Block() as block:

            @block.sync
            def _(sp):
                sp.dma_start(w[:], wq.rearrange("(k p) n -> p k n", p=128)).then_inc(loaded, 16)
                sp.dma_start(bq_sb[:], bq).then_inc(loaded, 16)
                for j in range(4):
                    sp.dma_start(wr[32 * j:32 * j + 16, :], wrT[:, lo:lo + RELS]).then_inc(loaded, 16)
                    sp.dma_start(wr[32 * j + 16:32 * j + 17, :], br[lo:lo + RELS].rearrange("(a n) -> a n", a=1)).then_inc(loaded, 16)

                def body(b, u, i):
                    sp.wait_ge(r_out, (b + 1) * NR)
                    sp.dma_start(scratch[bass.ds(b * H, H)].rearrange("h t r -> t h r"), rp[:, u, :, :]).then_inc(stored[u], 16)

                over_batches(sp, body)
                for u in range(2):
                    sp.wait_ge(stored[u], 16 * NPAIR)

            @block.tensor
            def _(pe):
                pe.wait_ge(loaded, 16 * 10)

                def body(b, u, i):
                    pe.wait_ge(xn_ready, b + 1)
                    wait(pe, pp_empty, b * 2 - 1)
                    for k in range(KD):
                        last = pe.transpose(pp[:, 0, k * T:(k + 1) * T], xn[:, u, k * 128:(k + 1) * 128], ident[0:T, 0:T])
                    last.then_inc(pp_ready, 1)
                    pe.wait_ge(pp_empty, b * 2 + 1)
                    for g in range(G):
                        for k in range(KD):
                            last = pe.matmul(pp[:, 1, g * T:(g + 1) * T], w[:, k, g * 128:(g + 1) * 128], xnT[:, u, k, :],
                                             start=k == 0, stop=k == KD - 1)
                    last.then_inc(pp_ready, 1)
                    pe.wait_ge(pp_empty, b * 2 + 2)
                    for n, (j, g0) in enumerate(pairs):
                        wait(pe, r_out, reuse(b, n, NR, 4))
                        for c in range(2):
                            r = slice(32 * j, 32 * j + 17)
                            last = pe.matmul(pr[0:T, n % 4, c * RELS:(c + 1) * RELS], qT[r, u, g0 + c, :], wr[r, :], start=True, stop=True)
                        last.then_inc(r_ready, 1)

                over_batches(pe, body)

            @block.scalar
            def _(a):
                st.scalar(a)
                a.wait_ge(bq_ready, 1)

                def body(b, u, i):
                    a.wait_ge(pp_ready, b * 2 + 1)
                    a.activation(xnT[:, u].rearrange("p k t -> p (k t)"), pp[:, 0, 0:KD * T], ACT.Copy).then_inc(pp_empty, 1)
                    a.wait_ge(pp_ready, b * 2 + 2)
                    for g in range(G):
                        last = a.activation(qT[:, u, g, :], pp[:, 1, g * T:(g + 1) * T], ACT.Identity, bias=bq_sb[:, g:g + 1])
                    last.then_inc(pp_empty, 1)

                over_batches(a, body)

            @block.vector
            def _(v):
                st.vector(v)
                v.wait_ge(loaded, 16 * 10)
                v.tensor_tensor(bq_sb[:], bq_sb[:], indcol[:, 0:1].broadcast_to([128, G]), ALU.add).then_inc(bq_ready, 1)

                def body(b, u, i):
                    wait(v, pp_ready, b * 2 - 3)
                    st.rows(v, b, xn[:, u, :], xn_ready)
                    wait(v, stored[u], i * 16)
                    for n, (j, g0) in enumerate(pairs):
                        v.wait_ge(r_ready, b * NR + n + 1)
                        dst = rp[:, u].rearrange("p (g j) r -> p j g r", j=4)[:, j, g0:g0 + 2, :]
                        v.tensor_copy(dst, pr[0:T, n % 4, 0:2 * RELS].rearrange("p (c r) -> p c r", c=2)).then_inc(r_out, 1)

                over_batches(v, body)



def gating(nc, name, x, K, xnT_all, wts, kind, wg, bg, b2, acc, norm="ln", norm_scale=None, h=None, clear_acc=False):
    ident, ones = K["ident"], K["ones"]
    with Phase(nc, name + "g") as p:
        xn, xnT = p.sb("xn", [T, 2, D]), p.sb("xnT", [128, 2, KD, T])
        wg_sb = p.sb("wg", [128, KD, NE])
        bg_sb = p.sb("bg", [T, NE])
        b2_sb = p.sb("b2", [NE, D])
        ns_sb = p.sb("ns", [T, D])
        ptx, plg = p.ps("ptx", [128, 2, 512]), p.ps("plg", [128, 2, 512])
        st = Norm(p, x, norm)
        big = [T, NB, NE]
        lg, pr, rem, eq, key, oh, cnt = (p.sb(s, big) for s in ("lg", "pr", "rem", "eq", "key", "oh", "cnt"))
        pref, prefi = p.sb("pref", [T, NE]), p.sb("prefi", [T, NE], I32)
        m = p.sb("m", [T, NB])
        wst, wT = p.sb("wst", [T, 2, NE]), p.sb("wT", [NE, 2, T])
        loaded, xn_ready, tx_ready, xT_ready, all_ready, l_ready, l_out = (
            p.sem(s) for s in ("loaded", "xn_ready", "tx_ready", "xT_ready", "all_ready", "l_ready", "l_out"))
        steps, iota_done, to_act, act_done, to_pe, pe_done = (
            p.sem(s) for s in ("steps", "iota_done", "to_act", "act_done", "to_pe", "pe_done"))
        ws_ready, wT_ps, wT_ready, y_ready, y_out, h_done = (
            p.sem(s) for s in ("ws_ready", "wT_ps", "wT_ready", "y_ready", "y_out", "h_done"))
        loads = []
        if kind:
            loads.append((wg_sb[:], wg.rearrange("(k p) n -> p k n", p=128)))
        if bg is not None:
            loads.append((bg_sb[:], row_bcast(bg, T)))
        if b2 is not None:
            loads.append((b2_sb[:], b2))
        if norm_scale is not None:
            loads.append((ns_sb[:], row_bcast(norm_scale, T)))
        with nc.Block() as block:

            @block.sync
            def _(sp):
                for dst, src in loads:
                    sp.dma_start(dst, src).then_inc(loaded, 16)

            @block.gpsimd
            def _(g):
                first = kind != "top2_last"
                g.iota(prefi[:], pattern=[[-1 if first else 1, NE]], base=NE if first else 1, channel_multiplier=0).then_inc(iota_done, 1)

            @block.tensor
            def _(pe):
                if loads:
                    pe.wait_ge(loaded, 16 * len(loads))

                def body(b, u, i):
                    pe.wait_ge(xn_ready, b + 1)
                    wait(pe, xT_ready, b - 1)
                    for k in range(KD):
                        last = pe.transpose(ptx[:, u, k * T:(k + 1) * T], xn[:, u, k * 128:(k + 1) * 128], ident[0:T, 0:T])
                    last.then_inc(tx_ready, 1)
                    if kind:
                        pe.wait_ge(xT_ready, b + 1)
                        wait(pe, l_out, b - 1)
                        for k in range(KD):
                            last = pe.matmul(plg[0:T, u, 0:NE], xnT[:, u, k, :], wg_sb[:, k, :], start=k == 0, stop=k == KD - 1)
                        last.then_inc(l_ready, 1)

                over_batches(pe, body)
                if kind == "top1_capacity":
                    pe.wait_ge(to_pe, 1)
                    pe.wait_ge(xT_ready, NB)
                    pe.matmul(ptx[0:T, 0, 0:NB * NE], K["upto"][0:T, 0:T], oh[:].rearrange("p b e -> p (b e)"), start=True, stop=False)
                    pe.matmul(ptx[0:T, 0, 0:NB * NE], ones[0:T, 0:T], cnt[:].rearrange("p b e -> p (b e)"), start=False, stop=True).then_inc(pe_done, 1)
                if b2 is not None:

                    pe.wait_ge(xT_ready, NB)

                    def biases(b, u, i):
                        pe.wait_ge(ws_ready, b + 1)
                        wait(pe, wT_ready, b - 1)
                        pe.transpose(ptx[0:NE, u, 0:T], wst[:, u, :], ident[0:T, 0:T]).then_inc(wT_ps, 1)
                        pe.wait_ge(wT_ready, b + 1)
                        wait(pe, y_out, b - 1)
                        pe.matmul(plg[0:T, u, 0:D], wT[:, u, :], b2_sb[:], start=True, stop=True).then_inc(y_ready, 1)

                    over_batches(pe, biases)

            @block.scalar
            def _(a):
                st.scalar(a)

                def body(b, u, i):
                    a.wait_ge(tx_ready, b + 1)
                    if kind:
                        wait(a, l_ready, b - 1)
                    wait(a, all_ready, b - 1)
                    a.activation(xnT[:, u].rearrange("p k t -> p (k t)"), ptx[:, u, 0:KD * T], ACT.Copy).then_inc(xT_ready, 1)

                over_batches(a, body)
                if kind:
                    a.wait_ge(to_act, 1)
                    a.activation(pr[:], lg[:], ACT.Exp).then_inc(act_done, 1)

            @block.vector
            def _(v):
                n = 0

                def chain(ins):
                    nonlocal n
                    n += 1
                    ins.then_inc(steps, 1)
                    v.wait_ge(steps, n)

                st.vector(v)
                if loads:
                    v.wait_ge(loaded, 16 * len(loads))
                v.wait_ge(iota_done, 1)
                chain(v.tensor_copy(pref[:], prefi[:]))

                def body(b, u, i):
                    wait(v, tx_ready, b - 1)
                    st.rows(v, b, xn[:, u, :], xn_ready, h=h, h_done=h_done, scale_row=ns_sb[:])
                    v.wait_ge(xT_ready, b + 1)
                    v.tensor_scalar(xnT_all[:, :, bass.ds(b * T, T)], xnT[:, u, :, :],
                                    1.0, None, ALU.mult).then_inc(all_ready, 1)
                    if kind:
                        v.wait_ge(l_ready, b + 1)
                        if bg is not None:
                            v.tensor_tensor(batch(lg, b), plg[0:T, u, 0:NE], bg_sb[:], ALU.add).then_inc(l_out, 1)
                        else:
                            v.tensor_copy(batch(lg, b), plg[0:T, u, 0:NE]).then_inc(l_out, 1)

                over_batches(v, body)
                if not kind:
                    return
                v.wait_ge(l_out, NB)

                def wide(t):
                    return t[:].unsqueeze(2).broadcast_to(big)

                chain(v.tensor_reduce(m[:], lg[:], AX_X, ALU.max))
                v.tensor_tensor(lg[:], lg[:], wide(m), ALU.subtract).then_inc(to_act, 1)
                v.wait_ge(act_done, 1)
                chain(v.tensor_reduce(m[:], pr[:], AX_X, ALU.add))
                chain(v.reciprocal(m[:], m[:]))
                chain(v.tensor_tensor(pr[:], pr[:], wide(m), ALU.mult))

                def pick(src, out):
                    chain(v.tensor_reduce(m[:], src[:], AX_X, ALU.max))
                    chain(v.tensor_tensor(eq[:], src[:], wide(m), ALU.is_equal))
                    chain(v.tensor_tensor(key[:], eq[:], pref[:].unsqueeze(1).broadcast_to(big), ALU.mult))
                    chain(v.tensor_reduce(m[:], key[:], AX_X, ALU.max))
                    chain(v.tensor_tensor(out[:], key[:], wide(m), ALU.is_equal))

                pick(pr, oh)
                if kind in ("top2_last", "top2_first"):
                    chain(v.scalar_tensor_tensor(rem[:], oh[:], -2.0, pr[:], ALU.mult, ALU.add))
                    pick(rem, cnt)
                    chain(v.tensor_tensor(oh[:], oh[:], cnt[:], ALU.add))
                if kind == "top1_capacity":
                    chain(v.memset(cnt[:, 0, :], 0.0))
                    for b in range(1, NB):
                        chain(v.tensor_tensor(cnt[:, b, :], cnt[:, b - 1, :], oh[:, b - 1, :], ALU.add))
                    v.sem_inc(to_pe, 1)
                    v.wait_ge(pe_done, 1)
                    place = ptx[0:T, 0, 0:NB * NE].rearrange("p (b e) -> p b e", e=NE)
                    chain(v.tensor_scalar(key[:], place, float(CAPACITY), None, ALU.is_le))
                    chain(v.tensor_tensor(oh[:], oh[:], key[:], ALU.mult))
                chain(v.tensor_tensor(wts[:], oh[:], pr[:], ALU.mult))
                if b2 is not None:

                    def biases(b, u, i):
                        wait(v, wT_ps, b - 1)
                        v.tensor_copy(wst[:, u, :], batch(wts, b)).then_inc(ws_ready, 1)
                        v.wait_ge(wT_ps, b + 1)
                        wait(v, y_ready, b - 1)
                        v.tensor_copy(wT[:, u, :], ptx[0:NE, u, 0:T]).then_inc(wT_ready, 1)
                        v.wait_ge(y_ready, b + 1)
                        if clear_acc:
                            v.tensor_copy(batch(acc, b), plg[0:T, u, 0:D]).then_inc(y_out, 1)
                        else:
                            v.tensor_tensor(batch(acc, b), batch(acc, b), plg[0:T, u, 0:D], ALU.add).then_inc(y_out, 1)

                    over_batches(v, biases)



CB = 4
NCH = NB // CB
CT = CB * T


def experts(nc, name, K, xnT_all, wts, acc, w_up, w_gate, w_down, b_up, b_gate, act, n_exp=NE):
    HID = w_up.shape[2]
    tiles = [min(128, HID - 128 * m) for m in range(-(-HID // 128))]
    NM = len(tiles)
    FULL = HID // 128
    two = w_gate is not None
    NHB = 2 if two else 1
    with Phase(nc, name + "e") as p:
        wu = p.sb("wu", [128, 2, KD, HID])
        wg = p.sb("wg", [128, 2, KD, HID]) if two else None
        wd = p.sb("wd", [128, 2, NM, D])
        bu = p.sb("bu", [128, 2, NM]) if b_up is not None else None
        bg = p.sb("bg", [128, 2, NM]) if b_gate is not None else None
        hT = p.sb("hT", [128, 2, NM, CT])
        hs = p.sb("hs", [128, 2, CT])
        hp = p.sb("hp", [128, 2, CT])
        ph = p.ps("ph", [128, 4, 512])
        py = p.ps("py", [128, 4, 512])
        HR = 2
        w_in = [p.sem(f"w_in{u}") for u in range(2)]
        h_ready = p.sem("h_ready")
        h_half = p.sem("h_half")
        h_prod = p.sem("h_prod")
        h_out = p.sem("h_out")
        y_ready = p.sem("y_ready")
        y_out = p.sem("y_out")
        n_w = 2 + two + (FULL < NM) + (b_up is not None) + (b_gate is not None)
        NPAIRE = max(1, n_exp // 2)

        def over_experts(eng, body):
            if n_exp == 1:
                for c in range(NCH):
                    body(0, 0, 0, c)
                return
            for u in range(2):
                for c in range(NCH):
                    body(u, u, 0, c)
            with eng.Fori(1, NPAIRE) as i:
                for u in range(2):
                    for c in range(NCH):
                        body(i * 2 + u, u, i, c)

        with nc.Block() as block:

            @block.sync
            def _(sp):
                def body(e, u, i, c):
                    if c:
                        return
                    wait(sp, y_ready, (e - 1) * NB)
                    one = bass.ds(e, 1)
                    for t, src in ((bu, b_up), (bg, b_gate)):
                        if t is not None:
                            sp.dma_start(t[:, u, :], src[one].rearrange("e p m -> p (e m)")).then_inc(w_in[u], 16)
                    sp.dma_start(wu[:, u], w_up[one].rearrange("e (k p) n -> p (e k) n", p=128)).then_inc(w_in[u], 16)
                    if two:
                        sp.dma_start(wg[:, u], w_gate[one].rearrange("e (k p) n -> p (e k) n", p=128)).then_inc(w_in[u], 16)
                    sp.dma_start(wd[:, u, 0:FULL, :], w_down[one, 0:FULL * 128, :].rearrange("e (k p) n -> p (e k) n", p=128)).then_inc(w_in[u], 16)
                    if FULL < NM:
                        sp.dma_start(wd[0:tiles[-1], u, FULL, :], w_down[one, FULL * 128:HID, :].rearrange("e p n -> p (e n)")).then_inc(w_in[u], 16)

                over_experts(sp, body)

            @block.tensor
            def _(pe):
                def hidden(e, u, i, c, m):
                    n = c * NM + m
                    wait(pe, h_out, reuse(e, n, NCH * NM, HR))
                    for w, k0 in ((wu, 0), (wg, 1))[0:NHB]:
                        bank = n % HR * 2 + k0
                        for k in range(KD):
                            last = pe.matmul(ph[0:tiles[m], bank, 0:CT], w[:, u, k, m * 128:m * 128 + tiles[m]],
                                             xnT_all[:, k, c * CT:(c + 1) * CT], start=k == 0, stop=k == KD - 1)
                    last.then_inc(h_ready, 1)

                def down(e, u, c, t):
                    n = c * CB + t
                    pe.wait_ge(h_out, e * (NCH * NM) + (c + 1) * NM)
                    wait(pe, y_out, reuse(e, n, NB, 4))
                    for m in range(NM):
                        last = pe.matmul(py[0:T, n % 4, 0:D], hT[0:tiles[m], c % 2, m, t * T:(t + 1) * T], wd[0:tiles[m], u, m, :],
                                         start=m == 0, stop=m == NM - 1)
                    last.then_inc(y_ready, 1)

                def body(e, u, i, c):
                    if c == 0:
                        pe.wait_ge(w_in[u], i * 16 * n_w + 16 * n_w)
                    for m in range(NM):
                        hidden(e, u, i, c, m)
                    if c:
                        for t in range(CB):
                            down(e, u, c - 1, t)
                    if c == NCH - 1:
                        for t in range(CB):
                            down(e, u, c, t)

                over_experts(pe, body)

            def bias(t, u, m):
                return t[0:tiles[m], u, m:m + 1]

            @block.scalar
            def _(a):
                def body(e, u, i, c):
                    for m in range(NM):
                        n, P = c * NM + m, tiles[m]
                        N = NCH * NM
                        up, gt = ph[0:P, n % HR * 2, 0:CT], ph[0:P, n % HR * 2 + 1, 0:CT]
                        a.wait_ge(h_ready, e * N + n + 1)
                        if m == 0:
                            wait(a, y_ready, reuse(e, c, NCH, 2) * CB)
                        if act == "relu":
                            a.activation(hT[0:P, c % 2, m, :], up, ACT.Relu, bias=bias(bu, u, m)).then_inc(h_out, 1)
                        if act == "swiglu":
                            wait(a, h_out, reuse(e, n, N, 2))
                            a.activation(hs[0:P, n % 2, :], gt, ACT.Silu).then_inc(h_half, 1)
                        if act == "silu_of_product":
                            wait(a, h_prod, reuse(e, n, N, 2))
                            a.activation(hs[0:P, n % 2, :], gt, ACT.Identity, bias=bias(bg, u, m)).then_inc(h_half, 1)
                            a.wait_ge(h_prod, e * N + n + 1)
                            a.activation(hT[0:P, c % 2, m, :], hp[0:P, n % 2, :], ACT.Silu).then_inc(h_out, 1)

                over_experts(a, body)

            @block.vector
            def _(v):
                N = NCH * NM

                def add(e, c, t):
                    n = c * CB + t
                    v.wait_ge(y_ready, e * NB + n + 1)
                    if wts is None:
                        v.tensor_tensor(batch(acc, n), batch(acc, n), py[0:T, n % 4, 0:D], ALU.add).then_inc(y_out, 1)
                    else:
                        v.scalar_tensor_tensor(batch(acc, n), py[0:T, n % 4, 0:D], wts[:, n, bass.ds(e, 1)],
                                               batch(acc, n), ALU.mult, ALU.add).then_inc(y_out, 1)

                def body(e, u, i, c):
                    for m in range(NM):
                        n, P = c * NM + m, tiles[m]
                        up = ph[0:P, n % HR * 2, 0:CT]
                        if act == "swiglu":
                            v.wait_ge(h_half, e * N + n + 1)
                            if m == 0:
                                wait(v, y_ready, reuse(e, c, NCH, 2) * CB)
                            v.tensor_tensor(hT[0:P, c % 2, m, :], up, hs[0:P, n % 2, :], ALU.mult).then_inc(h_out, 1)
                        if act == "silu_of_product":
                            v.wait_ge(h_half, e * N + n + 1)
                            wait(v, h_out, reuse(e, n, N, 2))
                            v.scalar_tensor_tensor(hp[0:P, n % 2, :], up, bias(bu, u, m), hs[0:P, n % 2, :],
                                                   ALU.add, ALU.mult).then_inc(h_prod, 1)
                    if c:
                        for t in range(CB):
                            add(e, c - 1, t)
                    if c == NCH - 1:
                        for t in range(CB):
                            add(e, c, t)

                over_experts(v, body)


def linear(nc, name, K, src, w, bias, dest):
    ident, ones = K["ident"], K["ones"]
    with Phase(nc, name) as p:
        w_sb, b_sb = p.sb("w", [128, KD, D]), p.sb("b", [1, D])
        st, sT = p.sb("st", [T, 2, D]), p.sb("sT", [128, 2, KD, T])
        pt, py = p.ps("pt", [128, 2, 512]), p.ps("py", [128, 2, 512])
        loaded, s_ready, t_ready, t_out, y_ready, y_out = (p.sem(s) for s in ("loaded", "s_ready", "t_ready", "t_out", "y_ready", "y_out"))
        with nc.Block() as block:

            @block.sync
            def _(sp):
                sp.dma_start(w_sb[:], w.rearrange("(k p) n -> p k n", p=128)).then_inc(loaded, 16)
                sp.dma_start(b_sb[:], bias.rearrange("(a n) -> a n", a=1)).then_inc(loaded, 16)

            @block.tensor
            def _(pe):
                pe.wait_ge(loaded, 32)

                def body(b, u, i):
                    pe.wait_ge(s_ready, b + 1)
                    wait(pe, t_out, b - 1)
                    for k in range(KD):
                        last = pe.transpose(pt[:, u, k * T:(k + 1) * T], st[:, u, k * 128:(k + 1) * 128], ident[0:T, 0:T])
                    last.then_inc(t_ready, 1)
                    pe.wait_ge(t_out, b + 1)
                    wait(pe, y_out, b - 1)
                    for k in range(KD):
                        pe.matmul(py[0:T, u, 0:D], sT[:, u, k, :], w_sb[:, k, :], start=k == 0, stop=False)
                    pe.matmul(py[0:T, u, 0:D], ones[0:1, 0:T], b_sb[0:1, :], start=False, stop=True).then_inc(y_ready, 1)

                over_batches(pe, body)

            @block.vector
            def _(v):
                def body(b, u, i):
                    wait(v, t_ready, b - 1)
                    v.tensor_scalar(st[:, u, :], batch(src, b), 1.0, None, ALU.mult).then_inc(s_ready, 1)
                    v.wait_ge(t_ready, b + 1)
                    wait(v, y_ready, b - 1)
                    v.tensor_copy(sT[:, u].rearrange("p k t -> p (k t)"), pt[:, u, 0:KD * T]).then_inc(t_out, 1)
                    v.wait_ge(y_ready, b + 1)
                    v.tensor_tensor(batch(dest, b), batch(dest, b), py[0:T, u, 0:D], ALU.add).then_inc(y_out, 1)

                over_batches(v, body)


def add_all(nc, name, dest, src):
    with Phase(nc, name) as p:
        done = p.sem("done")
        with nc.Block() as block:

            @block.vector
            def _(v):
                v.tensor_tensor(dest[:], dest[:], src[:], ALU.add).then_inc(done, 1)



def constants(nc, x, x_dram, K, masks):
    with Phase(nc, "init") as p:
        m1, m2 = p.sb("m1", [1, NB * SK], I32), p.sb("m2", [1, NB * SK], U8)
        fs = p.sb("fs", [1, NB * SK])
        x_in, set_done, m_in, ready, ind, mk = (p.sem(s) for s in ("x_in", "set_done", "m_in", "ready", "ind", "mk"))
        if1, bk0, fside = masks
        with nc.Block() as block:

            @block.sync
            def _(sp):
                sp.dma_start(x[:], x_dram.rearrange("b t d -> t b d")).then_inc(x_in, 16)
                sp.dma_start(m1[:], if1.rearrange("b s -> (b s)").rearrange("(a n) -> a n", a=1)).then_inc(m_in, 16)
                sp.dma_start(m2[:], bk0.rearrange("b s -> (b s)").rearrange("(a n) -> a n", a=1)).then_inc(m_in, 16)
                sp.dma_start(fs[:], fside.rearrange("b s -> (b s)").rearrange("(a n) -> a n", a=1)).then_inc(m_in, 16)
                sp.wait_ge(x_in, 16)

            @block.gpsimd
            def _(g):
                g.memset(K["ident"][:], 0.0).then_inc(set_done, 1)
                g.memset(K["upto"][:], 1.0).then_inc(set_done, 1)
                g.wait_ge(set_done, 2)
                g.affine_select(out=K["ident"][:], in_=K["ident"][:], compare_op=ALU.not_equal, fill=1.0, base=0,
                                pattern=[[-1, 128]], channel_multiplier=1).then_inc(ready, 1)
                g.affine_select(out=K["upto"][:], in_=K["upto"][:], compare_op=ALU.is_ge, fill=0.0, base=0,
                                pattern=[[1, 128]], channel_multiplier=-1).then_inc(ready, 1)

            @block.vector
            def _(v):
                v.memset(K["ones"][:], 1.0).then_inc(ind, 1)
                v.memset(K["indrow"][:], 0.0).then_inc(ind, 1)
                v.wait_ge(ind, 2)
                v.memset(K["indrow"][0:1, :].rearrange("p (j s) -> p j s", s=32)[:, :, 16:17], 1.0).then_inc(ind, 1)
                v.wait_ge(ready, 2)
                v.tensor_reduce(K["indcol"][:, 0:1], K["ident"][:].rearrange("p (j s) -> p s j", s=32)[:, 16, :], AX_X, ALU.add).then_inc(ind, 1)
                v.wait_ge(m_in, 48)
                v.tensor_scalar(K["mask_if1"][:], m1[:], 0.0, MASKED, ALU.is_equal, ALU.mult).then_inc(mk, 1)
                v.tensor_scalar(K["mask_bk0"][:], m2[:], 0.0, MASKED, ALU.is_equal, ALU.mult).then_inc(mk, 1)
                v.wait_ge(mk, 2)
                v.tensor_tensor(K["mask_bk0"][:], K["mask_bk0"][:], fs[:], ALU.add).then_inc(mk, 1)


def decoder(nc, A, out, last_stage=12):
    with ExitStack() as ctx:
        def sb(name, shape, dt=F32):
            return ctx.enter_context(nc.sbuf_tensor(name, shape, dt))

        x = sb("x", [T, NB, D])
        K = {"ident": sb("ident", [128, 128]), "upto": sb("upto", [128, 128]), "ones": sb("ones", [128, 128]),
             "indrow": sb("indrow", [1, 128]), "indcol": sb("indcol", [128, 1])}
        with ExitStack() as mctx:
            K["mask_if1"] = sb("mask_if1", [1, NB * SK])
            K["mask_bk0"] = sb("mask_bk0", [1, NB * SK])
        wts = sb("wts", [T, NB, NE])
        constants(nc, x, A["x"], K, (A["mask_BxS2_if1"], A["mask_BxS2_bk0"], A["fside_BxS2_0"]))
        ctxT = A["ctxT"]

        def ffn(name, kind, wg, bg, b2, w_up, w_gate, w_down, b_up, b_gate, act, acc, clear_acc=False):
            with nc.sbuf_tensor(name + "_xT", [128, KD, NB * T], F32) as xnT_all:
                gating(nc, name, x, K, xnT_all, wts, kind, wg, bg, b2, acc, clear_acc=clear_acc)
                experts(nc, name, K, xnT_all, wts, acc, w_up, w_gate, w_down, b_up, b_gate, act)

        def stages():
            channel_attention(nc, x, K, A["L0_attn_w_qkv"], A["L0_attn_w_out"])
            yield
            attention(nc, "l0x", x, K, heads=16, dh=64, dv=64, wq=A["L0_xattn_Wq"], wk=A["L0_xattn_Wk"], wv=A["L0_xattn_Wv"],
                      scale=64 ** -0.5, ctxT=ctxT, wo=A["L0_xattn_Wo"], bo=A["L0_xattn_bo"])
            yield
            with nc.sbuf_tensor("mixed", [T, NB, D], F32) as y:
                ffn("l0f", "top2_last", A["L0_ffn_Wg"], A["L0_ffn_bg"], A["L0_ffn_b2"], A["L0_ffn_W1"], A["L0_ffn_W3"], A["L0_ffn_W2"],
                    A["L0_ffn_b1"], A["L0_ffn_b3"], "silu_of_product", y, clear_acc=True)
                linear(nc, "l0w", K, y, A["L0_ffn_Wf"], A["L0_ffn_bf"], x)
            yield
            with nc.sbuf_tensor("inner", [T, NB, D], F32) as y:
                with nc.sbuf_tensor("offbias", [T, 16, T], F32) as bias:
                    scratch = nc.dram_tensor("bias_rows", [16, T, RELS], F32, kind="Internal").ap()
                    offset_bias(nc, bias, K, A["L1_attn_pos_bias"], A["L1_attn_offsets"], scratch)
                    attention(nc, "l1a", x, K, heads=16, dh=16, dv=16, wq=A["L1_q"], wk=A["L1_k"], wv=A["L1_v"], scale=0.25,
                              wo=A["L1_attn_w_out"], addend=bias, gate=(A["L1_attn_w_gate"], A["L1_attn_b_gate"]),
                              norm="ln_rms", norm_scale=A["L1_attn_norm1_scale"], y=y)
                with nc.sbuf_tensor("l1af_xT", [128, KD, NB * T], F32) as xnT_all:
                    gating(nc, "l1af", y, K, xnT_all, None, None, None, None, None, None, norm="rms",
                           norm_scale=A["L1_attn_norm2_scale"], h=y)
                    experts(nc, "l1af", K, xnT_all, None, y, A["L1_up"], A["L1_gate"], A["L1_down"], None, None, "swiglu", n_exp=1)
                add_all(nc, "l1add", x, y)
            yield
            attention(nc, "l1x", x, K, heads=1, dh=256, dv=256, wq=A["L1_xattn_Wq"], wk=A["L1_xattn_Wk"], wv=A["L1_xattn_Wv"],
                      scale=D ** -0.5, ctxT=ctxT, bq=A["L1_xattn_bq"], bk=A["L1_xattn_bk"], bv=A["L1_xattn_bv"])
            yield
            ffn("l1f", "top1_capacity", A["L1_ffn_gate_w"], A["L1_ffn_gate_b"], A["L1_ffn_b2"], A["L1_ffn_w1"], None, A["L1_ffn_w2"],
                A["L1_ffn_b1"], None, "relu", x)
            yield
            scratch = nc.dram_tensor("rel_rows", [NB * 16, T, RELS], F32, kind="Internal").ap()
            relative_positions(nc, x, K, A["L2_q"], A["L2_bq"], A["L2_attn_Wr"], A["L2_attn_br"], scratch)
            attention(nc, "l2a", x, K, heads=16, dh=16, dv=16, wq=A["L2_q"], wk=A["L2_k"], wv=A["L2_v"], scale=0.25,
                      bq=A["L2_bq"], bk=A["L2_bk"], bv=A["L2_bv"], pos_dram=lambda b: skewed(scratch, b, 16))
            yield
            attention(nc, "l2x", x, K, heads=16, dh=16, dv=16, wq=A["L2_xattn_Wq"], wk=A["L2_xattn_Wk"], wv=A["L2_xattn_Wv"],
                      scale=0.25, ctxT=ctxT, bq=A["L2_xattn_bq"], bk=A["L2_xattn_bk"], bv=A["L2_xattn_bv"],
                      wo=A["L2_xattn_Wo"], bo=A["L2_xattn_bo"], maskrow=K["mask_if1"])
            yield
            ffn("l2f", "top1", A["L2_ffn_Wr"], A["L2_ffn_br"], A["L2_ffn_b2"], A["L2_ffn_W1"], None, A["L2_ffn_W2"],
                A["L2_ffn_b1"], None, "relu", x)
            yield
            attention(nc, "l3a", x, K, heads=1, dh=256, dv=256, wq=A["L3_attn_Wq"], wk=A["L3_attn_Wk"], wv=A["L3_attn_Wv"],
                      scale=D ** -0.5)
            yield
            attention(nc, "l3x", x, K, heads=16, dh=16, dv=16, wq=A["L3_q"], wk=A["L3_k"], wv=A["L3_v"], scale=0.25, ctxT=ctxT,
                      bq=A["L3_bq"], bk=A["L3_bk"], bv=A["L3_bv"], wo=A["L3_xattn_out_w"], bo=A["L3_xattn_out_b"],
                      maskrow=K["mask_bk0"])
            yield
            ffn("l3f", "top2_first", A["L3_ffn_router_w"], None, None, A["L3_up"], A["L3_gate"], A["L3_ffn_w2"],
                None, None, "swiglu", x)
            yield

        for n, _ in enumerate(stages()):
            if n + 1 == last_stage:
                break

        with Phase(nc, "end") as p:
            stored = p.sem("stored")
            with nc.Block() as block:

                @block.sync
                def _(sp):
                    sp.dma_start(out.rearrange("b t d -> t b d"), x[:]).then_inc(stored, 16)
                    sp.wait_ge(stored, 16)



def layout(I):
    import numpy as np

    def c(a):
        return np.ascontiguousarray(a)

    def pad_heads(w):
        out = np.zeros((w.shape[0], 16, 32), w.dtype)
        out[:, :, :16] = w.reshape(w.shape[0], 16, 16)
        return out.reshape(w.shape[0], 512)

    def pad_bias(b):
        out = np.zeros((16, 32), b.dtype)
        out[:, :16] = b.reshape(16, 16)
        return c(out.reshape(4, 128).T)

    def tile_bias(b):
        return c(b.reshape(b.shape[0], -1, 128).transpose(0, 2, 1))

    A = {k: I[k] for k in ("x", "fside_BxS2_0", "mask_BxS2_if1", "L0_xattn_bo", "L0_ffn_W1", "L0_ffn_W3", "L0_ffn_W2", "L0_ffn_b2",
                           "L0_ffn_Wg", "L0_ffn_bg", "L0_ffn_Wf", "L0_ffn_bf", "L1_attn_norm1_scale", "L1_attn_norm2_scale",
                           "L1_attn_w_out", "L1_attn_w_gate", "L1_attn_b_gate", "L1_attn_offsets", "L1_xattn_Wq", "L1_xattn_Wk",
                           "L1_xattn_Wv", "L1_xattn_bv", "L1_ffn_gate_b", "L1_ffn_w1", "L1_ffn_w2", "L1_ffn_b2", "L2_attn_br",
                           "L2_xattn_Wv", "L2_xattn_bv", "L2_xattn_Wo", "L2_xattn_bo", "L2_ffn_Wr", "L2_ffn_br", "L2_ffn_W1",
                           "L2_ffn_W2", "L2_ffn_b2", "L3_xattn_out_b")}
    A["mask_BxS2_bk0"] = I["mask_BxS2_bk0"]
    A["ctxT"] = c(I["ctx_1024"].transpose(0, 2, 1))
    for k in ("L0_attn_w_qkv", "L0_attn_w_out", "L0_xattn_Wq", "L0_xattn_Wk", "L0_xattn_Wv", "L0_xattn_Wo", "L1_attn_pos_bias",
              "L1_ffn_gate_w", "L2_attn_Wr", "L3_attn_Wq", "L3_attn_Wk", "L3_attn_Wv", "L3_xattn_out_w", "L3_ffn_router_w"):
        A[k] = c(I[k].T)
    for k in ("L0_ffn_b1", "L0_ffn_b3", "L1_ffn_b1", "L2_ffn_b1"):
        A[k] = tile_bias(I[k])
    w = I["L1_attn_w_qkv"]
    A["L1_q"], A["L1_k"], A["L1_v"] = pad_heads(w[:, :256]), pad_heads(w[:, 256:512]), c(w[:, 512:])
    A["L1_gate"], A["L1_up"], A["L1_down"] = I["L1_attn_w_ffn_gate"][None], I["L1_attn_w_ffn_up"][None], I["L1_attn_w_ffn_down"][None]
    for k in ("bq", "bk"):
        A["L1_xattn_" + k] = c(I["L1_xattn_" + k].reshape(2, 128).T)
        A["L2_xattn_" + k] = pad_bias(I["L2_xattn_" + k])
    A["L2_xattn_Wq"], A["L2_xattn_Wk"] = pad_heads(I["L2_xattn_Wq"]), pad_heads(I["L2_xattn_Wk"])
    w = I["L2_attn_Wqkv"].reshape(16, 3, 16, 256).transpose(1, 3, 0, 2).reshape(3, 256, 256)
    b = I["L2_attn_bqkv"].reshape(16, 3, 16).transpose(1, 0, 2).reshape(3, 256)
    A["L2_q"], A["L2_k"], A["L2_v"] = pad_heads(w[0]), pad_heads(w[1]), c(w[2])
    A["L2_bq"], A["L2_bk"], A["L2_bv"] = pad_bias(b[0]), pad_bias(b[1]), c(b[2])
    wkv, bkv = I["L3_xattn_Wkv_w"], I["L3_xattn_Wkv_b"]
    A["L3_q"], A["L3_k"], A["L3_v"] = pad_heads(I["L3_xattn_Wq_w"].T), pad_heads(wkv[:256].T), c(wkv[256:].T)
    A["L3_bq"], A["L3_bk"], A["L3_bv"] = pad_bias(I["L3_xattn_Wq_b"]), pad_bias(bkv[:256]), c(bkv[256:])
    w = I["L3_ffn_w1"].transpose(0, 2, 1)
    A["L3_gate"], A["L3_up"] = c(w[:, :, :512]), c(w[:, :, 512:])
    A["L3_ffn_w2"] = c(I["L3_ffn_w2"].transpose(0, 2, 1))
    return {k: c(a) for k, a in A.items()}


def kernel(**inputs):
    import numpy as _np
    import concourse.bacc as _bacc
    from concourse import mybir as _mybir
    from concourse.bass_utils import run_bass_kernel_spmd as _run

    arrays = {f"in_{k}": a for k, a in layout({k: _np.asarray(v) for k, v in inputs.items()}).items()}
    nc = _bacc.Bacc("TRN2", target_bir_lowering=False, num_devices=1)
    A = {k[3:]: nc.dram_tensor(k, a.shape, _mybir.dt.from_np(a.dtype), kind="ExternalInput").ap() for k, a in arrays.items()}
    out = nc.dram_tensor("out_dram", (NB, T, D), F32, kind="ExternalOutput").ap()
    decoder(nc, A, out)
    r = _run(nc, [arrays], core_ids=[0])
    return r.results[0]["out_dram"]
```

```python
from contextlib import ExitStack

import concourse.bass as bass
from concourse import mybir

F32 = mybir.dt.float32
I32 = mybir.dt.int32
U8 = mybir.dt.uint8
U32 = mybir.dt.uint32
ACT = mybir.ActivationFunctionType
ALU = mybir.AluOpType
AX_X = mybir.AxisListType.X

NB = 16
T = 112
D = 256
KD = D // 128
SK = 375
KC = 125
NKC = SK // KC
NE = 8
NPAIR = NB // 2
RELS = 2 * T - 1
REL_WINDOW = 128
MASKED = -1.0e30
LN_EPS = 1e-5
RMS_EPS = 1e-6
CAPACITY = -(-(5 * NB * T) // (4 * NE))


MOE_TILE = 256


def wait(eng, sem, value):
    if isinstance(value, int) and value <= 0:
        return
    eng.wait_ge(sem, value)


def reuse(b, n, per, ring, uses=None):
    uses = per if uses is None else uses
    if n >= ring:
        return b * per + n - ring + 1
    last = n + (uses - 1 - n) // ring * ring
    return (b - 1) * per + last + 1


def over_batches(eng, body):
    for u in range(2):
        body(u, u, 0)
    with eng.Fori(1, NPAIR) as i:
        for u in range(2):
            body(i * 2 + u, u, i)


def over_batches_ahead(eng, body):
    for u in range(2):
        body(u, u, 0)
    with eng.Fori(1, NPAIR - 1) as i:
        for u in range(2):
            body(i * 2 + u, u, i)
    for u in range(2):
        body(NB - 2 + u, u, NPAIR - 1)


def is_static(b, value):
    return isinstance(b, int) and b == value


class Kept:

    def __init__(self, ctx, nc, name):
        self.sem, self.base = ctx.enter_context(nc.semaphore(name)), 0


class Phase:

    def __init__(self, nc, name):
        self.nc, self.name, self.ctx, self.sems = nc, name, ExitStack(), []

    def __enter__(self):
        return self

    def sb(self, name, shape, dt=F32):
        return self.ctx.enter_context(self.nc.sbuf_tensor(f"{self.name}_{name}", shape, dt))

    def ps(self, name, shape):
        return self.ctx.enter_context(self.nc.psum_tensor(f"{self.name}_{name}", shape, F32))

    def sem(self, name):
        s = self.ctx.enter_context(self.nc.semaphore(f"{self.name}_{name}"))
        self.sems.append(s)
        return s

    def __exit__(self, *exc):
        if exc[0] is None:
            for s in self.sems:
                self.nc.gpsimd.sem_clear(s)
            self.nc.all_engine_barrier()
        self.ctx.close()


def batch(t, b):
    return t[0:T, bass.ds(b, 1), :].rearrange("p b d -> p (b d)")


def column(t, b):
    return t[0:T, bass.ds(b, 1)]


def row_bcast(ap, n):
    return ap.rearrange("(a n) -> a n", a=1).broadcast_to([n, ap.shape[0]])



class Norm:
    def __init__(self, p, x, kind):
        self.x, self.kind = x, kind
        self.st = p.sb("bn", [T, NB, 6])
        self.w = p.sb("bnw", [T, 6, NB])
        self.mean = p.sb("mean", [T, NB])
        self.var = p.sb("var", [T, NB])
        self.rstd = p.sb("rstd", [T, NB])
        self.rms = p.sb("rms", [T, NB])
        self.std = p.sb("std", [T, 2, NB])
        self.rows_done = p.sem("bn_rows")
        self.steps = p.sem("bn_steps")
        self.to_sqrt = p.sem("to_sqrt")
        self.sqrt_done = p.sem("sqrt_done")

    def vector(self, v):
        with v.Fori(0, NB) as b:
            v.bn_stats(self.st[:, bass.ds(b, 1), :].rearrange("p b s -> p (b s)"), batch(self.x, b)).then_inc(self.rows_done, 1)
        v.wait_ge(self.rows_done, NB)
        me, qe, mo, qo = (self.st[:, :, k] for k in (1, 2, 4, 5))
        s, d, q, d2, ve, ms = (self.w[:, k, :] for k in range(6))
        n = 0

        def chain(ins):
            nonlocal n
            n += 1
            ins.then_inc(self.steps, 1)
            v.wait_ge(self.steps, n)

        v.tensor_tensor(s, me, mo, ALU.add).then_inc(self.steps, 1)
        v.tensor_tensor(d, me, mo, ALU.subtract).then_inc(self.steps, 1)
        n += 2
        chain(v.tensor_tensor(q, qe, qo, ALU.add))
        chain(v.scalar_tensor_tensor(d2, d, 0.25, d, ALU.mult, ALU.mult))
        v.tensor_scalar(self.mean[:], s, 0.5, None, ALU.mult).then_inc(self.steps, 1)
        n += 1
        chain(v.scalar_tensor_tensor(self.var[:], q, 1.0 / D, d2, ALU.mult, ALU.add))
        if self.kind != "rms":
            v.tensor_scalar(ve, self.var[:], LN_EPS, None, ALU.add).then_inc(self.to_sqrt, 1)
            v.wait_ge(self.sqrt_done, 1)
            chain(v.reciprocal(self.rstd[:], self.std[:, 0, :]))
        if self.kind == "ln_rms":
            chain(v.tensor_tensor(ms, self.var[:], self.rstd[:], ALU.mult))
            chain(v.tensor_tensor(ms, ms, self.rstd[:], ALU.mult))
        if self.kind == "rms":
            chain(v.tensor_tensor(ms, self.mean[:], self.mean[:], ALU.mult))
            chain(v.tensor_tensor(ms, ms, self.var[:], ALU.add))
        if self.kind != "ln":
            k = 2 if self.kind == "ln_rms" else 1
            v.tensor_scalar(ve, ms, RMS_EPS, None, ALU.add).then_inc(self.to_sqrt, 1)
            v.wait_ge(self.sqrt_done, k)
            chain(v.reciprocal(self.rms[:], self.std[:, 1, :]))

    def scalar(self, a):
        which = {"ln": (0,), "ln_rms": (0, 1), "rms": (1,)}[self.kind]
        for n, k in enumerate(which):
            a.wait_ge(self.to_sqrt, n + 1)
            a.activation(self.std[:, k, :], self.w[:, 4, :], ACT.Sqrt).then_inc(self.sqrt_done, 1)

    def rows(self, v, b, out, done, h=None, h_done=None, scale_row=None):
        if self.kind == "ln":
            v.tensor_scalar(out, batch(self.x, b), column(self.mean, b), column(self.rstd, b),
                            ALU.subtract, ALU.mult).then_inc(done, 1)
            return
        if self.kind == "ln_rms":
            v.tensor_scalar(batch(h, b), batch(self.x, b), column(self.mean, b), column(self.rstd, b),
                            ALU.subtract, ALU.mult).then_inc(h_done, 1)
            v.wait_ge(h_done, b + 1)
        v.scalar_tensor_tensor(out, batch(h, b), column(self.rms, b), scale_row,
                               ALU.mult, ALU.mult).then_inc(done, 1)



def attention(nc, name, x, K, *, heads, dh, dv, wq, wk, wv, scale, ctxT=None, bq=None, bk=None, bv=None,
              wo=None, bo=None, maskrow=None, addend=None, pos_dram=None, gate=None, norm="ln",
              norm_scale=None, y=None):
    cross = ctxT is not None
    G = wq.shape[1] // 128
    S = SK if cross else T
    kc, nkc = (KC, NKC) if cross else (T, 1)
    DV = heads * dv
    per_group = max(1, 128 // max(32, dh))
    slot = 128 // per_group
    rows = min(dh, 128) + (1 if maskrow is not None else 0)
    HU = 1 if cross or heads == 1 else 4
    if HU == 1:
        units = [[h] for h in range(heads)]
    else:
        units = [[per_group * g + j for g in range(heads // per_group)] for j in range(per_group)]
    NU = len(units)
    has_add = addend is not None or pos_dram is not None
    QPB = min(G, 4)
    NQ = G // QPB
    VW = min(DV, 512)
    NV = DV // VW
    jobs = [("x", 0)] + [("q", n) for n in range(NQ)]
    jobs += [("k", g) for g in range(G)] if cross else [("k", 0)]
    jobs += [("v", c * NV + n) for c in range(nkc) for n in range(NV)]
    jobs += [("g", 0)] if gate else []
    NPP = len(jobs)
    NBLK = DV // 128
    NTT = -(-NBLK // 4) if wo is not None else 0
    NTY = NTT + 1 if wo is not None else 0
    dest = x if y is None else y
    LT, LV = (2, 3) if NU > 1 else (1, 1)
    X0 = 4 if NU > 4 else NU - 1
    steps = max(1, NU - 1)
    jobs_at = [list(range(n * NPP // steps, (n + 1) * NPP // steps)) for n in range(steps)] + [[]] * (NU - steps)
    NPB = 1 if DV > 512 else 2

    def back(b, u, n, lag):
        over = -(-(lag - n) // NU) if lag > n else 0
        if isinstance(b, int) and b < over:
            return None
        return b - over, (u - over) % 2, n - lag + over * NU

    def slot_of(u, n, ring):
        return n % ring if NU > 1 else u

    def before(b, n, ring):
        return reuse(b, n, NU, ring) if NU > 1 else b - 1

    ident, ones, indcol = K["ident"], K["ones"], K["indcol"]

    with Phase(nc, name) as p:
        wq_sb = p.sb("wq", [128, KD, G * 128])
        wk_sb = p.sb("wk", [128, KD, G * 128])
        wv_sb = p.sb("wv", [128, KD, DV])
        wo_sb = p.sb("wo", [128, NBLK, D]) if wo is not None else None
        bq_sb = p.sb("bq", [128, G]) if bq is not None else None
        bk_sb = p.sb("bk", [128, G]) if bk is not None else None
        bv_sb = p.sb("bv", [T, DV]) if bv is not None else None
        bo_sb = p.sb("bo", [1, D]) if bo is not None else None
        gw_sb = p.sb("gw", [128, KD, D]) if gate else None
        gb_sb = p.sb("gb", [1, D]) if gate else None
        gate_sb = p.sb("gate", [T, 2, D]) if gate else None
        gate_w = p.sb("gate_w", [T, 2, D]) if gate else None
        ns_sb = p.sb("ns", [T, D]) if norm_scale is not None else None
        ctx_sb = p.sb("ctx", [128, 2, KD, SK]) if cross else None
        pos_sb = p.sb("pos", [T, 2, heads, T]) if pos_dram is not None else None
        xn = p.sb("xn", [T, 2, D])
        xnT = p.sb("xnT", [128, 2, KD, T])
        qT = p.sb("qT", [128, 2, G, T])
        kT = p.sb("kT", [128, 2, G, S])
        vs = p.sb("v", [kc, 2, nkc, DV])
        logit = p.sb("logit", [T, 2, HU, S]) if has_add else None
        probs = p.sb("probs", [T, 4, HU, S])
        pT = p.sb("pT", [kc, 2, HU * nkc, T])
        nmax = p.sb("nmax", [T, 2, NU, HU])
        den = p.sb("den", [T, 2, NU, HU])
        rden = p.sb("rden", [T, 2, NU, HU])
        o_sb = p.sb("o", [T, 2, DV])
        oT = p.sb("oT", [128, NBLK, T]) if wo is not None else None

        pp = p.ps("pp", [128, NPB, 512])
        sc = p.ps("sc", [128, 2, 512])
        tr = p.ps("tr", [128, 2, 512])
        PO2 = DV <= 512 and wo is None
        po = p.ps("po", [128, 2, 512] if DV > 512 or PO2 else [128, 1, 512])
        ty = None if wo is None else p.ps("ty", [128, 512])

        st = Norm(p, x, norm)
        loaded = p.sem("loaded")
        n_loads = 0
        scaled = p.sem("scaled")
        ctx_in = [p.sem(f"ctx_in{u}") for u in range(2)]
        pos_in = [p.sem(f"pos_in{u}") for u in range(2)]
        xn_ready = p.sem("xn_ready")
        h_done = p.sem("h_done")
        pp_ready = p.sem("pp_ready")
        pp_empty = p.sem("pp_empty")
        s_ready = p.sem("s_ready")
        l_ready = p.sem("l_ready")
        m_ready = p.sem("m_ready")
        e_ready = p.sem("e_ready")
        t_ready = p.sem("t_ready")
        t_empty = p.sem("t_empty")
        ty_ready = p.sem("ty_ready")
        ty_empty = p.sem("ty_empty")
        pv_done = p.sem("pv_done")
        rden_ready = p.sem("rden_ready")
        o_norm = p.sem("o_norm")
        o_bias = p.sem("o_bias")
        o_ready = p.sem("o_ready")
        g_steps = p.sem("g_steps")
        x_done = p.sem("x_done")

        loads = [(wq_sb[:], wq.rearrange("(k p) n -> p k n", p=128)),
                 (wk_sb[:], wk.rearrange("(k p) n -> p k n", p=128)),
                 (wv_sb[:], wv.rearrange("(k p) n -> p k n", p=128))]
        if bq is not None:
            loads.append((bq_sb[:], bq))
        if bk is not None:
            loads.append((bk_sb[:], bk))
        if bv is not None:
            loads.append((bv_sb[:], row_bcast(bv, T)))
        if wo is not None:
            loads.append((wo_sb[:], wo.rearrange("(k p) n -> p k n", p=128)))
        if bo is not None:
            loads.append((bo_sb[:], bo.rearrange("(a n) -> a n", a=1)))
        if gate:
            loads.append((gw_sb[:], gate[0].rearrange("(k p) n -> p k n", p=128)))
            loads.append((gb_sb[:], gate[1].rearrange("(a n) -> a n", a=1)))
        if norm_scale is not None:
            loads.append((ns_sb[:], row_bcast(norm_scale, T)))
        n_loads = len(loads)
        n_scaled = 2 if bq is not None else 1

        def o_cols(u, h):
            if DV > 512:
                return po[0:T, h * dv // 512, h * dv % 512:h * dv % 512 + dv]
            return po[0:T, u if PO2 else 0, h * dv:(h + 1) * dv]

        def o_all(u):
            return po[0:T, :, :].rearrange("p a n -> p (a n)") if DV > 512 else po[0:T, u if PO2 else 0, 0:DV]

        with nc.Block() as block:

            @block.sync
            def _(sp):
                for dst, src in loads:
                    sp.dma_start(dst, src).then_inc(loaded, 16)
                if not cross and pos_dram is None:
                    return

                def body(b, u, i):
                    if cross:
                        wait(sp, pp_ready, (b - 1) * NPP)
                        sp.dma_start(ctx_sb[:, u, :, :], ctxT[bass.ds(b, 1)].rearrange("b (k p) s -> p (b k) s", p=128)).then_inc(ctx_in[u], 16)
                    if pos_dram is not None:
                        wait(sp, l_ready, (b - 1) * NU)
                        sp.dma_start(pos_sb[:, u, :, :], pos_dram(b)).then_inc(pos_in[u], 16)

                over_batches(sp, body)

            @block.tensor
            def _(pe):
                pe.wait_ge(loaded, 16 * n_loads)
                pe.wait_ge(scaled, n_scaled)

                def project(b, u, i, which):
                    for j in which:
                        kind, n = jobs[j]
                        bank = pp[:, j % NPB, :]
                        wait(pe, pp_empty, reuse(b, j, NPP, NPB))
                        kv_src = ctx_sb[:, u] if cross else xnT[:, u]
                        if kind == "x":
                            pe.wait_ge(xn_ready, b + 1)
                            for k in range(KD):
                                last = pe.transpose(bank[:, k * T:(k + 1) * T], xn[:, u, k * 128:(k + 1) * 128], ident[0:T, 0:T])
                        if kind == "q":
                            if n == 0:
                                pe.wait_ge(pp_empty, b * NPP + 1)
                            for q in range(QPB):
                                for k in range(KD):
                                    g = n * QPB + q
                                    last = pe.matmul(bank[:, q * T:(q + 1) * T], wq_sb[:, k, g * 128:(g + 1) * 128],
                                                     xnT[:, u, k, :], start=k == 0, stop=k == KD - 1)
                        if kind == "k":
                            if cross and n == 0:
                                pe.wait_ge(ctx_in[u], i * 16 + 16)
                            for q in range(1 if cross else G):
                                g = n + q
                                for k in range(KD):
                                    last = pe.matmul(bank[:, q * S:(q + 1) * S], wk_sb[:, k, g * 128:(g + 1) * 128],
                                                     kv_src[:, k, :], start=k == 0, stop=k == KD - 1 and maskrow is None)
                                if maskrow is not None:
                                    last = pe.matmul(bank[:, q * S:(q + 1) * S], K["indrow"][0:1, :],
                                                     maskrow[0:1, bass.ds(b * SK, SK)], start=False, stop=True)
                        if kind == "v":
                            c, m = n // NV, n % NV
                            for k in range(KD):
                                last = pe.matmul(bank[0:kc, 0:VW], kv_src[:, k, c * kc:(c + 1) * kc],
                                                 wv_sb[:, k, m * VW:(m + 1) * VW], start=k == 0, stop=k == KD - 1)
                        if kind == "g":
                            for k in range(KD):
                                pe.matmul(bank[0:T, 0:D], xnT[:, u, k, :], gw_sb[:, k, :], start=k == 0, stop=False)
                            last = pe.matmul(bank[0:T, 0:D], ones[0:1, 0:T], gb_sb[0:1, :], start=False, stop=True)
                        last.then_inc(pp_ready, 1)

                def scores(b, u, n):
                    if n == 0:
                        pe.wait_ge(pp_empty, (b + 1) * NPP)
                    wait(pe, e_ready, before(b, n, 2))
                    for c, h in enumerate(units[n]):
                        out = sc[0:T, slot_of(u, n, 2), c * S:(c + 1) * S]
                        if dh > 128:
                            for g in range(G):
                                last = pe.matmul(out, qT[:, u, g, :], kT[:, u, g, :], start=g == 0, stop=g == G - 1)
                        else:
                            g, r = h // per_group, h % per_group * slot
                            last = pe.matmul(out, qT[r:r + rows, u, g, :], kT[r:r + rows, u, g, :], start=True, stop=True)
                    last.then_inc(s_ready, 1)

                def turn(b, u, n):
                    pe.wait_ge(e_ready, b * NU + n + 1)
                    wait(pe, t_empty, before(b, n, 2))
                    for c in range(HU):
                        for m in range(nkc):
                            s = c * nkc + m
                            last = pe.transpose(tr[0:kc, slot_of(u, n, 2), s * T:(s + 1) * T],
                                                probs[:, slot_of(u, n, 4), c, m * kc:(m + 1) * kc], ident[0:T, 0:T])
                    last.then_inc(t_ready, 1)

                def values(b, u, n):
                    pe.wait_ge(t_empty, b * NU + n + 1)
                    if n == 0:
                        wait(pe, o_norm, b - 1 if PO2 else b)
                    for c, h in enumerate(units[n]):
                        for m in range(nkc):
                            last = pe.matmul(o_cols(u, h), pT[:, slot_of(u, n, 2), c * nkc + m, :],
                                             vs[:, u, m, h * dv:(h + 1) * dv], start=m == 0, stop=m == nkc - 1)
                    last.then_inc(pv_done, 1)

                def turn_output(b, u, n):
                    if n == 0:
                        pe.wait_ge(o_ready, b + 1)
                    wait(pe, ty_empty, b * NTY + n)
                    for q in range(min(4, NBLK - 4 * n)):
                        k = 4 * n + q
                        last = pe.transpose(ty[:, q * T:(q + 1) * T], o_sb[:, u, k * 128:(k + 1) * 128], ident[0:T, 0:T])
                    last.then_inc(ty_ready, 1)

                def project_output(b):
                    pe.wait_ge(ty_empty, b * NTY + NTT)
                    for k in range(NBLK):
                        last = pe.matmul(ty[0:T, 0:D], oT[:, k, :], wo_sb[:, k, :], start=k == 0,
                                         stop=k == NBLK - 1 and bo is None)
                    if bo is not None:
                        last = pe.matmul(ty[0:T, 0:D], ones[0:1, 0:T], bo_sb[0:1, :], start=False, stop=True)
                    last.then_inc(ty_ready, 1)

                def body(b, u, i):
                    for n in range(NU):
                        scores(b, u, n)
                        out = wo is not None and not is_static(b, 0)
                        if out and 0 <= n - X0 < NTT:
                            turn_output(b - 1, 1 - u, n - X0)
                        if (at := back(b, u, n, LT)) is not None:
                            turn(*at)
                        if (at := back(b, u, n, LV)) is not None:
                            values(*at)
                        if out and n == X0 + NTT - 1:
                            project_output(b - 1)
                        if not is_static(b, NB - 1):
                            project(b + 1, 1 - u, i + u, jobs_at[n])

                project(0, 0, 0, range(NPP))
                over_batches_ahead(pe, body)
                for n in range(LV):
                    if n < LT:
                        turn(*back(NB, 0, n, LT))
                    values(*back(NB, 0, n, LV))
                for n in range(NTT):
                    turn_output(NB - 1, 1, n)
                if wo is not None:
                    project_output(NB - 1)

            @block.scalar
            def _(a):
                st.scalar(a)
                a.wait_ge(loaded, 16 * n_loads)
                if bq is not None:
                    a.wait_ge(scaled, n_scaled)

                def copy_out(b, u, which):
                    for j in which:
                        kind, n = jobs[j]
                        bank = pp[:, j % NPB, :]
                        a.wait_ge(pp_ready, b * NPP + j + 1)
                        if kind == "x":
                            last = a.activation(xnT[:, u, :, :].rearrange("p k t -> p (k t)"), bank[:, 0:KD * T], ACT.Copy)
                        if kind == "q":
                            if bq is None:
                                last = a.activation(qT[:, u, n * QPB:(n + 1) * QPB, :].rearrange("p g t -> p (g t)"), bank[:, 0:QPB * T], ACT.Copy)
                            else:
                                for q in range(QPB):
                                    g = n * QPB + q
                                    last = a.activation(qT[:, u, g, :], bank[:, q * T:(q + 1) * T], ACT.Identity, bias=bq_sb[:, g:g + 1])
                        if kind == "k":
                            if bk is None:
                                last = a.activation(kT[:, u, n:n + (1 if cross else G), :].rearrange("p g s -> p (g s)"),
                                                    bank[:, 0:(1 if cross else G) * S], ACT.Copy)
                            else:
                                for q in range(1 if cross else G):
                                    g = n + q
                                    last = a.activation(kT[:, u, g, :], bank[:, q * S:(q + 1) * S], ACT.Identity, bias=bk_sb[:, g:g + 1])
                        if kind == "v":
                            c, m = n // NV, n % NV
                            last = a.activation(vs[:, u, c, m * VW:(m + 1) * VW], bank[0:kc, 0:VW], ACT.Copy)
                        if kind == "g":
                            wait(a, o_ready, b - 1)
                            last = a.activation(gate_w[:, u, :], bank[0:T, 0:D], ACT.Exp, scale=-1.0)
                        last.then_inc(pp_empty, 1)

                def exponentials(b, u, n):
                    a.wait_ge(m_ready, b * NU + n + 1)
                    wait(a, t_ready, before(b, n, 4))
                    for c in range(HU):
                        src = logit[:, slot_of(u, n, 2), c, :] if has_add else sc[0:T, slot_of(u, n, 2), c * S:(c + 1) * S]
                        last = a.activation(probs[:, slot_of(u, n, 4), c, :], src, ACT.Exp, bias=nmax[:, u, n, c:c + 1],
                                            accum_out=den[:, u, n, c:c + 1])
                    last.then_inc(e_ready, 1)

                def body(b, u, i):
                    for n in range(NU):
                        exponentials(b, u, n)
                        if not is_static(b, NB - 1):
                            copy_out(b + 1, 1 - u, jobs_at[n])

                copy_out(0, 0, range(NPP))
                over_batches_ahead(a, body)

            @block.vector
            def _(v):
                st.vector(v)
                v.wait_ge(loaded, 16 * n_loads)
                v.tensor_scalar(wq_sb[:], wq_sb[:], scale, None, ALU.mult).then_inc(scaled, 1)
                if bq is not None:
                    if maskrow is not None:
                        v.scalar_tensor_tensor(bq_sb[:], bq_sb[:], scale, indcol[:, 0:1].broadcast_to([128, G]),
                                               ALU.mult, ALU.add).then_inc(scaled, 1)
                    else:
                        v.tensor_scalar(bq_sb[:], bq_sb[:], scale, None, ALU.mult).then_inc(scaled, 1)

                def normed_rows(b, u):
                    wait(v, pp_ready, (b - 2) * NPP + 1)
                    st.rows(v, b, xn[:, u, :], xn_ready, h=y, h_done=h_done, scale_row=ns_sb[:] if ns_sb is not None else None)

                def maxima(b, u, i, n):
                    v.wait_ge(s_ready, b * NU + n + 1)
                    src = sc[0:T, slot_of(u, n, 2), 0:HU * S].rearrange("p (c s) -> p c s", c=HU)
                    if has_add:
                        wait(v, e_ready, before(b, n, 2))
                        if pos_dram is not None:
                            if n == 0:
                                v.wait_ge(pos_in[u], i * 16 + 16)
                            add = pos_sb[:, u]
                        else:
                            add = addend[:]
                        add = add.rearrange("p (g j) s -> p j g s", j=per_group)[:, n, :, :]
                        v.tensor_tensor(logit[:, slot_of(u, n, 2), :, :], src, add, ALU.add).then_inc(l_ready, 1)
                        v.wait_ge(l_ready, b * NU + n + 1)
                        src = logit[:, slot_of(u, n, 2), :, :]
                    v.tensor_reduce(nmax[:, u, n, :], src, AX_X, ALU.max, negate=True).then_inc(m_ready, 1)

                def copy_turned(b, u, n):
                    v.wait_ge(t_ready, b * NU + n + 1)
                    wait(v, pv_done, before(b, n, 2))
                    v.tensor_copy(pT[:, slot_of(u, n, 2), :, :].rearrange("p c t -> p (c t)"),
                                  tr[0:kc, slot_of(u, n, 2), 0:HU * nkc * T]).then_inc(t_empty, 1)

                def normalise(b, u):
                    v.wait_ge(pv_done, (b + 1) * NU)
                    v.reciprocal(rden[:, u], den[:, u]).then_inc(rden_ready, 1)
                    v.wait_ge(rden_ready, b + 1)
                    o3 = o_sb[:, u, :].rearrange("p (h d) -> p h d", d=dv)
                    p3 = o_all(u).rearrange("p (h d) -> p h d", d=dv)
                    if HU == 1:
                        rd = rden[:, u].rearrange("p n c -> p (n c)").unsqueeze(2).broadcast_to([T, heads, dv])
                        v.tensor_tensor(o3, p3, rd, ALU.mult).then_inc(o_norm, 1)
                    else:
                        rd = rden[:, u].rearrange("p n c -> p c n").unsqueeze(3).broadcast_to([T, HU, NU, dv])
                        v.tensor_tensor(o3.rearrange("p (c n) d -> p c n d", n=NU), p3.rearrange("p (c n) d -> p c n d", n=NU),
                                        rd, ALU.mult).then_inc(o_norm, 1)
                    v.wait_ge(o_norm, b + 1)
                    if bv is not None:
                        last = v.tensor_tensor(o_sb[:, u, :], o_sb[:, u, :], bv_sb[:], ALU.add)
                        if wo is not None:
                            last.then_inc(o_ready, 1)
                        else:
                            last.then_inc(o_bias, 1)
                            v.wait_ge(o_bias, b + 1)
                    elif gate:
                        v.tensor_scalar(gate_w[:, u, :], gate_w[:, u, :], 1.0, None, ALU.add).then_inc(g_steps, 1)
                        v.wait_ge(g_steps, b * 2 + 1)
                        v.reciprocal(gate_sb[:, u, :], gate_w[:, u, :]).then_inc(g_steps, 1)
                        v.wait_ge(g_steps, b * 2 + 2)
                        v.tensor_tensor(o_sb[:, u, :], o_sb[:, u, :], gate_sb[:, u, :], ALU.mult).then_inc(o_ready, 1)
                    elif wo is not None:
                        v.sem_inc(o_ready, 1)
                    if wo is None:
                        v.tensor_tensor(batch(dest, b), batch(dest, b), o_sb[:, u, :], ALU.add).then_inc(x_done, 1)

                def copy_output(b, n):
                    v.wait_ge(ty_ready, b * NTY + n + 1)
                    blocks = min(4, NBLK - 4 * n)
                    v.tensor_copy(oT[:, 4 * n:4 * n + blocks, :].rearrange("p k t -> p (k t)"), ty[:, 0:blocks * T]).then_inc(ty_empty, 1)

                def add_output(b):
                    v.wait_ge(ty_ready, (b + 1) * NTY)
                    v.tensor_tensor(batch(dest, b), batch(dest, b), ty[0:T, 0:D], ALU.add).then_inc(ty_empty, 1)

                def body(b, u, i):
                    for n in range(NU):
                        maxima(b, u, i, n)
                        if n == 0 and not is_static(b, NB - 1):
                            normed_rows(b + 1, 1 - u)
                        out = wo is not None and not is_static(b, 0)
                        if out and 0 <= n - X0 < NTT:
                            copy_output(b - 1, n - X0)
                        if (at := back(b, u, n, LT)) is not None:
                            copy_turned(*at)
                        if n == LV - 1 and not is_static(b, 0):
                            normalise(b - 1, 1 - u)
                        if out and n == X0 + NTT - 1:
                            add_output(b - 1)

                normed_rows(0, 0)
                over_batches_ahead(v, body)
                for n in range(LT):
                    copy_turned(*back(NB, 0, n, LT))
                normalise(NB - 1, 1)
                for n in range(NTT):
                    copy_output(NB - 1, n)
                if wo is not None:
                    add_output(NB - 1)



HD0 = 64
ROWS = 8
NG0 = T // ROWS


def channel_attention(nc, x, K, wqkv, woutT):
    name = "l0a"
    ident = K["ident"]
    with Phase(nc, name + "o") as outer:
        qkv = outer.sb("qkv", [128, 3, NPAIR, T])
        num = outer.sb("num", [128, NPAIR, T])
        den = outer.sb("den", [128, NPAIR, T])
        nmx = outer.sb("nmx", [128, NPAIR, T])

        with Phase(nc, name + "p") as p:
            w = p.sb("w", [128, KD, 3 * HD0])
            xn = p.sb("xn", [T, 2, D])
            xnT = p.sb("xnT", [128, 2, KD, T])
            ptx = p.ps("ptx", [128, 2, 512])
            pqk = p.ps("pqk", [128, 2, 512])
            st = Norm(p, x, "ln")
            loaded, xn_ready, tx_ready = p.sem("loaded"), p.sem("xn_ready"), p.sem("tx_ready")
            xT_ready, qk_ready, qk_out = p.sem("xT_ready"), p.sem("qk_ready"), p.sem("qk_out")
            with nc.Block() as block:

                @block.sync
                def _(sp):
                    sp.dma_start(w[:], wqkv.rearrange("(k p) n -> p k n", p=128)).then_inc(loaded, 16)

                @block.vector
                def _(v):
                    st.vector(v)

                    def body(b, u, i):
                        wait(v, tx_ready, b - 1)
                        st.rows(v, b, xn[:, u, :], xn_ready)
                        v.wait_ge(tx_ready, b + 1)
                        wait(v, qk_ready, b - 1)
                        v.tensor_copy(xnT[:, u].rearrange("p k t -> p (k t)"), ptx[:, u, 0:KD * T]).then_inc(xT_ready, 1)

                    over_batches(v, body)

                @block.tensor
                def _(pe):
                    pe.wait_ge(loaded, 16)

                    def body(b, u, i):
                        pe.wait_ge(xn_ready, b + 1)
                        wait(pe, xT_ready, b - 1)
                        for k in range(KD):
                            last = pe.transpose(ptx[:, u, k * T:(k + 1) * T], xn[:, u, k * 128:(k + 1) * 128], ident[0:T, 0:T])
                        last.then_inc(tx_ready, 1)
                        pe.wait_ge(xT_ready, b + 1)
                        wait(pe, qk_out, b - 1)
                        for c in range(3):
                            for k in range(KD):
                                last = pe.matmul(pqk[64 * u:64 * u + 64, u, c * T:(c + 1) * T], w[:, k, c * HD0:(c + 1) * HD0],
                                                 xnT[:, u, k, :], start=k == 0, stop=k == KD - 1)
                        last.then_inc(qk_ready, 1)

                    over_batches(pe, body)

                @block.scalar
                def _(a):
                    st.scalar(a)

                    def body(b, u, i):
                        a.wait_ge(qk_ready, b + 1)
                        half = slice(64 * u, 64 * u + 64)
                        for c in range(3):
                            dst = qkv[half, c, bass.ds(i, 1), :].rearrange("p i t -> p (i t)")
                            last = a.activation(dst, pqk[half, u, c * T:(c + 1) * T], ACT.Copy, scale=HD0 ** -0.5 if c == 0 else 1.0)
                        last.then_inc(qk_out, 1)

                    over_batches(a, body)

        with Phase(nc, name + "s") as p:
            cmax, cmin = p.sb("cmax", [128, NPAIR, T]), p.sb("cmin", [128, NPAIR, T])
            ex = p.sb("ex", [128, NG0, ROWS, T])
            ev = p.sb("ev", [128, 2, ROWS, T])
            scans, max_ready = p.sem("scans"), p.sem("max_ready")
            e_ready, slot_free, prod = p.sem("e_ready"), p.sem("slot_free"), p.sem("prod")
            with nc.Block() as block:

                @block.vector
                def _(v):
                    for i in range(NPAIR):
                        k = qkv[:, 1, i, :]
                        v.tensor_tensor_scan(cmax[:, i, :], k, k, -3.0e38, ALU.max, ALU.max).then_inc(scans, 1)
                        v.tensor_tensor_scan(cmin[:, i, :], k, k, 3.0e38, ALU.min, ALU.min).then_inc(scans, 1)
                    v.wait_ge(scans, 2 * NPAIR)
                    v.tensor_tensor(cmax[:], cmax[:], qkv[:, 0], ALU.mult).then_inc(scans, 1)
                    v.tensor_tensor(cmin[:], cmin[:], qkv[:, 0], ALU.mult).then_inc(scans, 1)
                    v.wait_ge(scans, 2 * NPAIR + 2)
                    v.tensor_tensor(cmax[:], cmax[:], cmin[:], ALU.max).then_inc(scans, 1)
                    v.wait_ge(scans, 2 * NPAIR + 3)
                    v.tensor_scalar(nmx[:], cmax[:], -1.0, None, ALU.mult).then_inc(max_ready, 1)
                    v.memset(ex[:].rearrange("p g r t -> p (g r t)"), 0.0).then_inc(slot_free, NG0)
                    with v.Fori(0, NPAIR) as i:
                        for g in range(NG0):
                            v.wait_ge(e_ready, i * NG0 + g + 1)
                            L = (g + 1) * ROWS
                            e = ex[:, g, :, 0:L]
                            v.tensor_reduce(den[:, bass.ds(i, 1), g * ROWS:L].rearrange("p i t -> p (i t)"), e, AX_X, ALU.add)
                            vrow = qkv[:, 2, bass.ds(i, 1), 0:L].broadcast_to([128, ROWS, L])
                            v.wait_ge(slot_free, i * NG0 + NG0 + g - 1)
                            pv = ev[:, g % 2, :, 0:L]
                            v.tensor_tensor(pv, e, vrow, ALU.mult).then_inc(prod, 1)
                            v.wait_ge(prod, i * NG0 + g + 1)
                            v.tensor_reduce(num[:, bass.ds(i, 1), g * ROWS:L].rearrange("p i t -> p (i t)"), pv, AX_X, ALU.add).then_inc(slot_free, 1)

                @block.scalar
                def _(a):
                    a.wait_ge(max_ready, 1)
                    with a.Fori(0, NPAIR) as i:
                        for g in range(NG0):
                            a.wait_ge(slot_free, i * NG0 + g + 1)
                            for r in range(ROWS):
                                n = g * ROWS + r

                                def at(t, lo, hi):
                                    return t[:, bass.ds(i, 1), lo:hi].rearrange("p i t -> p (i t)")
                                last = a.activation(ex[:, g, r, 0:n + 1], at(qkv[:, 1], 0, n + 1), ACT.Exp, bias=at(nmx, n, n + 1),
                                                    scale=at(qkv[:, 0], n, n + 1))
                            last.then_inc(e_ready, 1)

        with Phase(nc, name + "y") as p:
            w = p.sb("w", [128, D])
            o_st = p.sb("o_st", [128, T])
            py = p.ps("py", [128, 2, 512])
            loaded, recip, o_ready, y_ready, x_done = (p.sem(s) for s in ("loaded", "recip", "o_ready", "y_ready", "x_done"))
            with nc.Block() as block:

                @block.sync
                def _(sp):
                    for u in range(2):
                        sp.dma_start(w[64 * u:64 * u + 64, :], woutT).then_inc(loaded, 16)

                @block.vector
                def _(v):
                    v.reciprocal(den[:], den[:]).then_inc(recip, 1)
                    v.wait_ge(recip, 1)

                    def body(b, u, i):
                        half = slice(64 * u, 64 * u + 64)
                        wait(v, y_ready, b - 1)
                        v.tensor_tensor(o_st[half, :], num[half, bass.ds(i, 1), :].rearrange("p i t -> p (i t)"),
                                        den[half, bass.ds(i, 1), :].rearrange("p i t -> p (i t)"), ALU.mult).then_inc(o_ready, 1)
                        v.wait_ge(y_ready, b + 1)
                        v.tensor_tensor(batch(x, b), batch(x, b), py[0:T, u, 0:D], ALU.add).then_inc(x_done, 1)

                    over_batches(v, body)

                @block.tensor
                def _(pe):
                    pe.wait_ge(loaded, 32)

                    def body(b, u, i):
                        half = slice(64 * u, 64 * u + 64)
                        pe.wait_ge(o_ready, b + 1)
                        wait(pe, x_done, b - 1)
                        pe.matmul(py[0:T, u, 0:D], o_st[half, :], w[half, :], start=True, stop=True).then_inc(y_ready, 1)

                    over_batches(pe, body)



def offset_bias(nc, bias, K, pos_biasT, offsets, scratch):
    H, NO = pos_biasT.shape
    with Phase(nc, "l1b") as p:
        pb, off, offf = p.sb("pb", [H, NO]), p.sb("off", [H, NO], I32), p.sb("offf", [H, NO])
        diff = p.sb("diff", [H, T], I32)
        difff = p.sb("difff", [H, T])
        a = p.sb("a", [H, T, NO])
        mx, sm, row = p.sb("mx", [H, T]), p.sb("sm", [H, T]), p.sb("row", [H, RELS])
        loaded, iota_done, steps, to_act, act_done, row_ready, stored, back = (
            p.sem(s) for s in ("loaded", "iota_done", "steps", "to_act", "act_done", "row_ready", "stored", "back"))
        with nc.Block() as block:

            @block.sync
            def _(sp):
                sp.dma_start(pb[:], pos_biasT).then_inc(loaded, 16)
                sp.dma_start(off[:], offsets.rearrange("(a n) -> a n", a=1).broadcast_to([H, NO])).then_inc(loaded, 16)
                sp.wait_ge(row_ready, 2)
                sp.dma_start(scratch, row[:].unsqueeze(1).broadcast_to([H, T, RELS])).then_inc(stored, 16)
                sp.wait_ge(stored, 16)
                sp.dma_start(bias[:], skewed(scratch, 0, H)).then_inc(back, 16)
                sp.wait_ge(back, 16)

            @block.gpsimd
            def _(g):
                g.iota(diff[:], pattern=[[-1, T]], base=T - 1, channel_multiplier=0).then_inc(iota_done, 1)

            @block.vector
            def _(v):
                n = 0

                def chain(ins):
                    nonlocal n
                    n += 1
                    ins.then_inc(steps, 1)
                    v.wait_ge(steps, n)

                v.memset(row[:], MASKED).then_inc(row_ready, 1)
                v.wait_ge(loaded, 32)
                v.wait_ge(iota_done, 1)
                chain(v.tensor_copy(offf[:], off[:]))
                chain(v.tensor_copy(difff[:], diff[:]))
                wide = [H, T, NO]
                chain(v.tensor_tensor(a[:], difff[:].unsqueeze(2).broadcast_to(wide), offf[:].unsqueeze(1).broadcast_to(wide), ALU.not_equal))
                chain(v.tensor_scalar(a[:], a[:], MASKED, None, ALU.mult))
                chain(v.tensor_tensor(a[:], a[:], pb[:].unsqueeze(1).broadcast_to(wide), ALU.add))
                chain(v.tensor_reduce(mx[:], a[:], AX_X, ALU.max))
                chain(v.tensor_tensor(a[:], a[:], mx[:].unsqueeze(2).broadcast_to(wide), ALU.subtract))
                v.sem_inc(to_act, 1)
                v.wait_ge(act_done, 1)
                v.tensor_reduce(sm[:], a[:], AX_X, ALU.add).then_inc(to_act, 1)
                v.wait_ge(act_done, 2)
                v.wait_ge(row_ready, 1)
                v.tensor_tensor(row[:, 0:T], sm[:], mx[:], ALU.add).then_inc(row_ready, 1)

            @block.scalar
            def _(s):
                s.wait_ge(to_act, 1)
                s.activation(a[:], a[:], ACT.Exp).then_inc(act_done, 1)
                s.wait_ge(to_act, 2)
                s.activation(sm[:], sm[:], ACT.Ln).then_inc(act_done, 1)


def skewed(scratch, b, H):
    flat = scratch.rearrange("h t r -> h (t r)")
    part = flat[bass.ds(b * H, H), T - 1:T - 1 + T * (RELS - 1)]
    return part.rearrange("h (t r) -> t h r", r=RELS - 1)[:, :, 0:T]



def relative_positions(nc, x, K, wq, bq, wrT, br, scratch):
    H, G = 16, 4
    ident, indcol = K["ident"], K["indcol"]
    with Phase(nc, "l2p") as p:
        w = p.sb("w", [128, KD, G * 128])
        wr = p.sb("wr", [128, RELS])
        bq_sb = p.sb("bq", [128, G])
        xn, xnT, qT = p.sb("xn", [T, 2, D]), p.sb("xnT", [128, 2, KD, T]), p.sb("qT", [128, 2, G, T])
        rp = p.sb("rp", [T, 2, H, RELS])
        pp, pr = p.ps("pp", [128, 2, 512]), p.ps("pr", [128, 4, 512])
        st = Norm(p, x, "ln")
        loaded, bq_ready, xn_ready, pp_ready, pp_empty, r_ready, r_out = (
            p.sem(s) for s in ("loaded", "bq_ready", "xn_ready", "pp_ready", "pp_empty", "r_ready", "r_out"))
        stored = [p.sem(f"stored{u}") for u in range(2)]
        lo = REL_WINDOW - (T - 1)
        NR = H // 2
        pairs = [(j, g) for j in range(4) for g in (0, 2)]
        with nc.Block() as block:

            @block.sync
            def _(sp):
                sp.dma_start(w[:], wq.rearrange("(k p) n -> p k n", p=128)).then_inc(loaded, 16)
                sp.dma_start(bq_sb[:], bq).then_inc(loaded, 16)
                for j in range(4):
                    sp.dma_start(wr[32 * j:32 * j + 16, :], wrT[:, lo:lo + RELS]).then_inc(loaded, 16)
                    sp.dma_start(wr[32 * j + 16:32 * j + 17, :], br[lo:lo + RELS].rearrange("(a n) -> a n", a=1)).then_inc(loaded, 16)

                def body(b, u, i):
                    sp.wait_ge(r_out, (b + 1) * NR)
                    sp.dma_start(scratch[bass.ds(b * H, H)].rearrange("h t r -> t h r"), rp[:, u, :, :]).then_inc(stored[u], 16)

                over_batches(sp, body)
                for u in range(2):
                    sp.wait_ge(stored[u], 16 * NPAIR)

            @block.tensor
            def _(pe):
                pe.wait_ge(loaded, 16 * 10)

                def body(b, u, i):
                    pe.wait_ge(xn_ready, b + 1)
                    wait(pe, pp_empty, b * 2 - 1)
                    for k in range(KD):
                        last = pe.transpose(pp[:, 0, k * T:(k + 1) * T], xn[:, u, k * 128:(k + 1) * 128], ident[0:T, 0:T])
                    last.then_inc(pp_ready, 1)
                    pe.wait_ge(pp_empty, b * 2 + 1)
                    for g in range(G):
                        for k in range(KD):
                            last = pe.matmul(pp[:, 1, g * T:(g + 1) * T], w[:, k, g * 128:(g + 1) * 128], xnT[:, u, k, :],
                                             start=k == 0, stop=k == KD - 1)
                    last.then_inc(pp_ready, 1)
                    pe.wait_ge(pp_empty, b * 2 + 2)
                    for n, (j, g0) in enumerate(pairs):
                        wait(pe, r_out, reuse(b, n, NR, 4))
                        for c in range(2):
                            r = slice(32 * j, 32 * j + 17)
                            last = pe.matmul(pr[0:T, n % 4, c * RELS:(c + 1) * RELS], qT[r, u, g0 + c, :], wr[r, :], start=True, stop=True)
                        last.then_inc(r_ready, 1)

                over_batches(pe, body)

            @block.scalar
            def _(a):
                st.scalar(a)
                a.wait_ge(bq_ready, 1)

                def body(b, u, i):
                    a.wait_ge(pp_ready, b * 2 + 1)
                    a.activation(xnT[:, u].rearrange("p k t -> p (k t)"), pp[:, 0, 0:KD * T], ACT.Copy).then_inc(pp_empty, 1)
                    a.wait_ge(pp_ready, b * 2 + 2)
                    for g in range(G):
                        last = a.activation(qT[:, u, g, :], pp[:, 1, g * T:(g + 1) * T], ACT.Identity, bias=bq_sb[:, g:g + 1])
                    last.then_inc(pp_empty, 1)

                over_batches(a, body)

            @block.vector
            def _(v):
                st.vector(v)
                v.wait_ge(loaded, 16 * 10)
                v.tensor_tensor(bq_sb[:], bq_sb[:], indcol[:, 0:1].broadcast_to([128, G]), ALU.add).then_inc(bq_ready, 1)

                def body(b, u, i):
                    wait(v, pp_ready, b * 2 - 3)
                    st.rows(v, b, xn[:, u, :], xn_ready)
                    wait(v, stored[u], i * 16)
                    for n, (j, g0) in enumerate(pairs):
                        v.wait_ge(r_ready, b * NR + n + 1)
                        dst = rp[:, u].rearrange("p (g j) r -> p j g r", j=4)[:, j, g0:g0 + 2, :]
                        v.tensor_copy(dst, pr[0:T, n % 4, 0:2 * RELS].rearrange("p (c r) -> p c r", c=2)).then_inc(r_out, 1)

                over_batches(v, body)



def normed_transposed(nc, name, y, K, xnT_all, norm_scale):
    ident = K["ident"]
    with Phase(nc, name + "n") as p:
        xn, xnT = p.sb("xn", [T, 2, D]), p.sb("xnT", [128, 2, KD, T])
        ns_sb = p.sb("ns", [T, D])
        ptx = p.ps("ptx", [128, 2, 512])
        st = Norm(p, y, "rms")
        loaded, xn_ready, tx_ready, xT_ready, all_ready, h_done = (
            p.sem(s) for s in ("loaded", "xn_ready", "tx_ready", "xT_ready", "all_ready", "h_done"))
        with nc.Block() as block:

            @block.sync
            def _(sp):
                sp.dma_start(ns_sb[:], row_bcast(norm_scale, T)).then_inc(loaded, 16)

            @block.tensor
            def _(pe):
                def body(b, u, i):
                    pe.wait_ge(xn_ready, b + 1)
                    wait(pe, xT_ready, b - 1)
                    for k in range(KD):
                        last = pe.transpose(ptx[:, u, k * T:(k + 1) * T], xn[:, u, k * 128:(k + 1) * 128], ident[0:T, 0:T])
                    last.then_inc(tx_ready, 1)

                over_batches(pe, body)

            @block.scalar
            def _(a):
                st.scalar(a)

                def body(b, u, i):
                    a.wait_ge(tx_ready, b + 1)
                    wait(a, all_ready, b - 1)
                    a.activation(xnT[:, u].rearrange("p k t -> p (k t)"), ptx[:, u, 0:KD * T], ACT.Copy).then_inc(xT_ready, 1)

                over_batches(a, body)

            @block.vector
            def _(v):
                st.vector(v)
                v.wait_ge(loaded, 16)

                def body(b, u, i):
                    wait(v, tx_ready, b - 1)
                    st.rows(v, b, xn[:, u, :], xn_ready, h=y, h_done=h_done, scale_row=ns_sb[:])
                    v.wait_ge(xT_ready, b + 1)
                    v.tensor_scalar(xnT_all[:, :, bass.ds(b * T, T)], xnT[:, u, :, :], 1.0, None, ALU.mult).then_inc(all_ready, 1)

                over_batches(v, body)



class Route:

    def __init__(self, ctx, nc, name, choices, S, capacity):
        def sb(n, shape, dt):
            return ctx.enter_context(nc.sbuf_tensor(f"{name}_{n}", shape, dt))

        self.choices, self.S, self.capacity = choices, S, capacity
        self.tiles = NE if capacity else (NB * T * choices + NE * (S - 1)) // S
        self.put = sb("put", [T, choices, NB], U32)
        self.get = sb("get", [T, choices, NB], U32)
        self.wt = sb("wt", [T, choices, NB], F32)
        self.expert = sb("expert", [1, self.tiles], I32)
        subs = -(-S // 128)
        self.sub = [min(-(-S // subs), S - i * -(-S // subs)) for i in range(subs)]


def route(nc, name, x, K, R, first_wins, wg, bg, slots):
    ident, ones = K["ident"], K["ones"]
    S = R.S
    with Phase(nc, name + "g") as p:
        xn, xnT, xn_all = p.sb("xn", [T, 2, D]), p.sb("xnT", [128, 2, KD, T]), p.sb("xn_all", [T, NB, D])
        wg_sb, bg_sb = p.sb("wg", [128, KD, NE]), p.sb("bg", [T, NE])
        ptx, plg = p.ps("ptx", [128, 2, 512]), p.ps("plg", [128, 2, 512])
        st = Norm(p, x, "ln")
        big = [T, NB, NE]
        lg, pr, rem, eq, key, chosen, cnt, slot = (p.sb(s, big) for s in ("lg", "pr", "rem", "eq", "key", "chosen", "cnt", "slot"))
        oh = [p.sb(f"oh{k}", big) for k in range(R.choices)]
        pref, prefi = p.sb("pref", [T, NE]), p.sb("prefi", [T, NE], I32)
        m = p.sb("m", [T, NB])
        tot, nt, nti, incl, base, basei = (p.sb(s, [T, NE], dt) for s, dt in (("tot", F32), ("nt", F32), ("nti", I32), ("incl", F32), ("base", F32), ("basei", I32)))
        tokeni, token = p.sb("tokeni", [T, NB], I32), p.sb("token", [T, NB])
        jti, jt, jte, je = p.sb("jti", [1, R.tiles], I32), p.sb("jt", [1, R.tiles]), p.sb("jte", [1, R.tiles, NE]), p.sb("je", [1, R.tiles])
        sl, kp = p.sb("sl", [T, NB]), p.sb("kp", [T, NB])
        loaded, xn_ready, tx_ready, xT_ready, l_ready, l_out, xa_ready = (
            p.sem(s) for s in ("loaded", "xn_ready", "tx_ready", "xT_ready", "l_ready", "l_out", "xa_ready"))
        steps, iota_done, to_act, act_done, to_pe, pe_done, put_ready = (
            p.sem(s) for s in ("steps", "iota_done", "to_act", "act_done", "to_pe", "pe_done", "put_ready"))
        sent = K["rows_sent"]
        loads = [(wg_sb[:], wg.rearrange("(k p) n -> p k n", p=128))]
        if bg is not None:
            loads.append((bg_sb[:], row_bcast(bg, T)))
        with nc.Block() as block:

            @block.sync
            def _(sp):
                for dst, src in loads:
                    sp.dma_start(dst, src).then_inc(loaded, 16)

            @block.gpsimd
            def _(g):
                g.iota(prefi[:], pattern=[[-1 if first_wins else 1, NE]], base=NE if first_wins else 1, channel_multiplier=0).then_inc(iota_done, 1)
                g.iota(basei[:], pattern=[[S, NE]], base=0, channel_multiplier=0).then_inc(iota_done, 1)
                g.iota(jti[:], pattern=[[1, R.tiles]], base=0, channel_multiplier=0).then_inc(iota_done, 1)
                g.iota(tokeni[:], pattern=[[T, NB]], base=R.tiles * S, channel_multiplier=1).then_inc(iota_done, 1)
                g.wait_ge(xa_ready, NB)
                for k in range(R.choices):
                    g.wait_ge(put_ready, k + 1)
                    for b in range(NB):
                        g.indirect_dma_start(slots, bass.IndirectOffsetOnAxis(ap=R.put[:, k, b:b + 1], axis=0),
                                             xn_all[:, b, :], None).then_inc(sent.sem, 16)
                sent.base += 16 * NB * R.choices
                g.wait_ge(sent.sem, sent.base)

            @block.tensor
            def _(pe):
                pe.wait_ge(loaded, 16 * len(loads))

                def body(b, u, i):
                    pe.wait_ge(xn_ready, b + 1)
                    wait(pe, xT_ready, b - 1)
                    for k in range(KD):
                        last = pe.transpose(ptx[:, u, k * T:(k + 1) * T], xn[:, u, k * 128:(k + 1) * 128], ident[0:T, 0:T])
                    last.then_inc(tx_ready, 1)
                    pe.wait_ge(xT_ready, b + 1)
                    wait(pe, l_out, b - 1)
                    for k in range(KD):
                        last = pe.matmul(plg[0:T, u, 0:NE], xnT[:, u, k, :], wg_sb[:, k, :], start=k == 0, stop=k == KD - 1)
                    last.then_inc(l_ready, 1)

                over_batches(pe, body)
                pe.wait_ge(to_pe, 1)
                pe.wait_ge(xT_ready, NB)
                pe.matmul(ptx[0:T, 0, 0:NB * NE], K["upto"][0:T, 0:T], chosen[:].rearrange("p b e -> p (b e)"), start=True, stop=False)
                pe.matmul(ptx[0:T, 0, 0:NB * NE], ones[0:T, 0:T], cnt[:].rearrange("p b e -> p (b e)"), start=False, stop=True)
                pe.matmul(ptx[0:T, 1, 0:NE], ones[0:T, 0:T], tot[:], start=True, stop=True).then_inc(pe_done, 1)

            @block.scalar
            def _(a):
                st.scalar(a)

                def body(b, u, i):
                    a.wait_ge(tx_ready, b + 1)
                    wait(a, l_ready, b - 1)
                    a.activation(xnT[:, u].rearrange("p k t -> p (k t)"), ptx[:, u, 0:KD * T], ACT.Copy).then_inc(xT_ready, 1)

                over_batches(a, body)
                a.wait_ge(to_act, 1)
                a.activation(pr[:], lg[:], ACT.Exp).then_inc(act_done, 1)

            @block.vector
            def _(v):
                n = 0

                def chain(ins):
                    nonlocal n
                    n += 1
                    ins.then_inc(steps, 1)
                    v.wait_ge(steps, n)

                def wide(t):
                    return t[:].unsqueeze(2).broadcast_to(big)

                def across(t):
                    return t[:].unsqueeze(1).broadcast_to(big)

                st.vector(v)
                v.wait_ge(loaded, 16 * len(loads))
                v.wait_ge(iota_done, 4)
                v.tensor_copy(pref[:], prefi[:]).then_inc(steps, 1)
                v.tensor_copy(base[:], basei[:]).then_inc(steps, 1)
                v.tensor_copy(jt[:], jti[:]).then_inc(steps, 1)
                n += 3
                chain(v.tensor_copy(token[:], tokeni[:]))

                def body(b, u, i):
                    wait(v, tx_ready, b - 1)
                    st.rows(v, b, xn[:, u, :], xn_ready)
                    st.rows(v, b, batch(xn_all, b), xa_ready)
                    v.wait_ge(l_ready, b + 1)
                    if bg is not None:
                        v.tensor_tensor(batch(lg, b), plg[0:T, u, 0:NE], bg_sb[:], ALU.add).then_inc(l_out, 1)
                    else:
                        v.tensor_copy(batch(lg, b), plg[0:T, u, 0:NE]).then_inc(l_out, 1)

                over_batches(v, body)
                v.wait_ge(l_out, NB)
                chain(v.tensor_reduce(m[:], lg[:], AX_X, ALU.max))
                v.tensor_tensor(lg[:], lg[:], wide(m), ALU.subtract).then_inc(to_act, 1)
                v.wait_ge(act_done, 1)
                chain(v.tensor_reduce(m[:], pr[:], AX_X, ALU.add))
                chain(v.reciprocal(m[:], m[:]))
                chain(v.tensor_tensor(pr[:], pr[:], wide(m), ALU.mult))

                def pick(src, out):
                    chain(v.tensor_reduce(m[:], src[:], AX_X, ALU.max))
                    chain(v.tensor_tensor(eq[:], src[:], wide(m), ALU.is_equal))
                    chain(v.tensor_tensor(key[:], eq[:], across(pref), ALU.mult))
                    chain(v.tensor_reduce(m[:], key[:], AX_X, ALU.max))
                    chain(v.tensor_tensor(out[:], key[:], wide(m), ALU.is_equal))

                pick(pr, oh[0])
                if R.choices == 2:
                    chain(v.scalar_tensor_tensor(rem[:], oh[0][:], -2.0, pr[:], ALU.mult, ALU.add))
                    pick(rem, oh[1])
                    chain(v.tensor_tensor(chosen[:], oh[0][:], oh[1][:], ALU.add))
                else:
                    chain(v.tensor_copy(chosen[:], oh[0][:]))
                chain(v.memset(cnt[:, 0, :], 0.0))
                for b in range(1, NB):
                    chain(v.tensor_tensor(cnt[:, b, :], cnt[:, b - 1, :], chosen[:, b - 1, :], ALU.add))
                v.tensor_tensor(tot[:], cnt[:, NB - 1, :], chosen[:, NB - 1, :], ALU.add).then_inc(to_pe, 1)
                v.wait_ge(pe_done, 1)
                place = ptx[0:T, 0, 0:NB * NE].rearrange("p (b e) -> p b e", e=NE)
                if not R.capacity:
                    chain(v.tensor_scalar(nti[:], ptx[0:T, 1, 0:NE], float(S - 1), None, ALU.add))
                    chain(v.tensor_scalar(nti[:], nti[:], S.bit_length() - 1, None, ALU.logical_shift_right))
                    chain(v.tensor_copy(nt[:], nti[:]))
                    chain(v.tensor_tensor_scan(incl[:], ones[0:T, 0:NE], nt[:], 0.0, ALU.mult, ALU.add))
                    chain(v.tensor_tensor(base[:], incl[:], nt[:], ALU.subtract))
                    chain(v.tensor_scalar(base[:], base[:], float(S), None, ALU.mult))
                    js = [1, R.tiles, NE]
                    chain(v.tensor_tensor(jte[:], jt[:].unsqueeze(2).broadcast_to(js), incl[0:1, :].unsqueeze(1).broadcast_to(js), ALU.is_ge))
                    chain(v.tensor_reduce(je[:], jte[:], AX_X, ALU.add))
                    chain(v.tensor_scalar(R.expert[:], je[:], float(NE - 1), None, ALU.min))
                else:
                    chain(v.tensor_scalar(key[:], place, float(CAPACITY), None, ALU.is_le))
                    chain(v.tensor_tensor(eq[:], key[:], chosen[:], ALU.mult))
                    chain(v.tensor_reduce(kp[:], eq[:], AX_X, ALU.add))
                chain(v.tensor_tensor(slot[:], place, across(base), ALU.add))
                for k in range(R.choices):
                    chain(v.tensor_tensor(eq[:], oh[k][:], slot[:], ALU.mult))
                    chain(v.tensor_reduce(sl[:], eq[:], AX_X, ALU.add))
                    chain(v.tensor_scalar(sl[:], sl[:], -1.0, None, ALU.add))
                    chain(v.tensor_tensor(key[:], oh[k][:], pr[:], ALU.mult))
                    chain(v.tensor_reduce(R.wt[:, k, :], key[:], AX_X, ALU.add))
                    if R.capacity:
                        chain(v.tensor_tensor(R.wt[:, k, :], R.wt[:, k, :], kp[:], ALU.mult))
                        chain(v.tensor_tensor(sl[:], sl[:], kp[:], ALU.mult))
                        chain(v.tensor_copy(R.get[:, k, :], sl[:]))
                        chain(v.tensor_scalar(kp[:], kp[:], -1.0, 1.0, ALU.mult, ALU.add))
                        chain(v.tensor_tensor(token[:], token[:], kp[:], ALU.mult))
                        chain(v.tensor_tensor(sl[:], sl[:], token[:], ALU.add))
                    else:
                        chain(v.tensor_copy(R.get[:, k, :], sl[:]))
                    v.tensor_copy(R.put[:, k, :], sl[:]).then_inc(put_ready, 1)


def over_tiles(eng, n, body):
    for u in range(2):
        body(u, u, 0)
    with eng.Fori(1, n // 2) as i:
        for u in range(2):
            body(i * 2 + u, u, i)
    if n % 2:
        body(n - 1, 0, n // 2)


def routed_experts(nc, name, K, R, slots, outs, w_up, w_gate, w_down, b_up, b_gate, b_down, act):
    ident, ones = K["ident"], K["ones"]
    S, NTL = R.S, R.tiles
    HID = w_up.shape[2]
    NM = HID // 128
    two = w_gate is not None
    NS = len(R.sub)
    SUB = R.sub[0]
    NY = 3
    with Phase(nc, name + "e") as p:
        wu = p.sb("wu", [128, 2, KD, HID])
        wg = p.sb("wg", [128, 2, KD, HID]) if two else None
        wd = p.sb("wd", [128, 2, NM, D])
        bu = p.sb("bu", [128, 2, NM]) if b_up is not None else None
        bg = p.sb("bg", [128, 2, NM]) if b_gate is not None else None
        bd = p.sb("bd", [1, 2, D]) if b_down is not None else None
        xs = p.sb("xs", [SUB, 2, NS, D])
        xT = p.sb("xT", [128, 2, KD, S])
        hT = p.sb("hT", [128, 2, NM, S])
        hs = p.sb("hs", [128, 2, S])
        hp = p.sb("hp", [128, 2, S])
        ys = p.sb("ys", [SUB, 2, NS, D])
        pt = p.ps("pt", [128, KD, 512])
        ph = p.ps("ph", [128, 2, 512])
        py = p.ps("py", [128, NY, 512])
        w_in = [p.sem(f"w_in{u}") for u in range(2)]
        x_in = [p.sem(f"x_in{u}") for u in range(2)]
        y_sent = K["tile_stored"]
        t_ready = p.sem("t_ready")
        t_out = p.sem("t_out")
        h_ready = p.sem("h_ready")
        h_half = p.sem("h_half")
        h_prod = p.sem("h_prod")
        h_out = p.sem("h_out")
        y_ready = p.sem("y_ready")
        y_out = p.sem("y_out")
        extra = [(t, src) for t, src in ((bu, b_up), (bg, b_gate)) if t is not None]
        n_w = 2 + two + len(extra) + (b_down is not None)

        def hb(j, u, m):
            return ph[:, m % 2, :]

        def yb(u, s):
            return s if NS > 1 else u

        def y_sent_before(j, u):
            return (j - u) // 2 * (16 * NS) if isinstance(j, int) else (j - u) * (8 * NS)

        stores = [16 * NS * ((NTL + 1 - u) // 2) for u in range(2)]

        with nc.Block() as block:

            @block.sync
            def _(sp):
                def body(j, u, i):
                    if R.capacity:
                        e = j
                    else:
                        e = sp.value_load(R.expert[0:1, bass.ds(j, 1)], min_val=0, max_val=NE - 1)
                    one = bass.ds(e, 1)
                    wait(sp, t_ready, j - 1)
                    for s, n in enumerate(R.sub):
                        sp.dma_start(xs[0:n, u, s, :], slots[bass.ds(j * S + s * SUB, n), :]).then_inc(x_in[u], 16)
                    wait(sp, y_ready, (j - 1) * NS)
                    for t, src in extra:
                        sp.dma_start(t[:, u, :], src[one].rearrange("e p m -> p (e m)")).then_inc(w_in[u], 16)
                    sp.dma_start(wu[:, u], w_up[one].rearrange("e (k p) n -> p (e k) n", p=128)).then_inc(w_in[u], 16)
                    if two:
                        sp.dma_start(wg[:, u], w_gate[one].rearrange("e (k p) n -> p (e k) n", p=128)).then_inc(w_in[u], 16)
                    sp.dma_start(wd[:, u], w_down[one].rearrange("e (k p) n -> p (e k) n", p=128)).then_inc(w_in[u], 16)
                    if bd is not None:
                        sp.dma_start(bd[:, u, :], b_down[one]).then_inc(w_in[u], 16)

                over_tiles(sp, NTL, body)

            @block.gpsimd
            def _(g):
                def body(j, u, i):
                    g.wait_ge(y_out, (j + 1) * NS)
                    for s, n in enumerate(R.sub):
                        g.dma_start(outs[bass.ds(j * S + s * SUB, n), :], ys[0:n, u, s, :]).then_inc(y_sent[u].sem, 16)

                over_tiles(g, NTL, body)
                for u in range(2):
                    g.wait_ge(y_sent[u].sem, y_sent[u].base + stores[u])

            @block.tensor
            def _(pe):
                def turn(j, u, i):
                    pe.wait_ge(x_in[u], i * (16 * NS) + 16 * NS)
                    wait(pe, t_out, j)
                    for k in range(KD):
                        for s, n in enumerate(R.sub):
                            last = pe.transpose(pt[:, k, s * SUB:s * SUB + n], xs[0:n, u, s, k * 128:(k + 1) * 128], ident[0:n, 0:n])
                    last.then_inc(t_ready, 1)

                def hidden(j, u, m):
                    wait(pe, h_out, j * NM + m - 1)
                    for c, w in enumerate((wu, wg)[0:1 + two]):
                        for k in range(KD):
                            last = pe.matmul(hb(j, u, m)[:, c * S:(c + 1) * S], w[:, u, k, m * 128:(m + 1) * 128], xT[:, u, k, :],
                                             start=k == 0, stop=k == KD - 1)
                    last.then_inc(h_ready, 1)

                def down(j, u):
                    pe.wait_ge(h_out, (j + 1) * NM)
                    for s, n in enumerate(R.sub):
                        wait(pe, y_out, (j - 1) * NS + s + 1 if NS > 1 else j - 1)
                        out = py[0:n, yb(u, s), 0:D]
                        for m in range(NM):
                            last = pe.matmul(out, hT[:, u, m, s * SUB:s * SUB + n], wd[:, u, m, :], start=m == 0,
                                             stop=m == NM - 1 and bd is None)
                        if bd is not None:
                            last = pe.matmul(out, ones[0:1, 0:n], bd[0:1, u, :], start=False, stop=True)
                        last.then_inc(y_ready, 1)

                def body(j, u, i):
                    turn(j, u, i)
                    if not (isinstance(j, int) and j == 0):
                        down(j - 1, 1 - u)
                    pe.wait_ge(t_out, j + 1)
                    pe.wait_ge(w_in[u], i * (16 * n_w) + 16 * n_w)
                    for m in range(NM):
                        hidden(j, u, m)

                over_tiles(pe, NTL, body)
                down(NTL - 1, (NTL - 1) % 2)

            @block.scalar
            def _(a):
                def body(j, u, i):
                    a.wait_ge(t_ready, j + 1)
                    for k in range(KD):
                        last = a.activation(xT[:, u, k, :], pt[:, k, 0:S], ACT.Copy)
                    last.then_inc(t_out, 1)
                    for m in range(NM):
                        up, gt = hb(j, u, m)[:, 0:S], hb(j, u, m)[:, S:2 * S] if two else None
                        a.wait_ge(h_ready, j * NM + m + 1)
                        if act == "relu":
                            a.activation(hT[:, u, m, :], up, ACT.Relu, bias=bu[:, u, m:m + 1]).then_inc(h_out, 1)
                        if act == "swiglu":
                            wait(a, h_out, j * NM + m - 1)
                            a.activation(hs[:, m % 2, :], gt, ACT.Silu).then_inc(h_half, 1)
                        if act == "silu_of_product":
                            wait(a, h_prod, j * NM + m - 1)
                            a.activation(hs[:, m % 2, :], gt, ACT.Identity, bias=bg[:, u, m:m + 1]).then_inc(h_half, 1)
                            a.wait_ge(h_prod, j * NM + m + 1)
                            a.activation(hT[:, u, m, :], hp[:, m % 2, :], ACT.Silu).then_inc(h_out, 1)

                over_tiles(a, NTL, body)

            @block.vector
            def _(v):
                def out(j, u):
                    if not (isinstance(j, int) and j < 2):
                        v.wait_ge(y_sent[u].sem, y_sent[u].base + y_sent_before(j, u))
                    for s, n in enumerate(R.sub):
                        v.wait_ge(y_ready, j * NS + s + 1)
                        v.tensor_copy(ys[0:n, u, s, :], py[0:n, yb(u, s), 0:D]).then_inc(y_out, 1)

                def body(j, u, i):
                    if not (isinstance(j, int) and j == 0):
                        out(j - 1, 1 - u)
                    for m in range(NM if two else 0):
                        up = hb(j, u, m)[:, 0:S]
                        v.wait_ge(h_half, j * NM + m + 1)
                        if act == "swiglu":
                            v.tensor_tensor(hT[:, u, m, :], up, hs[:, m % 2, :], ALU.mult).then_inc(h_out, 1)
                        if act == "silu_of_product":
                            wait(v, h_out, j * NM + m - 1)
                            v.scalar_tensor_tensor(hp[:, m % 2, :], up, bu[:, u, m:m + 1], hs[:, m % 2, :],
                                                   ALU.add, ALU.mult).then_inc(h_prod, 1)

                over_tiles(v, NTL, body)
                out(NTL - 1, (NTL - 1) % 2)

        for u in range(2):
            y_sent[u].base += stores[u]


def combine(nc, name, K, R, outs, acc, first):
    QB = 4
    with Phase(nc, name + "c") as p:
        y = p.sb("y", [T, NB, R.choices, D])
        got = K["rows_got"]
        step = p.sem("step")
        with nc.Block() as block:

            @block.gpsimd
            def _(g):
                for b in range(NB):
                    for k in range(R.choices):
                        g.indirect_dma_start(y[:, b, k, :], None, outs, bass.IndirectOffsetOnAxis(ap=R.get[:, k, b:b + 1], axis=0)).then_inc(got[b // QB].sem, 16)

            @block.vector
            def _(v):
                n = 0
                for b in range(NB):
                    if b % QB == 0:
                        got[b // QB].base += 16 * QB * R.choices
                        v.wait_ge(got[b // QB].sem, got[b // QB].base)
                    for k in range(R.choices):
                        w = R.wt[:, k, b:b + 1]
                        if k:
                            v.wait_ge(step, n)
                        n += 1
                        if first and k == 0:
                            v.tensor_scalar(acc[:, b, :], y[:, b, k, :], w, None, ALU.mult).then_inc(step, 1)
                        else:
                            v.scalar_tensor_tensor(acc[:, b, :], y[:, b, k, :], w, acc[:, b, :], ALU.mult, ALU.add).then_inc(step, 1)



CB = 4
NCH = NB // CB
CT = CB * T


def experts(nc, name, K, xnT_all, wts, acc, w_up, w_gate, w_down, b_up, b_gate, act, n_exp=NE):
    HID = w_up.shape[2]
    tiles = [min(128, HID - 128 * m) for m in range(-(-HID // 128))]
    NM = len(tiles)
    FULL = HID // 128
    two = w_gate is not None
    NHB = 2 if two else 1
    with Phase(nc, name + "e") as p:
        wu = p.sb("wu", [128, 2, KD, HID])
        wg = p.sb("wg", [128, 2, KD, HID]) if two else None
        wd = p.sb("wd", [128, 2, NM, D])
        bu = p.sb("bu", [128, 2, NM]) if b_up is not None else None
        bg = p.sb("bg", [128, 2, NM]) if b_gate is not None else None
        hT = p.sb("hT", [128, 2, NM, CT])
        hs = p.sb("hs", [128, 2, CT])
        hp = p.sb("hp", [128, 2, CT])
        ph = p.ps("ph", [128, 4, 512])
        py = p.ps("py", [128, 4, 512])
        HR = 2
        w_in = [p.sem(f"w_in{u}") for u in range(2)]
        h_ready = p.sem("h_ready")
        h_half = p.sem("h_half")
        h_prod = p.sem("h_prod")
        h_out = p.sem("h_out")
        y_ready = p.sem("y_ready")
        y_out = p.sem("y_out")
        n_w = 2 + two + (FULL < NM) + (b_up is not None) + (b_gate is not None)
        NPAIRE = max(1, n_exp // 2)

        def over_experts(eng, body):
            if n_exp == 1:
                for c in range(NCH):
                    body(0, 0, 0, c)
                return
            for u in range(2):
                for c in range(NCH):
                    body(u, u, 0, c)
            with eng.Fori(1, NPAIRE) as i:
                for u in range(2):
                    for c in range(NCH):
                        body(i * 2 + u, u, i, c)

        with nc.Block() as block:

            @block.sync
            def _(sp):
                def body(e, u, i, c):
                    if c:
                        return
                    wait(sp, y_ready, (e - 1) * NB)
                    one = bass.ds(e, 1)
                    for t, src in ((bu, b_up), (bg, b_gate)):
                        if t is not None:
                            sp.dma_start(t[:, u, :], src[one].rearrange("e p m -> p (e m)")).then_inc(w_in[u], 16)
                    sp.dma_start(wu[:, u], w_up[one].rearrange("e (k p) n -> p (e k) n", p=128)).then_inc(w_in[u], 16)
                    if two:
                        sp.dma_start(wg[:, u], w_gate[one].rearrange("e (k p) n -> p (e k) n", p=128)).then_inc(w_in[u], 16)
                    sp.dma_start(wd[:, u, 0:FULL, :], w_down[one, 0:FULL * 128, :].rearrange("e (k p) n -> p (e k) n", p=128)).then_inc(w_in[u], 16)
                    if FULL < NM:
                        sp.dma_start(wd[0:tiles[-1], u, FULL, :], w_down[one, FULL * 128:HID, :].rearrange("e p n -> p (e n)")).then_inc(w_in[u], 16)

                over_experts(sp, body)

            @block.tensor
            def _(pe):
                def hidden(e, u, i, c, m):
                    n = c * NM + m
                    wait(pe, h_out, reuse(e, n, NCH * NM, HR))
                    for w, k0 in ((wu, 0), (wg, 1))[0:NHB]:
                        bank = n % HR * 2 + k0
                        for k in range(KD):
                            last = pe.matmul(ph[0:tiles[m], bank, 0:CT], w[:, u, k, m * 128:m * 128 + tiles[m]],
                                             xnT_all[:, k, c * CT:(c + 1) * CT], start=k == 0, stop=k == KD - 1)
                    last.then_inc(h_ready, 1)

                def down(e, u, c, t):
                    n = c * CB + t
                    pe.wait_ge(h_out, e * (NCH * NM) + (c + 1) * NM)
                    wait(pe, y_out, reuse(e, n, NB, 4))
                    for m in range(NM):
                        last = pe.matmul(py[0:T, n % 4, 0:D], hT[0:tiles[m], c % 2, m, t * T:(t + 1) * T], wd[0:tiles[m], u, m, :],
                                         start=m == 0, stop=m == NM - 1)
                    last.then_inc(y_ready, 1)

                def body(e, u, i, c):
                    if c == 0:
                        pe.wait_ge(w_in[u], i * 16 * n_w + 16 * n_w)
                    for m in range(NM):
                        hidden(e, u, i, c, m)
                    if c:
                        for t in range(CB):
                            down(e, u, c - 1, t)
                    if c == NCH - 1:
                        for t in range(CB):
                            down(e, u, c, t)

                over_experts(pe, body)

            def bias(t, u, m):
                return t[0:tiles[m], u, m:m + 1]

            @block.scalar
            def _(a):
                def body(e, u, i, c):
                    for m in range(NM):
                        n, P = c * NM + m, tiles[m]
                        N = NCH * NM
                        up, gt = ph[0:P, n % HR * 2, 0:CT], ph[0:P, n % HR * 2 + 1, 0:CT]
                        a.wait_ge(h_ready, e * N + n + 1)
                        if m == 0:
                            wait(a, y_ready, reuse(e, c, NCH, 2) * CB)
                        if act == "relu":
                            a.activation(hT[0:P, c % 2, m, :], up, ACT.Relu, bias=bias(bu, u, m)).then_inc(h_out, 1)
                        if act == "swiglu":
                            wait(a, h_out, reuse(e, n, N, 2))
                            a.activation(hs[0:P, n % 2, :], gt, ACT.Silu).then_inc(h_half, 1)
                        if act == "silu_of_product":
                            wait(a, h_prod, reuse(e, n, N, 2))
                            a.activation(hs[0:P, n % 2, :], gt, ACT.Identity, bias=bias(bg, u, m)).then_inc(h_half, 1)
                            a.wait_ge(h_prod, e * N + n + 1)
                            a.activation(hT[0:P, c % 2, m, :], hp[0:P, n % 2, :], ACT.Silu).then_inc(h_out, 1)

                over_experts(a, body)

            @block.vector
            def _(v):
                N = NCH * NM

                def add(e, c, t):
                    n = c * CB + t
                    v.wait_ge(y_ready, e * NB + n + 1)
                    if wts is None:
                        v.tensor_tensor(batch(acc, n), batch(acc, n), py[0:T, n % 4, 0:D], ALU.add).then_inc(y_out, 1)
                    else:
                        v.scalar_tensor_tensor(batch(acc, n), py[0:T, n % 4, 0:D], wts[:, n, bass.ds(e, 1)],
                                               batch(acc, n), ALU.mult, ALU.add).then_inc(y_out, 1)

                def body(e, u, i, c):
                    for m in range(NM):
                        n, P = c * NM + m, tiles[m]
                        up = ph[0:P, n % HR * 2, 0:CT]
                        if act == "swiglu":
                            v.wait_ge(h_half, e * N + n + 1)
                            if m == 0:
                                wait(v, y_ready, reuse(e, c, NCH, 2) * CB)
                            v.tensor_tensor(hT[0:P, c % 2, m, :], up, hs[0:P, n % 2, :], ALU.mult).then_inc(h_out, 1)
                        if act == "silu_of_product":
                            v.wait_ge(h_half, e * N + n + 1)
                            wait(v, h_out, reuse(e, n, N, 2))
                            v.scalar_tensor_tensor(hp[0:P, n % 2, :], up, bias(bu, u, m), hs[0:P, n % 2, :],
                                                   ALU.add, ALU.mult).then_inc(h_prod, 1)
                    if c:
                        for t in range(CB):
                            add(e, c - 1, t)
                    if c == NCH - 1:
                        for t in range(CB):
                            add(e, c, t)

                over_experts(v, body)


def linear(nc, name, K, src, w, bias, dest):
    ident, ones = K["ident"], K["ones"]
    with Phase(nc, name) as p:
        w_sb, b_sb = p.sb("w", [128, KD, D]), p.sb("b", [1, D])
        st, sT = p.sb("st", [T, 2, D]), p.sb("sT", [128, 2, KD, T])
        pt, py = p.ps("pt", [128, 2, 512]), p.ps("py", [128, 2, 512])
        loaded, s_ready, t_ready, t_out, y_ready, y_out = (p.sem(s) for s in ("loaded", "s_ready", "t_ready", "t_out", "y_ready", "y_out"))
        with nc.Block() as block:

            @block.sync
            def _(sp):
                sp.dma_start(w_sb[:], w.rearrange("(k p) n -> p k n", p=128)).then_inc(loaded, 16)
                sp.dma_start(b_sb[:], bias.rearrange("(a n) -> a n", a=1)).then_inc(loaded, 16)

            @block.tensor
            def _(pe):
                pe.wait_ge(loaded, 32)

                def body(b, u, i):
                    pe.wait_ge(s_ready, b + 1)
                    wait(pe, t_out, b - 1)
                    for k in range(KD):
                        last = pe.transpose(pt[:, u, k * T:(k + 1) * T], st[:, u, k * 128:(k + 1) * 128], ident[0:T, 0:T])
                    last.then_inc(t_ready, 1)
                    pe.wait_ge(t_out, b + 1)
                    wait(pe, y_out, b - 1)
                    for k in range(KD):
                        pe.matmul(py[0:T, u, 0:D], sT[:, u, k, :], w_sb[:, k, :], start=k == 0, stop=False)
                    pe.matmul(py[0:T, u, 0:D], ones[0:1, 0:T], b_sb[0:1, :], start=False, stop=True).then_inc(y_ready, 1)

                over_batches(pe, body)

            @block.vector
            def _(v):
                def body(b, u, i):
                    wait(v, t_ready, b - 1)
                    v.tensor_scalar(st[:, u, :], batch(src, b), 1.0, None, ALU.mult).then_inc(s_ready, 1)
                    v.wait_ge(t_ready, b + 1)
                    wait(v, y_ready, b - 1)
                    v.tensor_copy(sT[:, u].rearrange("p k t -> p (k t)"), pt[:, u, 0:KD * T]).then_inc(t_out, 1)
                    v.wait_ge(y_ready, b + 1)
                    v.tensor_tensor(batch(dest, b), batch(dest, b), py[0:T, u, 0:D], ALU.add).then_inc(y_out, 1)

                over_batches(v, body)


def add_all(nc, name, dest, src):
    with Phase(nc, name) as p:
        done = p.sem("done")
        with nc.Block() as block:

            @block.vector
            def _(v):
                v.tensor_tensor(dest[:], dest[:], src[:], ALU.add).then_inc(done, 1)



def constants(nc, x, x_dram, K, masks, slots):
    with Phase(nc, "init") as p:
        m1, m2 = p.sb("m1", [1, NB * SK], I32), p.sb("m2", [1, NB * SK], U8)
        fs = p.sb("fs", [1, NB * SK])
        zeros = p.sb("zeros", [128, D])
        x_in, set_done, m_in, ready, ind, mk, z_set, z_out = (
            p.sem(s) for s in ("x_in", "set_done", "m_in", "ready", "ind", "mk", "z_set", "z_out"))
        if1, bk0, fside = masks
        with nc.Block() as block:

            @block.sync
            def _(sp):
                sp.dma_start(x[:], x_dram.rearrange("b t d -> t b d")).then_inc(x_in, 16)
                sp.dma_start(m1[:], if1.rearrange("b s -> (b s)").rearrange("(a n) -> a n", a=1)).then_inc(m_in, 16)
                sp.dma_start(m2[:], bk0.rearrange("b s -> (b s)").rearrange("(a n) -> a n", a=1)).then_inc(m_in, 16)
                sp.dma_start(fs[:], fside.rearrange("b s -> (b s)").rearrange("(a n) -> a n", a=1)).then_inc(m_in, 16)
                sp.wait_ge(z_set, 1)
                n = slots.shape[0] // 128
                sp.dma_start(slots.rearrange("(p n) d -> p n d", p=128), zeros[:].unsqueeze(1).broadcast_to([128, n, D])).then_inc(z_out, 16)
                sp.wait_ge(x_in, 16)
                sp.wait_ge(z_out, 16)

            @block.gpsimd
            def _(g):
                g.memset(K["ident"][:], 0.0).then_inc(set_done, 1)
                g.memset(K["upto"][:], 1.0).then_inc(set_done, 1)
                g.wait_ge(set_done, 2)
                g.affine_select(out=K["ident"][:], in_=K["ident"][:], compare_op=ALU.not_equal, fill=1.0, base=0,
                                pattern=[[-1, 128]], channel_multiplier=1).then_inc(ready, 1)
                g.affine_select(out=K["upto"][:], in_=K["upto"][:], compare_op=ALU.is_ge, fill=0.0, base=0,
                                pattern=[[1, 128]], channel_multiplier=-1).then_inc(ready, 1)

            @block.vector
            def _(v):
                v.memset(zeros[:], 0.0).then_inc(z_set, 1)
                v.memset(K["ones"][:], 1.0).then_inc(ind, 1)
                v.memset(K["indrow"][:], 0.0).then_inc(ind, 1)
                v.wait_ge(ind, 2)
                v.memset(K["indrow"][0:1, :].rearrange("p (j s) -> p j s", s=32)[:, :, 16:17], 1.0).then_inc(ind, 1)
                v.wait_ge(ready, 2)
                v.tensor_reduce(K["indcol"][:, 0:1], K["ident"][:].rearrange("p (j s) -> p s j", s=32)[:, 16, :], AX_X, ALU.add).then_inc(ind, 1)
                v.wait_ge(m_in, 48)
                v.tensor_scalar(K["mask_if1"][:], m1[:], 0.0, MASKED, ALU.is_equal, ALU.mult).then_inc(mk, 1)
                v.tensor_scalar(K["mask_bk0"][:], m2[:], 0.0, MASKED, ALU.is_equal, ALU.mult).then_inc(mk, 1)
                v.wait_ge(mk, 2)
                v.tensor_tensor(K["mask_bk0"][:], K["mask_bk0"][:], fs[:], ALU.add).then_inc(mk, 1)


def decoder(nc, A, out, last_stage=12):
    with ExitStack() as ctx:
        def sb(name, shape, dt=F32):
            return ctx.enter_context(nc.sbuf_tensor(name, shape, dt))

        x = sb("x", [T, NB, D])
        K = {"ident": sb("ident", [128, 128]), "upto": sb("upto", [128, 128]), "ones": sb("ones", [128, 128]),
             "indrow": sb("indrow", [1, 128]), "indcol": sb("indcol", [128, 1])}
        with ExitStack() as mctx:
            K["mask_if1"] = sb("mask_if1", [1, NB * SK])
            K["mask_bk0"] = sb("mask_bk0", [1, NB * SK])
        K["rows_sent"] = Kept(ctx, nc, "rows_sent")
        K["tile_stored"] = [Kept(ctx, nc, f"tile_stored{u}") for u in range(2)]
        K["rows_got"] = [Kept(ctx, nc, f"rows_got{q}") for q in range(4)]
        rows = (2 * NB * T + NE * (MOE_TILE - 1)) // MOE_TILE * MOE_TILE
        slots = nc.dram_tensor("slots", [rows, D], F32, kind="Internal").ap()
        outs = nc.dram_tensor("outs", [rows, D], F32, kind="Internal").ap()
        constants(nc, x, A["x"], K, (A["mask_BxS2_if1"], A["mask_BxS2_bk0"], A["fside_BxS2_0"]), slots)
        ctxT = A["ctxT"]

        def ffn(name, choices, S, capacity, first_wins, wg, bg, w_up, w_gate, w_down, b_up, b_gate, b_down, act, acc, first=False):
            with ExitStack() as c:
                R = Route(c, nc, name, choices, S, capacity)
                route(nc, name, x, K, R, first_wins, wg, bg, slots)
                routed_experts(nc, name, K, R, slots, outs, w_up, w_gate, w_down, b_up, b_gate, b_down, act)
                combine(nc, name, K, R, outs, acc, first)

        def stages():
            channel_attention(nc, x, K, A["L0_attn_w_qkv"], A["L0_attn_w_out"])
            yield
            attention(nc, "l0x", x, K, heads=16, dh=64, dv=64, wq=A["L0_xattn_Wq"], wk=A["L0_xattn_Wk"], wv=A["L0_xattn_Wv"],
                      scale=64 ** -0.5, ctxT=ctxT, wo=A["L0_xattn_Wo"], bo=A["L0_xattn_bo"])
            yield
            with nc.sbuf_tensor("mixed", [T, NB, D], F32) as y:
                ffn("l0f", 2, MOE_TILE, False, False, A["L0_ffn_Wg"], A["L0_ffn_bg"], A["L0_ffn_W1"], A["L0_ffn_W3"], A["L0_ffn_W2"],
                    A["L0_ffn_b1"], A["L0_ffn_b3"], A["L0_ffn_b2"], "silu_of_product", y, first=True)
                linear(nc, "l0w", K, y, A["L0_ffn_Wf"], A["L0_ffn_bf"], x)
            yield
            with nc.sbuf_tensor("inner", [T, NB, D], F32) as y:
                with nc.sbuf_tensor("offbias", [T, 16, T], F32) as bias:
                    scratch = nc.dram_tensor("bias_rows", [16, T, RELS], F32, kind="Internal").ap()
                    offset_bias(nc, bias, K, A["L1_attn_pos_bias"], A["L1_attn_offsets"], scratch)
                    attention(nc, "l1a", x, K, heads=16, dh=16, dv=16, wq=A["L1_q"], wk=A["L1_k"], wv=A["L1_v"], scale=0.25,
                              wo=A["L1_attn_w_out"], addend=bias, gate=(A["L1_attn_w_gate"], A["L1_attn_b_gate"]),
                              norm="ln_rms", norm_scale=A["L1_attn_norm1_scale"], y=y)
                with nc.sbuf_tensor("l1af_xT", [128, KD, NB * T], F32) as xnT_all:
                    normed_transposed(nc, "l1af", y, K, xnT_all, A["L1_attn_norm2_scale"])
                    experts(nc, "l1af", K, xnT_all, None, y, A["L1_up"], A["L1_gate"], A["L1_down"], None, None, "swiglu", n_exp=1)
                add_all(nc, "l1add", x, y)
            yield
            attention(nc, "l1x", x, K, heads=1, dh=256, dv=256, wq=A["L1_xattn_Wq"], wk=A["L1_xattn_Wk"], wv=A["L1_xattn_Wv"],
                      scale=D ** -0.5, ctxT=ctxT, bq=A["L1_xattn_bq"], bk=A["L1_xattn_bk"], bv=A["L1_xattn_bv"])
            yield
            ffn("l1f", 1, CAPACITY, True, True, A["L1_ffn_gate_w"], A["L1_ffn_gate_b"], A["L1_ffn_w1"], None, A["L1_ffn_w2"],
                A["L1_ffn_b1"], None, A["L1_ffn_b2"], "relu", x)
            yield
            scratch = nc.dram_tensor("rel_rows", [NB * 16, T, RELS], F32, kind="Internal").ap()
            relative_positions(nc, x, K, A["L2_q"], A["L2_bq"], A["L2_attn_Wr"], A["L2_attn_br"], scratch)
            attention(nc, "l2a", x, K, heads=16, dh=16, dv=16, wq=A["L2_q"], wk=A["L2_k"], wv=A["L2_v"], scale=0.25,
                      bq=A["L2_bq"], bk=A["L2_bk"], bv=A["L2_bv"], pos_dram=lambda b: skewed(scratch, b, 16))
            yield
            attention(nc, "l2x", x, K, heads=16, dh=16, dv=16, wq=A["L2_xattn_Wq"], wk=A["L2_xattn_Wk"], wv=A["L2_xattn_Wv"],
                      scale=0.25, ctxT=ctxT, bq=A["L2_xattn_bq"], bk=A["L2_xattn_bk"], bv=A["L2_xattn_bv"],
                      wo=A["L2_xattn_Wo"], bo=A["L2_xattn_bo"], maskrow=K["mask_if1"])
            yield
            ffn("l2f", 1, 128, False, True, A["L2_ffn_Wr"], A["L2_ffn_br"], A["L2_ffn_W1"], None, A["L2_ffn_W2"],
                A["L2_ffn_b1"], None, A["L2_ffn_b2"], "relu", x)
            yield
            attention(nc, "l3a", x, K, heads=1, dh=256, dv=256, wq=A["L3_attn_Wq"], wk=A["L3_attn_Wk"], wv=A["L3_attn_Wv"],
                      scale=D ** -0.5)
            yield
            attention(nc, "l3x", x, K, heads=16, dh=16, dv=16, wq=A["L3_q"], wk=A["L3_k"], wv=A["L3_v"], scale=0.25, ctxT=ctxT,
                      bq=A["L3_bq"], bk=A["L3_bk"], bv=A["L3_bv"], wo=A["L3_xattn_out_w"], bo=A["L3_xattn_out_b"],
                      maskrow=K["mask_bk0"])
            yield
            ffn("l3f", 2, MOE_TILE, False, True, A["L3_ffn_router_w"], None, A["L3_up"], A["L3_gate"], A["L3_ffn_w2"],
                None, None, None, "swiglu", x)
            yield

        for n, _ in enumerate(stages()):
            if n + 1 == last_stage:
                break

        with Phase(nc, "end") as p:
            stored = p.sem("stored")
            with nc.Block() as block:

                @block.sync
                def _(sp):
                    sp.dma_start(out.rearrange("b t d -> t b d"), x[:]).then_inc(stored, 16)
                    sp.wait_ge(stored, 16)



def layout(I):
    import numpy as np

    def c(a):
        return np.ascontiguousarray(a)

    def pad_heads(w):
        out = np.zeros((w.shape[0], 16, 32), w.dtype)
        out[:, :, :16] = w.reshape(w.shape[0], 16, 16)
        return out.reshape(w.shape[0], 512)

    def pad_bias(b):
        out = np.zeros((16, 32), b.dtype)
        out[:, :16] = b.reshape(16, 16)
        return c(out.reshape(4, 128).T)

    def tile_bias(b):
        return c(b.reshape(b.shape[0], -1, 128).transpose(0, 2, 1))

    A = {k: I[k] for k in ("x", "fside_BxS2_0", "mask_BxS2_if1", "L0_xattn_bo", "L0_ffn_W1", "L0_ffn_W3", "L0_ffn_W2", "L0_ffn_b2",
                           "L0_ffn_Wg", "L0_ffn_bg", "L0_ffn_Wf", "L0_ffn_bf", "L1_attn_norm1_scale", "L1_attn_norm2_scale",
                           "L1_attn_w_out", "L1_attn_w_gate", "L1_attn_b_gate", "L1_attn_offsets", "L1_xattn_Wq", "L1_xattn_Wk",
                           "L1_xattn_Wv", "L1_xattn_bv", "L1_ffn_gate_b", "L1_ffn_w1", "L1_ffn_w2", "L1_ffn_b2", "L2_attn_br",
                           "L2_xattn_Wv", "L2_xattn_bv", "L2_xattn_Wo", "L2_xattn_bo", "L2_ffn_Wr", "L2_ffn_br", "L2_ffn_W1",
                           "L2_ffn_W2", "L2_ffn_b2", "L3_xattn_out_b")}
    A["mask_BxS2_bk0"] = I["mask_BxS2_bk0"]
    A["ctxT"] = c(I["ctx_1024"].transpose(0, 2, 1))
    for k in ("L0_attn_w_qkv", "L0_attn_w_out", "L0_xattn_Wq", "L0_xattn_Wk", "L0_xattn_Wv", "L0_xattn_Wo", "L1_attn_pos_bias",
              "L1_ffn_gate_w", "L2_attn_Wr", "L3_attn_Wq", "L3_attn_Wk", "L3_attn_Wv", "L3_xattn_out_w", "L3_ffn_router_w"):
        A[k] = c(I[k].T)
    for k in ("L0_ffn_b1", "L0_ffn_b3", "L1_ffn_b1", "L2_ffn_b1"):
        A[k] = tile_bias(I[k])
    w = I["L1_attn_w_qkv"]
    A["L1_q"], A["L1_k"], A["L1_v"] = pad_heads(w[:, :256]), pad_heads(w[:, 256:512]), c(w[:, 512:])
    A["L1_gate"], A["L1_up"], A["L1_down"] = I["L1_attn_w_ffn_gate"][None], I["L1_attn_w_ffn_up"][None], I["L1_attn_w_ffn_down"][None]
    for k in ("bq", "bk"):
        A["L1_xattn_" + k] = c(I["L1_xattn_" + k].reshape(2, 128).T)
        A["L2_xattn_" + k] = pad_bias(I["L2_xattn_" + k])
    A["L2_xattn_Wq"], A["L2_xattn_Wk"] = pad_heads(I["L2_xattn_Wq"]), pad_heads(I["L2_xattn_Wk"])
    w = I["L2_attn_Wqkv"].reshape(16, 3, 16, 256).transpose(1, 3, 0, 2).reshape(3, 256, 256)
    b = I["L2_attn_bqkv"].reshape(16, 3, 16).transpose(1, 0, 2).reshape(3, 256)
    A["L2_q"], A["L2_k"], A["L2_v"] = pad_heads(w[0]), pad_heads(w[1]), c(w[2])
    A["L2_bq"], A["L2_bk"], A["L2_bv"] = pad_bias(b[0]), pad_bias(b[1]), c(b[2])
    wkv, bkv = I["L3_xattn_Wkv_w"], I["L3_xattn_Wkv_b"]
    A["L3_q"], A["L3_k"], A["L3_v"] = pad_heads(I["L3_xattn_Wq_w"].T), pad_heads(wkv[:256].T), c(wkv[256:].T)
    A["L3_bq"], A["L3_bk"], A["L3_bv"] = pad_bias(I["L3_xattn_Wq_b"]), pad_bias(bkv[:256]), c(bkv[256:])
    w = I["L3_ffn_w1"].transpose(0, 2, 1)
    A["L3_gate"], A["L3_up"] = c(w[:, :, :512]), c(w[:, :, 512:])
    A["L3_ffn_w2"] = c(I["L3_ffn_w2"].transpose(0, 2, 1))
    return {k: c(a) for k, a in A.items()}


def kernel(**inputs):
    import numpy as _np
    import concourse.bacc as _bacc
    from concourse import mybir as _mybir
    from concourse.bass_utils import run_bass_kernel_spmd as _run

    arrays = {f"in_{k}": a for k, a in layout({k: _np.asarray(v) for k, v in inputs.items()}).items()}
    nc = _bacc.Bacc("TRN2", target_bir_lowering=False, num_devices=1)
    A = {k[3:]: nc.dram_tensor(k, a.shape, _mybir.dt.from_np(a.dtype), kind="ExternalInput").ap() for k, a in arrays.items()}
    out = nc.dram_tensor("out_dram", (NB, T, D), F32, kind="ExternalOutput").ap()
    decoder(nc, A, out)
    r = _run(nc, [arrays], core_ids=[0])
    return r.results[0]["out_dram"]
```

```python
from contextlib import ExitStack

import concourse.bass as bass
from concourse import mybir

F32 = mybir.dt.float32
F32R = mybir.dt.float32r
I32 = mybir.dt.int32
U8 = mybir.dt.uint8
U32 = mybir.dt.uint32
ACT = mybir.ActivationFunctionType
ALU = mybir.AluOpType
AX_X = mybir.AxisListType.X

NB = 16
T = 112
D = 256
KD = D // 128
SK = 375
KC = 125
NKC = SK // KC
NE = 8
NPAIR = NB // 2
RELS = 2 * T - 1
REL_WINDOW = 128
MASKED = -1.0e30
LN_EPS = 1e-5
RMS_EPS = 1e-6
CAPACITY = -(-(5 * NB * T) // (4 * NE))


GROUPS = [(0, 8), (8, 8)]
MASKED_GROUPS = [(0, 6), (6, 5), (11, 5)]
MASK_ROW = 96
MOE_TILE = 256


def wait(eng, sem, value):
    if isinstance(value, int) and value <= 0:
        return
    eng.wait_ge(sem, value)


def reuse(b, n, per, ring, uses=None):
    uses = per if uses is None else uses
    if n >= ring:
        return b * per + n - ring + 1
    last = n + (uses - 1 - n) // ring * ring
    return (b - 1) * per + last + 1


def over_batches(eng, body):
    for u in range(2):
        body(u, u, 0)
    with eng.Fori(1, NPAIR) as i:
        for u in range(2):
            body(i * 2 + u, u, i)


def over_batches_ahead(eng, body):
    for u in range(2):
        body(u, u, 0)
    with eng.Fori(1, NPAIR - 1) as i:
        for u in range(2):
            body(i * 2 + u, u, i)
    for u in range(2):
        body(NB - 2 + u, u, NPAIR - 1)


def is_static(b, value):
    return isinstance(b, int) and b == value


class Kept:

    def __init__(self, ctx, nc, name):
        self.sem, self.base = ctx.enter_context(nc.semaphore(name)), 0


class Phase:

    def __init__(self, nc, name):
        self.nc, self.name, self.ctx, self.sems = nc, name, ExitStack(), []

    def __enter__(self):
        return self

    def sb(self, name, shape, dt=F32):
        return self.ctx.enter_context(self.nc.sbuf_tensor(f"{self.name}_{name}", shape, dt))

    def ps(self, name, shape):
        return self.ctx.enter_context(self.nc.psum_tensor(f"{self.name}_{name}", shape, F32))

    def sem(self, name):
        s = self.ctx.enter_context(self.nc.semaphore(f"{self.name}_{name}"))
        self.sems.append(s)
        return s

    def __exit__(self, *exc):
        if exc[0] is None:
            for s in self.sems:
                self.nc.gpsimd.sem_clear(s)
            self.nc.all_engine_barrier()
        self.ctx.close()


def batch(t, b):
    return t[0:T, bass.ds(b, 1), :].rearrange("p b d -> p (b d)")


def column(t, b):
    return t[0:T, bass.ds(b, 1)]


def row_bcast(ap, n):
    return ap.rearrange("(a n) -> a n", a=1).broadcast_to([n, ap.shape[0]])



class Norm:
    def __init__(self, p, x, kind):
        self.x, self.kind = x, kind
        self.st = p.sb("bn", [T, NB, 6])
        self.w = p.sb("bnw", [T, 6, NB])
        self.mean = p.sb("mean", [T, NB])
        self.var = p.sb("var", [T, NB])
        self.rstd = p.sb("rstd", [T, NB])
        self.rms = p.sb("rms", [T, NB])
        self.std = p.sb("std", [T, 2, NB])
        self.rows_done = p.sem("bn_rows")
        self.steps = p.sem("bn_steps")
        self.to_sqrt = p.sem("to_sqrt")
        self.sqrt_done = p.sem("sqrt_done")

    def vector(self, v):
        with v.Fori(0, 2) as half:
            for c in range(NB // 2):
                b = half * (NB // 2) + c
                v.bn_stats(self.st[:, bass.ds(b, 1), :].rearrange("p b s -> p (b s)"), batch(self.x, b)).then_inc(self.rows_done, 1)
        v.wait_ge(self.rows_done, NB)
        me, qe, mo, qo = (self.st[:, :, k] for k in (1, 2, 4, 5))
        s, d, q, d2, ve, ms = (self.w[:, k, :] for k in range(6))
        n = 0

        def chain(ins):
            nonlocal n
            n += 1
            ins.then_inc(self.steps, 1)
            v.wait_ge(self.steps, n)

        v.tensor_tensor(s, me, mo, ALU.add).then_inc(self.steps, 1)
        v.tensor_tensor(d, me, mo, ALU.subtract).then_inc(self.steps, 1)
        n += 2
        chain(v.tensor_tensor(q, qe, qo, ALU.add))
        chain(v.scalar_tensor_tensor(d2, d, 0.25, d, ALU.mult, ALU.mult))
        v.tensor_scalar(self.mean[:], s, 0.5, None, ALU.mult).then_inc(self.steps, 1)
        n += 1
        chain(v.scalar_tensor_tensor(self.var[:], q, 1.0 / D, d2, ALU.mult, ALU.add))
        if self.kind != "rms":
            v.tensor_scalar(ve, self.var[:], LN_EPS, None, ALU.add).then_inc(self.to_sqrt, 1)
            v.wait_ge(self.sqrt_done, 1)
            chain(v.reciprocal(self.rstd[:], self.std[:, 0, :]))
        if self.kind == "ln_rms":
            chain(v.tensor_tensor(ms, self.var[:], self.rstd[:], ALU.mult))
            chain(v.tensor_tensor(ms, ms, self.rstd[:], ALU.mult))
        if self.kind == "rms":
            chain(v.tensor_tensor(ms, self.mean[:], self.mean[:], ALU.mult))
            chain(v.tensor_tensor(ms, ms, self.var[:], ALU.add))
        if self.kind != "ln":
            k = 2 if self.kind == "ln_rms" else 1
            v.tensor_scalar(ve, ms, RMS_EPS, None, ALU.add).then_inc(self.to_sqrt, 1)
            v.wait_ge(self.sqrt_done, k)
            chain(v.reciprocal(self.rms[:], self.std[:, 1, :]))

    def scalar(self, a):
        which = {"ln": (0,), "ln_rms": (0, 1), "rms": (1,)}[self.kind]
        for n, k in enumerate(which):
            a.wait_ge(self.to_sqrt, n + 1)
            a.activation(self.std[:, k, :], self.w[:, 4, :], ACT.Sqrt).then_inc(self.sqrt_done, 1)

    def rows(self, v, b, out, done, h=None, h_done=None, scale_row=None):
        if self.kind == "ln":
            v.tensor_scalar(out, batch(self.x, b), column(self.mean, b), column(self.rstd, b),
                            ALU.subtract, ALU.mult).then_inc(done, 1)
            return
        if self.kind == "ln_rms":
            v.tensor_scalar(batch(h, b), batch(self.x, b), column(self.mean, b), column(self.rstd, b),
                            ALU.subtract, ALU.mult).then_inc(h_done, 1)
            v.wait_ge(h_done, b + 1)
        v.scalar_tensor_tensor(out, batch(h, b), column(self.rms, b), scale_row,
                               ALU.mult, ALU.mult).then_inc(done, 1)



def attention(nc, name, x, K, *, heads, dh, dv, wq, wk, wv, scale, ctxT=None, bq=None, bk=None, bv=None,
              wo=None, bo=None, maskrow=None, addend=None, pos_dram=None, gate=None, norm="ln",
              norm_scale=None, y=None):
    cross = ctxT is not None
    S = SK if cross else T
    kc, nkc = (KC, NKC) if cross else (T, 1)
    DV = heads * dv
    spread = dh < 64
    if spread:
        groups = MASKED_GROUPS if maskrow is not None else GROUPS
        sel = K["sel_masked"] if maskrow is not None else K["sel"]
    else:
        groups = [(g * (128 // dh), 128 // dh) for g in range(heads * dh // 128)] if dh <= 128 else [(0, 1)] * (dh // 128)
    col0 = [h * dh for h, _ in groups] if dh <= 128 else [g * 128 for g in range(len(groups))]
    rows = [n * dh if dh <= 128 else 128 for _, n in groups]
    G = len(groups)
    group_of = {h: g for g, (h0, n) in enumerate(groups) for h in range(h0, h0 + n)}
    KR = MASK_ROW + 1 if maskrow is not None else 128
    NQT = heads if spread else G
    HU = 1 if cross or heads == 1 else 2
    units = [list(range(h, h + HU)) for h in range(0, heads, HU)]
    NU = len(units)
    has_add = addend is not None or pos_dram is not None
    QPB = min(G, 4)
    NQ = G // QPB
    VW = min(DV, 512)
    NV = DV // VW
    q_jobs = [("q", n) for n in range(NQ)]
    jobs = [("x", 0)] + ([("k", g) for g in range(G)] + q_jobs if cross else q_jobs + [("k", 0)])
    jobs += [("v", c * NV + n) for c in range(nkc) for n in range(NV)]
    jobs += [("g", 0)] if gate else []
    NPP = len(jobs)
    NBLK = DV // 128
    NTT = -(-NBLK // 4) if wo is not None else 0
    NTY = NTT + 1 if wo is not None else 0
    dest = x if y is None else y
    LT, LV = (2, 3) if NU > 1 else (1, 1)
    X0 = 4 if NU > 4 else NU - 1
    steps = max(1, NU - 1)
    jobs_at = [list(range(n * NPP // steps, (n + 1) * NPP // steps)) for n in range(steps)] + [[]] * (NU - steps)
    NPB = 1 if DV > 512 else 2
    EARLY = (2 if cross else 1) if NU == 1 else 0

    def back(b, u, n, lag):
        over = -(-(lag - n) // NU) if lag > n else 0
        if isinstance(b, int) and b < over:
            return None
        return b - over, (u - over) % 2, n - lag + over * NU

    def slot_of(u, n, ring):
        return n % ring if NU > 1 else u

    def before(b, n, ring):
        return reuse(b, n, NU, ring) if NU > 1 else b - 1

    ident, ones = K["ident"], K["ones"]

    with Phase(nc, name) as p:
        wq_sb = p.sb("wq", [128, KD, heads * dh])
        q_sb = p.sb("q", [128, 2, G, T]) if spread else None
        wo_sb = p.sb("wo", [128, NBLK, D]) if wo is not None else None
        bq_sb = p.sb("bq", [128, G]) if bq is not None else None
        bk_sb = p.sb("bk", [128, G]) if bk is not None else None
        bv_sb = p.sb("bv", [T, DV]) if bv is not None else None
        bo_sb = p.sb("bo", [1, D]) if bo is not None else None
        gw_sb = p.sb("gw", [128, KD, D]) if gate else None
        gb_sb = p.sb("gb", [1, D]) if gate else None
        gate_sb = p.sb("gate", [T, 2, D]) if gate else None
        gate_w = p.sb("gate_w", [T, 2, D]) if gate else None
        ns_sb = p.sb("ns", [T, D]) if norm_scale is not None else None
        pos_sb = p.sb("pos", [T, 2, heads, T]) if pos_dram is not None else None
        xn = p.sb("xn", [T, 2, D])
        xnT = p.sb("xnT", [128, 2, KD, T])
        qT = p.sb("qT", [128, 2, NQT, T])
        kT = p.sb("kT", [128, 2, G, S])
        vs = p.sb("v", [kc, 2, nkc, DV])
        if cross:
            wk_hi, wk_lo = (p.sb(s, [128, KD, heads * dh], F32R) for s in ("wk_hi", "wk_lo"))
            wv_hi, wv_lo = (p.sb(s, [128, KD, DV], F32R) for s in ("wv_hi", "wv_lo"))
            if heads * dh > 512:
                flat = kT[:].rearrange("p u g s -> p (u g s)")
                wk_sb, wv_sb = (flat[:, n * KD * DV:(n + 1) * KD * DV].rearrange("p (k n) -> p k n", k=KD) for n in range(2))
            else:
                wk_sb, wv_sb = p.sb("wk", [128, KD, heads * dh])[:], p.sb("wv", [128, KD, DV])[:]
            SX = SK + SK % 2
            ctx_sb = p.sb("ctx", [128, KD, SX])
            ctx_hi, ctx_lo = (p.sb(s, [128, 2, KD, SX], F32R) for s in ("ctx_hi", "ctx_lo"))
        else:
            SX = S
            wk_sb, wv_sb = p.sb("wk", [128, KD, heads * dh])[:], p.sb("wv", [128, KD, DV])[:]
        logit = p.sb("logit", [T, 2, HU, S]) if has_add else None
        probs = p.sb("probs", [T, 4, HU, S])
        pT = p.sb("pT", [kc, 2, HU * nkc, T])
        nmax = p.sb("nmax", [T, 2, NU, HU])
        den = p.sb("den", [T, 2, NU, HU])
        rden = p.sb("rden", [T, 2, NU, HU])
        OS = 2 if wo is None else 1
        o_sb = p.sb("o", [T, OS, DV])
        oT = p.sb("oT", [128, NBLK, T]) if wo is not None else None

        pp = p.ps("pp", [128, NPB, 512])
        sc = p.ps("sc", [128, 2, 512])
        tr = p.ps("tr", [128, 2, 512])
        PO2 = DV <= 512 and wo is None
        po = p.ps("po", [128, 2, 512] if DV > 512 or PO2 else [128, 1, 512])
        ty = None if wo is None else p.ps("ty", [128, 512])

        st = Norm(p, x, norm)
        loaded = p.sem("loaded")
        n_loads = 0
        scaled = p.sem("scaled")
        q_spread = p.sem("q_spread")
        filled = p.sem("filled")
        mask_in = [p.sem(f"mask_in{u}") for u in range(2)]
        ctx_in = [p.sem(f"ctx_in{u}") for u in range(2)]
        pos_in = [p.sem(f"pos_in{u}") for u in range(2)]
        w_split = p.sem("w_split")
        c_hi = p.sem("c_hi")
        c_split = p.sem("c_split")
        xn_ready = p.sem("xn_ready")
        h_done = p.sem("h_done")
        pp_ready = p.sem("pp_ready")
        pp_empty = p.sem("pp_empty")
        s_ready = p.sem("s_ready")
        l_ready = p.sem("l_ready")
        m_ready = p.sem("m_ready")
        e_ready = p.sem("e_ready")
        t_ready = p.sem("t_ready")
        t_empty = p.sem("t_empty")
        ty_ready = p.sem("ty_ready")
        ty_empty = p.sem("ty_empty")
        pv_done = p.sem("pv_done")
        rden_ready = p.sem("rden_ready")
        o_norm = p.sem("o_norm")
        o_bias = p.sem("o_bias")
        o_ready = p.sem("o_ready")
        g_steps = p.sem("g_steps")
        x_done = p.sem("x_done")

        loads = [(wq_sb[:], wq.rearrange("(k p) n -> p k n", p=128)),
                 (wk_sb, wk.rearrange("(k p) n -> p k n", p=128)),
                 (wv_sb, wv.rearrange("(k p) n -> p k n", p=128))]
        for dst, src in ((bq_sb, bq), (bk_sb, bk)):
            if src is not None:
                for g in range(G):
                    loads.append((dst[0:rows[g], g:g + 1], src[col0[g]:col0[g] + rows[g]].rearrange("(n a) -> n a", a=1)))
        if bv is not None:
            loads.append((bv_sb[:], row_bcast(bv, T)))
        if wo is not None:
            loads.append((wo_sb[:], wo.rearrange("(k p) n -> p k n", p=128)))
        if bo is not None:
            loads.append((bo_sb[:], bo.rearrange("(a n) -> a n", a=1)))
        if gate:
            loads.append((gw_sb[:], gate[0].rearrange("(k p) n -> p k n", p=128)))
            loads.append((gb_sb[:], gate[1].rearrange("(a n) -> a n", a=1)))
        if norm_scale is not None:
            loads.append((ns_sb[:], row_bcast(norm_scale, T)))
        n_loads = len(loads)
        spread_at = min(NU - 1, 1 + next(n for n in range(NU) if jobs.index(("q", 0)) in jobs_at[n]))

        def o_cols(u, h):
            if DV > 512:
                return po[0:T, h * dv // 512, h * dv % 512:h * dv % 512 + dv]
            return po[0:T, u if PO2 else 0, h * dv:(h + 1) * dv]

        def o_all(u):
            return po[0:T, :, :].rearrange("p a n -> p (a n)") if DV > 512 else po[0:T, u if PO2 else 0, 0:DV]

        with nc.Block() as block:

            @block.sync
            def _(sp):
                for dst, src in loads:
                    sp.dma_start(dst, src).then_inc(loaded, 16)
                if not cross and pos_dram is None:
                    return

                def body(b, u, i):
                    if cross:
                        wait(sp, c_split, b)
                        if is_static(b, 0):
                            sp.wait_ge(c_hi, 1)
                        sp.dma_start(ctx_sb[:, :, 0:SK], ctxT[bass.ds(b, 1)].rearrange("b (k p) s -> p (b k) s", p=128)).then_inc(ctx_in[u], 16)
                        if maskrow is not None:
                            if is_static(b, 0):
                                sp.wait_ge(filled, 1)
                            wait(sp, s_ready, (b - 1) * NU)
                            sp.dma_start(kT[MASK_ROW:MASK_ROW + 1, u, :, :], maskrow.rearrange("a (b s) -> a b s", s=SK)[0:1, bass.ds(b, 1), :].broadcast_to([1, G, SK])).then_inc(mask_in[u], 16)
                    if pos_dram is not None:
                        wait(sp, l_ready, (b - 1) * NU)
                        sp.dma_start(pos_sb[:, u, :, :], pos_dram(b)).then_inc(pos_in[u], 16)

                over_batches(sp, body)

            @block.gpsimd
            def _(g):
                if cross:
                    g.memset(ctx_sb[:].rearrange("p k s -> p (k s)"), 0.0).then_inc(c_hi, 1)
                    g.wait_ge(c_hi, 1)
                if spread:
                    if maskrow is not None:
                        g.memset(kT[:].rearrange("p u g s -> p (u g s)"), 0.0).then_inc(filled, 1)
                    g.memset(qT[:].rearrange("p u h t -> p (u h t)"), 0.0).then_inc(filled, 1)
                    if maskrow is not None:
                        g.wait_ge(filled, 2)
                        g.memset(qT[MASK_ROW:MASK_ROW + 1].rearrange("p u h t -> p (u h t)"), 1.0).then_inc(filled, 1)
                if cross:
                    if spread:
                        g.wait_ge(filled, 3 if maskrow is not None else 1)
                    g.wait_ge(loaded, 16 * n_loads)
                    g.tensor_copy(wv_hi[:], wv_sb).then_inc(w_split, 1)

                    def body(b, u, i):
                        wait(g, pp_ready, (b - 1) * NPP)
                        g.wait_ge(ctx_in[u], i * 16 + 16)
                        g.tensor_tensor(ctx_hi[:, u], ctx_sb[:], ones[:, 0:1].unsqueeze(2).broadcast_to([128, KD, SX]), ALU.mult).then_inc(c_hi, 1)
                        g.wait_ge(c_hi, b + 2)
                        g.tensor_tensor(ctx_lo[:, u], ctx_sb[:], ctx_hi[:, u].bitcast(F32), ALU.subtract).then_inc(c_split, 1)

                    over_batches(g, body)

            @block.tensor
            def _(pe):
                pe.wait_ge(loaded, 16 * n_loads)
                if cross:
                    pe.wait_ge(w_split, 4)

                def project(b, u, i, which):
                    for j in which:
                        kind, n = jobs[j]
                        bank = pp[:, j % NPB, :]
                        wait(pe, pp_empty, reuse(b, j, NPP, NPB))
                        parts = ((ctx_hi, wk_hi, wv_hi), (ctx_hi, wk_lo, wv_lo), (ctx_lo, wk_hi, wv_hi)) if cross else ((xnT, wk_sb, wv_sb),)
                        if kind == "x":
                            pe.wait_ge(xn_ready, b + 1)
                            for k in range(KD):
                                last = pe.transpose(bank[:, k * T:(k + 1) * T], xn[:, u, k * 128:(k + 1) * 128], ident[0:T, 0:T])
                        if kind == "q":
                            if n == 0:
                                pe.wait_ge(pp_empty, b * NPP + 1)
                            for q in range(QPB):
                                for k in range(KD):
                                    g = n * QPB + q
                                    last = pe.matmul(bank[0:rows[g], q * T:(q + 1) * T], wq_sb[:, k, col0[g]:col0[g] + rows[g]],
                                                     xnT[:, u, k, :], start=k == 0, stop=k == KD - 1)
                        if kind == "k":
                            if cross and n == 0:
                                pe.wait_ge(c_split, b + 1)
                            for q in range(1 if cross else G):
                                g = n + q
                                for m, (src, w, _) in enumerate(parts):
                                    for k in range(KD):
                                        last = pe.matmul(bank[0:rows[g], q * S:q * S + SX], w[:, k, col0[g]:col0[g] + rows[g]],
                                                         src[:, u, k, 0:SX], start=m == k == 0, stop=(m, k) == (len(parts) - 1, KD - 1))
                        if kind == "v":
                            c, m = n // NV, n % NV
                            for r, (src, _, w) in enumerate(parts):
                                for k in range(KD):
                                    last = pe.matmul(bank[0:kc, 0:VW], src[:, u, k, c * kc:(c + 1) * kc],
                                                     w[:, k, m * VW:(m + 1) * VW], start=r == k == 0, stop=(r, k) == (len(parts) - 1, KD - 1))
                        if kind == "g":
                            for k in range(KD):
                                pe.matmul(bank[0:T, 0:D], xnT[:, u, k, :], gw_sb[:, k, :], start=k == 0, stop=False)
                            last = pe.matmul(bank[0:T, 0:D], ones[0:1, 0:T], gb_sb[0:1, :], start=False, stop=True)
                        last.then_inc(pp_ready, 1)

                def scores(b, u, i, n):
                    if n == 0:
                        pe.wait_ge(pp_empty, (b + 1) * NPP)
                        if spread:
                            pe.wait_ge(q_spread, (b + 1) * G)
                        if maskrow is not None:
                            pe.wait_ge(mask_in[u], i * 16 + 16)
                    wait(pe, l_ready if has_add else e_ready, before(b, n, 2))
                    for c, h in enumerate(units[n]):
                        out = sc[0:T, slot_of(u, n, 2), c * S:(c + 1) * S]
                        if dh > 128:
                            for g in range(G):
                                last = pe.matmul(out, qT[:, u, g, :], kT[:, u, g, :], start=g == 0, stop=g == G - 1)
                        elif spread:
                            last = pe.matmul(out, qT[0:KR, u, h, :], kT[0:KR, u, group_of[h], :], start=True, stop=True)
                        else:
                            g = group_of[h]
                            r = slice((h - groups[g][0]) * dh, (h - groups[g][0] + 1) * dh)
                            last = pe.matmul(out, qT[r, u, g, :], kT[r, u, g, :], start=True, stop=True)
                    last.then_inc(s_ready, 1)

                def turn(b, u, n):
                    pe.wait_ge(e_ready, b * NU + n + 1)
                    wait(pe, t_empty, before(b, n, 2))
                    for c in range(HU):
                        for m in range(nkc):
                            s = c * nkc + m
                            last = pe.transpose(tr[0:kc, slot_of(u, n, 2), s * T:(s + 1) * T],
                                                probs[:, slot_of(u, n, 4), c, m * kc:(m + 1) * kc], ident[0:T, 0:T])
                    last.then_inc(t_ready, 1)

                def values(b, u, n):
                    pe.wait_ge(t_empty, b * NU + n + 1)
                    if n == 0:
                        wait(pe, o_norm, b - 1 if PO2 else b)
                    for c, h in enumerate(units[n]):
                        for m in range(nkc):
                            last = pe.matmul(o_cols(u, h), pT[:, slot_of(u, n, 2), c * nkc + m, :],
                                             vs[:, u, m, h * dv:(h + 1) * dv], start=m == 0, stop=m == nkc - 1)
                    last.then_inc(pv_done, 1)

                def turn_output(b, u, n):
                    if n == 0:
                        pe.wait_ge(o_ready, b + 1)
                    wait(pe, ty_empty, b * NTY + n)
                    for q in range(min(4, NBLK - 4 * n)):
                        k = 4 * n + q
                        last = pe.transpose(ty[:, q * T:(q + 1) * T], o_sb[:, u % OS, k * 128:(k + 1) * 128], ident[0:T, 0:T])
                    last.then_inc(ty_ready, 1)

                def project_output(b):
                    pe.wait_ge(ty_empty, b * NTY + NTT)
                    for k in range(NBLK):
                        last = pe.matmul(ty[0:T, 0:D], oT[:, k, :], wo_sb[:, k, :], start=k == 0,
                                         stop=k == NBLK - 1 and bo is None)
                    if bo is not None:
                        last = pe.matmul(ty[0:T, 0:D], ones[0:1, 0:T], bo_sb[0:1, :], start=False, stop=True)
                    last.then_inc(ty_ready, 1)

                def body(b, u, i):
                    for n in range(NU):
                        scores(b, u, i, n)
                        out = wo is not None and not is_static(b, 0)
                        if out and 0 <= n - X0 < NTT:
                            turn_output(b - 1, 1 - u, n - X0)
                        if (at := back(b, u, n, LT)) is not None:
                            turn(*at)
                        if not is_static(b, NB - 1):
                            project(b + 1, 1 - u, i + u, jobs_at[n][:EARLY])
                        if (at := back(b, u, n, LV)) is not None:
                            values(*at)
                        if out and n == X0 + NTT - 1:
                            project_output(b - 1)
                        if not is_static(b, NB - 1):
                            project(b + 1, 1 - u, i + u, jobs_at[n][EARLY:])

                project(0, 0, 0, range(NPP))
                over_batches_ahead(pe, body)
                for n in range(LV):
                    if n < LT:
                        turn(*back(NB, 0, n, LT))
                    values(*back(NB, 0, n, LV))
                for n in range(NTT):
                    turn_output(NB - 1, 1, n)
                if wo is not None:
                    project_output(NB - 1)

            @block.scalar
            def _(a):
                st.scalar(a)
                a.wait_ge(loaded, 16 * n_loads)
                if bq is not None:
                    a.wait_ge(scaled, 1)
                if maskrow is not None:
                    a.wait_ge(filled, 1)

                def copy_out(b, u, which):
                    for j in which:
                        kind, n = jobs[j]
                        bank = pp[:, j % NPB, :]
                        a.wait_ge(pp_ready, b * NPP + j + 1)
                        if kind == "x":
                            last = a.activation(xnT[:, u, :, :].rearrange("p k t -> p (k t)"), bank[:, 0:KD * T], ACT.Copy)
                        if kind == "q":
                            dst = q_sb if spread else qT
                            if spread:
                                wait(a, q_spread, (b - 1) * G)
                            if bq is None:
                                last = a.activation(dst[:, u, n * QPB:(n + 1) * QPB, :].rearrange("p g t -> p (g t)"), bank[:, 0:QPB * T], ACT.Copy, scale=scale)
                            else:
                                for q in range(QPB):
                                    g = n * QPB + q
                                    r = slice(0, rows[g])
                                    last = a.activation(dst[r, u, g, :], bank[r, q * T:(q + 1) * T], ACT.Identity, bias=bq_sb[r, g:g + 1], scale=scale)
                        if kind == "k":
                            if bk is None:
                                last = a.activation(kT[:, u, n:n + (1 if cross else G), :].rearrange("p g s -> p (g s)"),
                                                    bank[:, 0:(1 if cross else G) * S], ACT.Copy)
                            else:
                                for q in range(1 if cross else G):
                                    g = n + q
                                    last = a.activation(kT[0:rows[g], u, g, :], bank[0:rows[g], q * S:(q + 1) * S], ACT.Identity, bias=bk_sb[0:rows[g], g:g + 1])
                        if kind == "v":
                            c, m = n // NV, n % NV
                            last = a.activation(vs[:, u, c, m * VW:(m + 1) * VW], bank[0:kc, 0:VW], ACT.Copy)
                        if kind == "g":
                            wait(a, o_ready, b - 1)
                            last = a.activation(gate_w[:, u, :], bank[0:T, 0:D], ACT.Exp, scale=-1.0)
                        last.then_inc(pp_empty, 1)

                def exponentials(b, u, n):
                    a.wait_ge(m_ready, b * NU + n + 1)
                    wait(a, t_ready, before(b, n, 4))
                    for c in range(HU):
                        src = logit[:, slot_of(u, n, 2), c, :] if has_add else sc[0:T, slot_of(u, n, 2), c * S:(c + 1) * S]
                        last = a.activation(probs[:, slot_of(u, n, 4), c, :], src, ACT.Exp, bias=nmax[:, u, n, c:c + 1],
                                            accum_out=den[:, u, n, c:c + 1])
                    last.then_inc(e_ready, 1)

                def body(b, u, i):
                    for n in range(NU):
                        exponentials(b, u, n)
                        if not is_static(b, NB - 1):
                            copy_out(b + 1, 1 - u, jobs_at[n])

                copy_out(0, 0, range(NPP))
                over_batches_ahead(a, body)

            @block.vector
            def _(v):
                st.vector(v)
                v.wait_ge(loaded, 16 * n_loads)
                if cross:
                    v.tensor_copy(wk_hi[:], wk_sb).then_inc(w_split, 1)
                    v.wait_ge(w_split, 2)
                    v.tensor_tensor(wk_lo[:], wk_sb, wk_hi[:].bitcast(F32), ALU.subtract).then_inc(w_split, 1)
                    v.tensor_tensor(wv_lo[:], wv_sb, wv_hi[:].bitcast(F32), ALU.subtract).then_inc(w_split, 1)
                if bq is not None:
                    for g in range(G):
                        last = v.tensor_scalar(bq_sb[0:rows[g], g:g + 1], bq_sb[0:rows[g], g:g + 1], scale, None, ALU.mult)
                    last.then_inc(scaled, 1)
                if spread:
                    v.wait_ge(filled, 3 if maskrow is not None else 1)

                def normed_rows(b, u):
                    wait(v, pp_ready, (b - 2) * NPP + 1)
                    st.rows(v, b, xn[:, u, :], xn_ready, h=y, h_done=h_done, scale_row=ns_sb[:] if ns_sb is not None else None)

                def spread_queries(b, u, g):
                    v.wait_ge(pp_empty, b * NPP + jobs.index(("q", 0)) + 1)
                    wait(v, s_ready, (b - 1) * NU)
                    h0, m = groups[g]
                    r = slice(0, rows[g])
                    v.tensor_tensor(qT[r, u, h0:h0 + m, :], q_sb[r, u, g:g + 1, :].broadcast_to([rows[g], m, T]),
                                    sel[r, h0:h0 + m].unsqueeze(2).broadcast_to([rows[g], m, T]), ALU.mult).then_inc(q_spread, 1)

                def maxima(b, u, i, n):
                    v.wait_ge(s_ready, b * NU + n + 1)
                    src = sc[0:T, slot_of(u, n, 2), 0:HU * S].rearrange("p (c s) -> p c s", c=HU)
                    if has_add:
                        wait(v, e_ready, before(b, n, 2))
                        if pos_dram is not None:
                            if n == 0:
                                v.wait_ge(pos_in[u], i * 16 + 16)
                            add = pos_sb[:, u]
                        else:
                            add = addend[:]
                        add = add[:, n * HU:(n + 1) * HU, :]
                        v.tensor_tensor(logit[:, slot_of(u, n, 2), :, :], src, add, ALU.add).then_inc(l_ready, 1)
                        v.wait_ge(l_ready, b * NU + n + 1)
                        src = logit[:, slot_of(u, n, 2), :, :]
                    v.tensor_reduce(nmax[:, u, n, :], src, AX_X, ALU.max, negate=True).then_inc(m_ready, 1)

                def copy_turned(b, u, n):
                    v.wait_ge(t_ready, b * NU + n + 1)
                    wait(v, pv_done, before(b, n, 2))
                    v.tensor_copy(pT[:, slot_of(u, n, 2), :, :].rearrange("p c t -> p (c t)"),
                                  tr[0:kc, slot_of(u, n, 2), 0:HU * nkc * T]).then_inc(t_empty, 1)

                def normalise(b, u):
                    v.wait_ge(pv_done, (b + 1) * NU)
                    v.reciprocal(rden[:, u], den[:, u]).then_inc(rden_ready, 1)
                    v.wait_ge(rden_ready, b + 1)
                    o3 = o_sb[:, u % OS, :].rearrange("p (h d) -> p h d", d=dv)
                    p3 = o_all(u).rearrange("p (h d) -> p h d", d=dv)
                    rd = rden[:, u].rearrange("p n c -> p (n c)").unsqueeze(2).broadcast_to([T, heads, dv])
                    v.tensor_tensor(o3, p3, rd, ALU.mult).then_inc(o_norm, 1)
                    v.wait_ge(o_norm, b + 1)
                    if bv is not None:
                        last = v.tensor_tensor(o_sb[:, u % OS, :], o_sb[:, u % OS, :], bv_sb[:], ALU.add)
                        if wo is not None:
                            last.then_inc(o_ready, 1)
                        else:
                            last.then_inc(o_bias, 1)
                            v.wait_ge(o_bias, b + 1)
                    elif gate:
                        v.tensor_scalar(gate_w[:, u, :], gate_w[:, u, :], 1.0, None, ALU.add).then_inc(g_steps, 1)
                        v.wait_ge(g_steps, b * 2 + 1)
                        v.reciprocal(gate_sb[:, u, :], gate_w[:, u, :]).then_inc(g_steps, 1)
                        v.wait_ge(g_steps, b * 2 + 2)
                        v.tensor_tensor(o_sb[:, u % OS, :], o_sb[:, u % OS, :], gate_sb[:, u, :], ALU.mult).then_inc(o_ready, 1)
                    elif wo is not None:
                        v.sem_inc(o_ready, 1)
                    if wo is None:
                        v.tensor_tensor(batch(dest, b), batch(dest, b), o_sb[:, u % OS, :], ALU.add).then_inc(x_done, 1)

                def copy_output(b, n):
                    v.wait_ge(ty_ready, b * NTY + n + 1)
                    blocks = min(4, NBLK - 4 * n)
                    v.tensor_copy(oT[:, 4 * n:4 * n + blocks, :].rearrange("p k t -> p (k t)"), ty[:, 0:blocks * T]).then_inc(ty_empty, 1)

                def add_output(b):
                    v.wait_ge(ty_ready, (b + 1) * NTY)
                    v.tensor_tensor(batch(dest, b), batch(dest, b), ty[0:T, 0:D], ALU.add).then_inc(ty_empty, 1)

                def body(b, u, i):
                    for n in range(NU):
                        if NU == 1 and not is_static(b, NB - 1):
                            normed_rows(b + 1, 1 - u)
                        maxima(b, u, i, n)
                        if NU > 1 and n == 0 and not is_static(b, NB - 1):
                            normed_rows(b + 1, 1 - u)
                        out = wo is not None and not is_static(b, 0)
                        if out and 0 <= n - X0 < NTT:
                            copy_output(b - 1, n - X0)
                        if (at := back(b, u, n, LT)) is not None:
                            copy_turned(*at)
                        if n == LV - 1 and not is_static(b, 0):
                            normalise(b - 1, 1 - u)
                        if out and n == X0 + NTT - 1:
                            add_output(b - 1)
                        for g in range(G):
                            if spread and n == min(NU - 1, spread_at + g) and not is_static(b, NB - 1):
                                spread_queries(b + 1, 1 - u, g)

                normed_rows(0, 0)
                for g in range(G):
                    if spread:
                        spread_queries(0, 0, g)
                over_batches_ahead(v, body)
                for n in range(LT):
                    copy_turned(*back(NB, 0, n, LT))
                normalise(NB - 1, 1)
                for n in range(NTT):
                    copy_output(NB - 1, n)
                if wo is not None:
                    add_output(NB - 1)



HD0 = 64
ROWS = 8
NG0 = T // ROWS
NGP = 7


def channel_attention(nc, x, K, wqkv, woutT):
    name = "l0a"
    ident = K["ident"]
    with Phase(nc, name + "o") as outer:
        qkv = outer.sb("qkv", [128, 3, NPAIR, T])
        num = outer.sb("num", [128, NPAIR, T])
        den = outer.sb("den", [128, NPAIR, T])
        nmx = outer.sb("nmx", [128, NPAIR, T])

        with Phase(nc, name + "p") as p:
            w = p.sb("w", [128, KD, 3 * HD0])
            xn = p.sb("xn", [T, 2, D])
            xnT = p.sb("xnT", [128, 2, KD, T])
            ptx = p.ps("ptx", [128, 2, 512])
            pqk = p.ps("pqk", [128, 2, 512])
            st = Norm(p, x, "ln")
            loaded, xn_ready, tx_ready = p.sem("loaded"), p.sem("xn_ready"), p.sem("tx_ready")
            xT_ready, qk_ready, qk_out = p.sem("xT_ready"), p.sem("qk_ready"), p.sem("qk_out")
            with nc.Block() as block:

                @block.sync
                def _(sp):
                    sp.dma_start(w[:], wqkv.rearrange("(k p) n -> p k n", p=128)).then_inc(loaded, 16)

                @block.vector
                def _(v):
                    st.vector(v)

                    def normed_rows(b, u):
                        wait(v, tx_ready, b - 1)
                        st.rows(v, b, xn[:, u, :], xn_ready)

                    def body(b, u, i):
                        if not is_static(b, NB - 1):
                            normed_rows(b + 1, 1 - u)
                        v.wait_ge(tx_ready, b + 1)
                        wait(v, qk_ready, b - 1)
                        v.tensor_copy(xnT[:, u].rearrange("p k t -> p (k t)"), ptx[:, u, 0:KD * T]).then_inc(xT_ready, 1)

                    normed_rows(0, 0)
                    over_batches_ahead(v, body)

                @block.tensor
                def _(pe):
                    pe.wait_ge(loaded, 16)

                    def turn(b, u):
                        pe.wait_ge(xn_ready, b + 1)
                        wait(pe, xT_ready, b - 1)
                        for k in range(KD):
                            last = pe.transpose(ptx[:, u, k * T:(k + 1) * T], xn[:, u, k * 128:(k + 1) * 128], ident[0:T, 0:T])
                        last.then_inc(tx_ready, 1)

                    def body(b, u, i):
                        if not is_static(b, NB - 1):
                            turn(b + 1, 1 - u)
                        pe.wait_ge(xT_ready, b + 1)
                        wait(pe, qk_out, b - 1)
                        for c in range(3):
                            for k in range(KD):
                                last = pe.matmul(pqk[64 * u:64 * u + 64, u, c * T:(c + 1) * T], w[:, k, c * HD0:(c + 1) * HD0],
                                                 xnT[:, u, k, :], start=k == 0, stop=k == KD - 1)
                        last.then_inc(qk_ready, 1)

                    turn(0, 0)
                    over_batches_ahead(pe, body)

                @block.scalar
                def _(a):
                    st.scalar(a)

                    def body(b, u, i):
                        a.wait_ge(qk_ready, b + 1)
                        half = slice(64 * u, 64 * u + 64)
                        for c in range(3):
                            dst = qkv[half, c, bass.ds(i, 1), :].rearrange("p i t -> p (i t)")
                            last = a.activation(dst, pqk[half, u, c * T:(c + 1) * T], ACT.Copy, scale=HD0 ** -0.5 if c == 0 else 1.0)
                        last.then_inc(qk_out, 1)

                    over_batches(a, body)

        with Phase(nc, name + "s") as p:
            cmax, cmin = p.sb("cmax", [128, NPAIR, T]), p.sb("cmin", [128, NPAIR, T])
            past = p.sb("past", [128, ROWS, ROWS])
            ex = p.sb("ex", [128, NG0, ROWS, T])
            ev = p.sb("ev", [128, 2, ROWS, T])
            scans, max_ready = p.sem("scans"), p.sem("max_ready")
            e_ready, slot_free, prod = p.sem("e_ready"), p.sem("slot_free"), p.sem("prod")
            past_set, l_steps, l_ready, zeroed = (p.sem(s) for s in ("past_set", "l_steps", "l_ready", "zeroed"))
            with nc.Block() as block:

                @block.gpsimd
                def _(g):
                    g.memset(past[:].rearrange("p r s -> p (r s)"), 0.0).then_inc(past_set, 1)
                    g.wait_ge(past_set, 1)
                    g.affine_select(out=past[:], in_=past[:], compare_op=ALU.is_ge, fill=MASKED, base=0,
                                    pattern=[[1, ROWS], [-1, ROWS]], channel_multiplier=0).then_inc(past_set, 1)
                    g.wait_ge(past_set, 2)
                    g.memset(ex[:, NGP:].rearrange("p g r t -> p (g r t)"), 0.0).then_inc(zeroed, 1)
                    g.wait_ge(zeroed, 1)
                    g.wait_ge(max_ready, 1)
                    with g.Fori(0, NPAIR) as i:
                        for n in range(NGP):
                            L = (n + 1) * ROWS
                            rows = slice(n * ROWS, L)
                            e = ex[:, n, :, 0:L]
                            wide = [128, ROWS, L]

                            def across(t):
                                return t.rearrange("p i t -> p (i t)").unsqueeze(2).broadcast_to(wide)
                            g.wait_ge(slot_free, i * NG0 + n + 1)
                            g.tensor_tensor(e, across(qkv[:, 0, bass.ds(i, 1), rows]), qkv[:, 1, bass.ds(i, 1), 0:L].broadcast_to(wide),
                                            ALU.mult).then_inc(l_steps, 1)
                            g.wait_ge(l_steps, i * (2 * NGP) + 2 * n + 1)
                            g.tensor_tensor(e, e, across(nmx[:, bass.ds(i, 1), rows]), ALU.add).then_inc(l_steps, 1)
                            g.wait_ge(l_steps, i * (2 * NGP) + 2 * n + 2)
                            d = ex[:, n, :, L - ROWS:L]
                            g.tensor_tensor(d, d, past[:], ALU.add).then_inc(l_ready, 1)
                            g.wait_ge(l_ready, i * NGP + n + 1)

                @block.vector
                def _(v):
                    for i in range(NPAIR):
                        k = qkv[:, 1, i, :]
                        v.tensor_tensor_scan(cmax[:, i, :], k, k, -3.0e38, ALU.max, ALU.max).then_inc(scans, 1)
                        v.tensor_tensor_scan(cmin[:, i, :], k, k, 3.0e38, ALU.min, ALU.min).then_inc(scans, 1)
                    v.wait_ge(scans, 2 * NPAIR)
                    v.tensor_tensor(cmax[:], cmax[:], qkv[:, 0], ALU.mult).then_inc(scans, 1)
                    v.tensor_tensor(cmin[:], cmin[:], qkv[:, 0], ALU.mult).then_inc(scans, 1)
                    v.wait_ge(scans, 2 * NPAIR + 2)
                    v.tensor_tensor(cmax[:], cmax[:], cmin[:], ALU.max).then_inc(scans, 1)
                    v.wait_ge(scans, 2 * NPAIR + 3)
                    v.tensor_scalar(nmx[:], cmax[:], -1.0, None, ALU.mult).then_inc(max_ready, 1)
                    v.sem_inc(slot_free, NG0)
                    with v.Fori(0, NPAIR) as i:
                        for g in range(NG0):
                            v.wait_ge(e_ready, i * NG0 + g + 1)
                            L = (g + 1) * ROWS
                            e = ex[:, g, :, 0:L]
                            v.tensor_reduce(den[:, bass.ds(i, 1), g * ROWS:L].rearrange("p i t -> p (i t)"), e, AX_X, ALU.add)
                            vrow = qkv[:, 2, bass.ds(i, 1), 0:L].broadcast_to([128, ROWS, L])
                            v.wait_ge(slot_free, i * NG0 + NG0 + g - 1)
                            pv = ev[:, g % 2, :, 0:L]
                            v.tensor_tensor(pv, e, vrow, ALU.mult).then_inc(prod, 1)
                            v.wait_ge(prod, i * NG0 + g + 1)
                            v.tensor_reduce(num[:, bass.ds(i, 1), g * ROWS:L].rearrange("p i t -> p (i t)"), pv, AX_X, ALU.add).then_inc(slot_free, 1)

                @block.scalar
                def _(a):
                    a.wait_ge(max_ready, 1)
                    a.wait_ge(zeroed, 1)
                    with a.Fori(0, NPAIR) as i:
                        for g in range(NG0):
                            if g < NGP:
                                a.wait_ge(l_ready, i * NGP + g + 1)
                                e = ex[:, g, :, 0:(g + 1) * ROWS]
                                a.activation(e, e, ACT.Exp).then_inc(e_ready, 1)
                                continue
                            a.wait_ge(slot_free, i * NG0 + g + 1)
                            for r in range(ROWS):
                                n = g * ROWS + r

                                def at(t, lo, hi):
                                    return t[:, bass.ds(i, 1), lo:hi].rearrange("p i t -> p (i t)")
                                last = a.activation(ex[:, g, r, 0:n + 1], at(qkv[:, 1], 0, n + 1), ACT.Exp, bias=at(nmx, n, n + 1),
                                                    scale=at(qkv[:, 0], n, n + 1))
                            last.then_inc(e_ready, 1)

        with Phase(nc, name + "y") as p:
            w = p.sb("w", [128, D])
            o_st = p.sb("o_st", [128, T])
            py = p.ps("py", [128, 2, 512])
            loaded, recip, o_ready, y_ready, x_done = (p.sem(s) for s in ("loaded", "recip", "o_ready", "y_ready", "x_done"))
            with nc.Block() as block:

                @block.sync
                def _(sp):
                    for u in range(2):
                        sp.dma_start(w[64 * u:64 * u + 64, :], woutT).then_inc(loaded, 16)

                @block.vector
                def _(v):
                    v.reciprocal(den[:], den[:]).then_inc(recip, 1)
                    v.wait_ge(recip, 1)

                    def outputs(b, u, i):
                        half = slice(64 * u, 64 * u + 64)
                        wait(v, y_ready, b - 1)
                        v.tensor_tensor(o_st[half, :], num[half, bass.ds(i, 1), :].rearrange("p i t -> p (i t)"),
                                        den[half, bass.ds(i, 1), :].rearrange("p i t -> p (i t)"), ALU.mult).then_inc(o_ready, 1)

                    def body(b, u, i):
                        if not is_static(b, NB - 1):
                            outputs(b + 1, 1 - u, i + u)
                        v.wait_ge(y_ready, b + 1)
                        v.tensor_tensor(batch(x, b), batch(x, b), py[0:T, u, 0:D], ALU.add).then_inc(x_done, 1)

                    outputs(0, 0, 0)
                    over_batches_ahead(v, body)

                @block.tensor
                def _(pe):
                    pe.wait_ge(loaded, 32)

                    def body(b, u, i):
                        half = slice(64 * u, 64 * u + 64)
                        pe.wait_ge(o_ready, b + 1)
                        wait(pe, x_done, b - 1)
                        pe.matmul(py[0:T, u, 0:D], o_st[half, :], w[half, :], start=True, stop=True).then_inc(y_ready, 1)

                    over_batches(pe, body)



def offset_bias(nc, bias, K, pos_biasT, offsets, scratch):
    H, NO = pos_biasT.shape
    with Phase(nc, "l1b") as p:
        pb, off, offf = p.sb("pb", [H, NO]), p.sb("off", [H, NO], I32), p.sb("offf", [H, NO])
        diff = p.sb("diff", [H, T], I32)
        difff = p.sb("difff", [H, T])
        a = p.sb("a", [H, T, NO])
        mx, sm, row = p.sb("mx", [H, T]), p.sb("sm", [H, T]), p.sb("row", [H, RELS])
        loaded, iota_done, steps, to_act, act_done, row_ready, stored, back = (
            p.sem(s) for s in ("loaded", "iota_done", "steps", "to_act", "act_done", "row_ready", "stored", "back"))
        with nc.Block() as block:

            @block.sync
            def _(sp):
                sp.dma_start(pb[:], pos_biasT).then_inc(loaded, 16)
                sp.dma_start(off[:], offsets.rearrange("(a n) -> a n", a=1).broadcast_to([H, NO])).then_inc(loaded, 16)
                sp.wait_ge(row_ready, 2)
                sp.dma_start(scratch, row[:].unsqueeze(1).broadcast_to([H, T, RELS])).then_inc(stored, 16)
                sp.wait_ge(stored, 16)
                sp.dma_start(bias[:], skewed(scratch, 0, H)).then_inc(back, 16)
                sp.wait_ge(back, 16)

            @block.gpsimd
            def _(g):
                g.iota(diff[:], pattern=[[-1, T]], base=T - 1, channel_multiplier=0).then_inc(iota_done, 1)

            @block.vector
            def _(v):
                n = 0

                def chain(ins):
                    nonlocal n
                    n += 1
                    ins.then_inc(steps, 1)
                    v.wait_ge(steps, n)

                v.memset(row[:], MASKED).then_inc(row_ready, 1)
                v.wait_ge(loaded, 32)
                v.wait_ge(iota_done, 1)
                chain(v.tensor_copy(offf[:], off[:]))
                chain(v.tensor_copy(difff[:], diff[:]))
                wide = [H, T, NO]
                chain(v.tensor_tensor(a[:], difff[:].unsqueeze(2).broadcast_to(wide), offf[:].unsqueeze(1).broadcast_to(wide), ALU.not_equal))
                chain(v.tensor_scalar(a[:], a[:], MASKED, None, ALU.mult))
                chain(v.tensor_tensor(a[:], a[:], pb[:].unsqueeze(1).broadcast_to(wide), ALU.add))
                chain(v.tensor_reduce(mx[:], a[:], AX_X, ALU.max))
                chain(v.tensor_tensor(a[:], a[:], mx[:].unsqueeze(2).broadcast_to(wide), ALU.subtract))
                v.sem_inc(to_act, 1)
                v.wait_ge(act_done, 1)
                v.tensor_reduce(sm[:], a[:], AX_X, ALU.add).then_inc(to_act, 1)
                v.wait_ge(act_done, 2)
                v.wait_ge(row_ready, 1)
                v.tensor_tensor(row[:, 0:T], sm[:], mx[:], ALU.add).then_inc(row_ready, 1)

            @block.scalar
            def _(s):
                s.wait_ge(to_act, 1)
                s.activation(a[:], a[:], ACT.Exp).then_inc(act_done, 1)
                s.wait_ge(to_act, 2)
                s.activation(sm[:], sm[:], ACT.Ln).then_inc(act_done, 1)


def skewed(scratch, b, H):
    flat = scratch.rearrange("h t r -> h (t r)")
    part = flat[bass.ds(b * H, H), T - 1:T - 1 + T * (RELS - 1)]
    return part.rearrange("h (t r) -> t h r", r=RELS - 1)[:, :, 0:T]



def relative_positions(nc, x, K, wq, bq, wrT, br, scratch):
    H, HD, G = 16, 16, len(GROUPS)
    ident, sel = K["ident"], K["sel"]
    with Phase(nc, "l2p") as p:
        w = p.sb("w", [128, KD, G * 128])
        wr = p.sb("wr", [128, RELS])
        br_sb = p.sb("br", [T, RELS])
        bq_sb = p.sb("bq", [128, G])
        q_bias = p.sb("q_bias", [128, H])
        xn, xnT, qT = p.sb("xn", [T, 2, D]), p.sb("xnT", [128, 2, KD, T]), p.sb("qT", [128, 2, H, T])
        rp = p.sb("rp", [T, 2, H, RELS])
        pp, pr = p.ps("pp", [128, 2, 512]), p.ps("pr", [128, 4, 512])
        st = Norm(p, x, "ln")
        loaded, bq_ready, xn_ready, pp_ready, pp_empty, r_ready, r_out = (
            p.sem(s) for s in ("loaded", "bq_ready", "xn_ready", "pp_ready", "pp_empty", "r_ready", "r_out"))
        stored = [p.sem(f"stored{u}") for u in range(2)]
        lo = REL_WINDOW - (T - 1)
        NR = H // 2
        loads = [(w[:], wq.rearrange("(k p) n -> p k n", p=128)), (br_sb[:], row_bcast(br[lo:lo + RELS], T))]
        loads += [(bq_sb[:, g:g + 1], bq[g * 128:(g + 1) * 128].rearrange("(n a) -> n a", a=1)) for g in range(G)]
        loads += [(wr[HD * h:HD * (h + 1), :], wrT[:, lo:lo + RELS]) for h in range(128 // HD)]
        with nc.Block() as block:

            @block.sync
            def _(sp):
                for dst, src in loads:
                    sp.dma_start(dst, src).then_inc(loaded, 16)

                def body(b, u, i):
                    sp.wait_ge(r_out, (b + 1) * NR)
                    sp.dma_start(scratch[bass.ds(b * H, H)].rearrange("h t r -> t h r"), rp[:, u, :, :]).then_inc(stored[u], 16)

                over_batches(sp, body)
                for u in range(2):
                    sp.wait_ge(stored[u], 16 * NPAIR)

            @block.tensor
            def _(pe):
                pe.wait_ge(loaded, 16 * len(loads))

                def queries(b, u):
                    pe.wait_ge(xn_ready, b + 1)
                    wait(pe, pp_empty, b * 2 - 1)
                    for k in range(KD):
                        last = pe.transpose(pp[:, 0, k * T:(k + 1) * T], xn[:, u, k * 128:(k + 1) * 128], ident[0:T, 0:T])
                    last.then_inc(pp_ready, 1)
                    pe.wait_ge(pp_empty, b * 2 + 1)
                    for g in range(G):
                        for k in range(KD):
                            last = pe.matmul(pp[:, 1, g * T:(g + 1) * T], w[:, k, g * 128:(g + 1) * 128], xnT[:, u, k, :],
                                             start=k == 0, stop=k == KD - 1)
                    last.then_inc(pp_ready, 1)

                def body(b, u, i):
                    pe.wait_ge(pp_empty, b * 2 + 2)
                    for n in range(NR):
                        wait(pe, r_out, reuse(b, n, NR, 4))
                        for c in range(2):
                            last = pe.matmul(pr[0:T, n % 4, c * RELS:(c + 1) * RELS], qT[:, u, 2 * n + c, :], wr[:], start=True, stop=True)
                        last.then_inc(r_ready, 1)
                        if n == 3 and not is_static(b, NB - 1):
                            queries(b + 1, 1 - u)

                queries(0, 0)
                over_batches_ahead(pe, body)

            @block.scalar
            def _(a):
                st.scalar(a)
                a.wait_ge(bq_ready, G)

                def body(b, u, i):
                    a.wait_ge(pp_ready, b * 2 + 1)
                    a.activation(xnT[:, u].rearrange("p k t -> p (k t)"), pp[:, 0, 0:KD * T], ACT.Copy).then_inc(pp_empty, 1)
                    a.wait_ge(pp_ready, b * 2 + 2)
                    wait(a, r_ready, (b - 1) * NR)
                    for h in range(H):
                        g = h // 8
                        last = a.activation(qT[:, u, h, :], pp[:, 1, g * T:(g + 1) * T], ACT.Identity, scale=sel[:, h:h + 1], bias=q_bias[:, h:h + 1])
                    last.then_inc(pp_empty, 1)

                over_batches(a, body)

            @block.vector
            def _(v):
                st.vector(v)
                v.wait_ge(loaded, 16 * len(loads))
                for g, (h0, m) in enumerate(GROUPS):
                    v.tensor_scalar(q_bias[:, h0:h0 + m], sel[:, h0:h0 + m], bq_sb[:, g:g + 1], None, ALU.mult).then_inc(bq_ready, 1)

                def normed_rows(b, u):
                    wait(v, pp_ready, b * 2 - 3)
                    st.rows(v, b, xn[:, u, :], xn_ready)

                def body(b, u, i):
                    if not is_static(b, NB - 1):
                        normed_rows(b + 1, 1 - u)
                    wait(v, stored[u], i * 16)
                    for n in range(NR):
                        v.wait_ge(r_ready, b * NR + n + 1)
                        v.tensor_tensor(rp[:, u, 2 * n:2 * n + 2, :], pr[0:T, n % 4, 0:2 * RELS].rearrange("p (c r) -> p c r", c=2),
                                        br_sb[:].unsqueeze(1).broadcast_to([T, 2, RELS]), ALU.add).then_inc(r_out, 1)

                normed_rows(0, 0)
                over_batches_ahead(v, body)



def normed_transposed(nc, name, y, K, xnT_all, norm_scale):
    ident = K["ident"]
    with Phase(nc, name + "n") as p:
        xn, xnT = p.sb("xn", [T, 2, D]), p.sb("xnT", [128, 2, KD, T])
        ns_sb = p.sb("ns", [T, D])
        ptx = p.ps("ptx", [128, 2, 512])
        st = Norm(p, y, "rms")
        loaded, xn_ready, tx_ready, xT_ready, all_ready, h_done = (
            p.sem(s) for s in ("loaded", "xn_ready", "tx_ready", "xT_ready", "all_ready", "h_done"))
        with nc.Block() as block:

            @block.sync
            def _(sp):
                sp.dma_start(ns_sb[:], row_bcast(norm_scale, T)).then_inc(loaded, 16)

            @block.tensor
            def _(pe):
                def body(b, u, i):
                    pe.wait_ge(xn_ready, b + 1)
                    wait(pe, xT_ready, b - 1)
                    for k in range(KD):
                        last = pe.transpose(ptx[:, u, k * T:(k + 1) * T], xn[:, u, k * 128:(k + 1) * 128], ident[0:T, 0:T])
                    last.then_inc(tx_ready, 1)

                over_batches(pe, body)

            @block.scalar
            def _(a):
                st.scalar(a)

                def body(b, u, i):
                    a.wait_ge(tx_ready, b + 1)
                    wait(a, all_ready, b - 1)
                    a.activation(xnT[:, u].rearrange("p k t -> p (k t)"), ptx[:, u, 0:KD * T], ACT.Copy).then_inc(xT_ready, 1)

                over_batches(a, body)

            @block.vector
            def _(v):
                st.vector(v)
                v.wait_ge(loaded, 16)

                def normed_rows(b, u):
                    wait(v, tx_ready, b - 1)
                    st.rows(v, b, xn[:, u, :], xn_ready, h=y, h_done=h_done, scale_row=ns_sb[:])

                def body(b, u, i):
                    if not is_static(b, NB - 1):
                        normed_rows(b + 1, 1 - u)
                    v.wait_ge(xT_ready, b + 1)
                    v.tensor_scalar(xnT_all[:, :, bass.ds(b * T, T)], xnT[:, u, :, :], 1.0, None, ALU.mult).then_inc(all_ready, 1)

                normed_rows(0, 0)
                over_batches_ahead(v, body)



class Route:

    def __init__(self, ctx, nc, name, choices, S, capacity):
        def sb(n, shape, dt):
            return ctx.enter_context(nc.sbuf_tensor(f"{name}_{n}", shape, dt))

        self.choices, self.S, self.capacity = choices, S, capacity
        self.tiles = NE if capacity else (NB * T * choices + NE * (S - 1)) // S
        self.put = sb("put", [T, choices, NB], U32)
        self.get = sb("get", [T, choices, NB], U32)
        self.wt = sb("wt", [T, choices, NB], F32)
        self.expert = sb("expert", [1, self.tiles], I32)
        subs = -(-S // 128)
        self.sub = [min(-(-S // subs), S - i * -(-S // subs)) for i in range(subs)]


def route(nc, name, x, K, R, first_wins, wg, bg, slots):
    ident, ones = K["ident"], K["ones"]
    S = R.S
    with Phase(nc, name + "g") as p:
        xn, xnT, xn_all = p.sb("xn", [T, 2, D]), p.sb("xnT", [128, 2, KD, T]), p.sb("xn_all", [T, NB, D])
        wg_sb, bg_sb = p.sb("wg", [128, KD, NE]), p.sb("bg", [T, NE])
        ptx, plg = p.ps("ptx", [128, 2, 512]), p.ps("plg", [128, 2, 512])
        st = Norm(p, x, "ln")
        big = [T, NB, NE]
        lg, pr, rem, eq, key, chosen, cnt, slot = (p.sb(s, big) for s in ("lg", "pr", "rem", "eq", "key", "chosen", "cnt", "slot"))
        oh = [p.sb(f"oh{k}", big) for k in range(R.choices)]
        pref, prefi = p.sb("pref", [T, NE]), p.sb("prefi", [T, NE], I32)
        m = p.sb("m", [T, NB])
        tot, nt, nti, incl, base, basei = (p.sb(s, [T, NE], dt) for s, dt in (("tot", F32), ("nt", F32), ("nti", I32), ("incl", F32), ("base", F32), ("basei", I32)))
        tokeni, token = p.sb("tokeni", [T, NB], I32), p.sb("token", [T, NB])
        jti, jt, jte, je = p.sb("jti", [1, R.tiles], I32), p.sb("jt", [1, R.tiles]), p.sb("jte", [1, R.tiles, NE]), p.sb("je", [1, R.tiles])
        sl, kp = p.sb("sl", [T, NB]), p.sb("kp", [T, NB])
        loaded, xn_ready, tx_ready, xT_ready, l_ready, l_out, xa_ready = (
            p.sem(s) for s in ("loaded", "xn_ready", "tx_ready", "xT_ready", "l_ready", "l_out", "xa_ready"))
        steps, iota_done, to_act, act_done, to_pe, pe_done, put_ready = (
            p.sem(s) for s in ("steps", "iota_done", "to_act", "act_done", "to_pe", "pe_done", "put_ready"))
        sent = K["rows_sent"]
        loads = [(wg_sb[:], wg.rearrange("(k p) n -> p k n", p=128))]
        if bg is not None:
            loads.append((bg_sb[:], row_bcast(bg, T)))
        with nc.Block() as block:

            @block.sync
            def _(sp):
                for dst, src in loads:
                    sp.dma_start(dst, src).then_inc(loaded, 16)

            @block.gpsimd
            def _(g):
                g.iota(prefi[:], pattern=[[-1 if first_wins else 1, NE]], base=NE if first_wins else 1, channel_multiplier=0).then_inc(iota_done, 1)
                g.iota(basei[:], pattern=[[S, NE]], base=0, channel_multiplier=0).then_inc(iota_done, 1)
                g.iota(jti[:], pattern=[[1, R.tiles]], base=0, channel_multiplier=0).then_inc(iota_done, 1)
                g.iota(tokeni[:], pattern=[[T, NB]], base=R.tiles * S, channel_multiplier=1).then_inc(iota_done, 1)
                g.wait_ge(xa_ready, NB)
                for k in range(R.choices):
                    g.wait_ge(put_ready, k + 1)
                    for b in range(NB):
                        g.indirect_dma_start(slots, bass.IndirectOffsetOnAxis(ap=R.put[:, k, b:b + 1], axis=0),
                                             xn_all[:, b, :], None).then_inc(sent.sem, 16)
                sent.base += 16 * NB * R.choices
                g.wait_ge(sent.sem, sent.base)

            @block.tensor
            def _(pe):
                pe.wait_ge(loaded, 16 * len(loads))

                def turn(b, u):
                    pe.wait_ge(xn_ready, b + 1)
                    wait(pe, xT_ready, b - 1)
                    for k in range(KD):
                        last = pe.transpose(ptx[:, u, k * T:(k + 1) * T], xn[:, u, k * 128:(k + 1) * 128], ident[0:T, 0:T])
                    last.then_inc(tx_ready, 1)

                def body(b, u, i):
                    if not is_static(b, NB - 1):
                        turn(b + 1, 1 - u)
                    pe.wait_ge(xT_ready, b + 1)
                    wait(pe, l_out, b - 1)
                    for k in range(KD):
                        last = pe.matmul(plg[0:T, u, 0:NE], xnT[:, u, k, :], wg_sb[:, k, :], start=k == 0, stop=k == KD - 1)
                    last.then_inc(l_ready, 1)

                turn(0, 0)
                over_batches_ahead(pe, body)
                pe.wait_ge(to_pe, 1)
                pe.wait_ge(xT_ready, NB)
                pe.matmul(ptx[0:T, 0, 0:NB * NE], K["upto"][0:T, 0:T], chosen[:].rearrange("p b e -> p (b e)"), start=True, stop=False)
                pe.matmul(ptx[0:T, 0, 0:NB * NE], ones[0:T, 0:T], cnt[:].rearrange("p b e -> p (b e)"), start=False, stop=True)
                pe.matmul(ptx[0:T, 1, 0:NE], ones[0:T, 0:T], tot[:], start=True, stop=True).then_inc(pe_done, 1)

            @block.scalar
            def _(a):
                st.scalar(a)

                def body(b, u, i):
                    a.wait_ge(tx_ready, b + 1)
                    wait(a, l_ready, b - 1)
                    a.activation(xnT[:, u].rearrange("p k t -> p (k t)"), ptx[:, u, 0:KD * T], ACT.Copy).then_inc(xT_ready, 1)

                over_batches(a, body)
                a.wait_ge(to_act, 1)
                a.activation(pr[:], lg[:], ACT.Exp).then_inc(act_done, 1)

            @block.vector
            def _(v):
                n = 0

                def chain(ins):
                    nonlocal n
                    n += 1
                    ins.then_inc(steps, 1)
                    v.wait_ge(steps, n)

                def wide(t):
                    return t[:].unsqueeze(2).broadcast_to(big)

                def across(t):
                    return t[:].unsqueeze(1).broadcast_to(big)

                st.vector(v)
                v.wait_ge(loaded, 16 * len(loads))
                v.wait_ge(iota_done, 4)
                v.tensor_copy(pref[:], prefi[:]).then_inc(steps, 1)
                v.tensor_copy(base[:], basei[:]).then_inc(steps, 1)
                v.tensor_copy(jt[:], jti[:]).then_inc(steps, 1)
                n += 3
                chain(v.tensor_copy(token[:], tokeni[:]))

                def normed_rows(b, u):
                    wait(v, tx_ready, b - 1)
                    st.rows(v, b, xn[:, u, :], xn_ready)
                    st.rows(v, b, batch(xn_all, b), xa_ready)

                def body(b, u, i):
                    if not is_static(b, NB - 1):
                        normed_rows(b + 1, 1 - u)
                    v.wait_ge(l_ready, b + 1)
                    if bg is not None:
                        v.tensor_tensor(batch(lg, b), plg[0:T, u, 0:NE], bg_sb[:], ALU.add).then_inc(l_out, 1)
                    else:
                        v.tensor_copy(batch(lg, b), plg[0:T, u, 0:NE]).then_inc(l_out, 1)

                normed_rows(0, 0)
                over_batches_ahead(v, body)
                v.wait_ge(l_out, NB)
                chain(v.tensor_reduce(m[:], lg[:], AX_X, ALU.max))
                v.tensor_tensor(lg[:], lg[:], wide(m), ALU.subtract).then_inc(to_act, 1)
                v.wait_ge(act_done, 1)
                chain(v.tensor_reduce(m[:], pr[:], AX_X, ALU.add))
                chain(v.reciprocal(m[:], m[:]))
                chain(v.tensor_tensor(pr[:], pr[:], wide(m), ALU.mult))

                def pick(src, out):
                    chain(v.tensor_reduce(m[:], src[:], AX_X, ALU.max))
                    chain(v.tensor_tensor(eq[:], src[:], wide(m), ALU.is_equal))
                    chain(v.tensor_tensor(key[:], eq[:], across(pref), ALU.mult))
                    chain(v.tensor_reduce(m[:], key[:], AX_X, ALU.max))
                    chain(v.tensor_tensor(out[:], key[:], wide(m), ALU.is_equal))

                pick(pr, oh[0])
                if R.choices == 2:
                    chain(v.scalar_tensor_tensor(rem[:], oh[0][:], -2.0, pr[:], ALU.mult, ALU.add))
                    pick(rem, oh[1])
                    chain(v.tensor_tensor(chosen[:], oh[0][:], oh[1][:], ALU.add))
                else:
                    chain(v.tensor_copy(chosen[:], oh[0][:]))
                chain(v.memset(cnt[:, 0, :], 0.0))
                for b in range(1, NB):
                    chain(v.tensor_tensor(cnt[:, b, :], cnt[:, b - 1, :], chosen[:, b - 1, :], ALU.add))
                v.tensor_tensor(tot[:], cnt[:, NB - 1, :], chosen[:, NB - 1, :], ALU.add).then_inc(to_pe, 1)
                v.wait_ge(pe_done, 1)
                place = ptx[0:T, 0, 0:NB * NE].rearrange("p (b e) -> p b e", e=NE)
                if not R.capacity:
                    chain(v.tensor_scalar(nti[:], ptx[0:T, 1, 0:NE], float(S - 1), None, ALU.add))
                    chain(v.tensor_scalar(nti[:], nti[:], S.bit_length() - 1, None, ALU.logical_shift_right))
                    chain(v.tensor_copy(nt[:], nti[:]))
                    chain(v.tensor_tensor_scan(incl[:], ones[0:T, 0:NE], nt[:], 0.0, ALU.mult, ALU.add))
                    chain(v.tensor_tensor(base[:], incl[:], nt[:], ALU.subtract))
                    chain(v.tensor_scalar(base[:], base[:], float(S), None, ALU.mult))
                    js = [1, R.tiles, NE]
                    chain(v.tensor_tensor(jte[:], jt[:].unsqueeze(2).broadcast_to(js), incl[0:1, :].unsqueeze(1).broadcast_to(js), ALU.is_ge))
                    chain(v.tensor_reduce(je[:], jte[:], AX_X, ALU.add))
                    chain(v.tensor_scalar(R.expert[:], je[:], float(NE - 1), None, ALU.min))
                else:
                    chain(v.tensor_scalar(key[:], place, float(CAPACITY), None, ALU.is_le))
                    chain(v.tensor_tensor(eq[:], key[:], chosen[:], ALU.mult))
                    chain(v.tensor_reduce(kp[:], eq[:], AX_X, ALU.add))
                chain(v.tensor_tensor(slot[:], place, across(base), ALU.add))
                for k in range(R.choices):
                    chain(v.tensor_tensor(eq[:], oh[k][:], slot[:], ALU.mult))
                    chain(v.tensor_reduce(sl[:], eq[:], AX_X, ALU.add))
                    chain(v.tensor_scalar(sl[:], sl[:], -1.0, None, ALU.add))
                    chain(v.tensor_tensor(key[:], oh[k][:], pr[:], ALU.mult))
                    chain(v.tensor_reduce(R.wt[:, k, :], key[:], AX_X, ALU.add))
                    if R.capacity:
                        chain(v.tensor_tensor(R.wt[:, k, :], R.wt[:, k, :], kp[:], ALU.mult))
                        chain(v.tensor_tensor(sl[:], sl[:], kp[:], ALU.mult))
                        chain(v.tensor_copy(R.get[:, k, :], sl[:]))
                        chain(v.tensor_scalar(kp[:], kp[:], -1.0, 1.0, ALU.mult, ALU.add))
                        chain(v.tensor_tensor(token[:], token[:], kp[:], ALU.mult))
                        chain(v.tensor_tensor(sl[:], sl[:], token[:], ALU.add))
                    else:
                        chain(v.tensor_copy(R.get[:, k, :], sl[:]))
                    v.tensor_copy(R.put[:, k, :], sl[:]).then_inc(put_ready, 1)


def over_tiles(eng, n, body):
    for u in range(2):
        body(u, u, 0)
    with eng.Fori(1, n // 2) as i:
        for u in range(2):
            body(i * 2 + u, u, i)
    if n % 2:
        body(n - 1, 0, n // 2)


def routed_experts(nc, name, K, R, slots, outs, w_up, w_gate, w_down, b_up, b_gate, b_down, act):
    ident, ones = K["ident"], K["ones"]
    S, NTL = R.S, R.tiles
    HID = w_up.shape[2]
    NM = HID // 128
    two = w_gate is not None
    NS = len(R.sub)
    SUB = R.sub[0]
    NY = 3
    with Phase(nc, name + "e") as p:
        wu = p.sb("wu", [128, 2, KD, HID])
        wg = p.sb("wg", [128, 2, KD, HID]) if two else None
        wd = p.sb("wd", [128, 2, NM, D])
        bu = p.sb("bu", [128, 2, NM]) if b_up is not None else None
        bg = p.sb("bg", [128, 2, NM]) if b_gate is not None else None
        bd = p.sb("bd", [1, 2, D]) if b_down is not None else None
        xs = p.sb("xs", [SUB, 2, NS, D])
        xT = p.sb("xT", [128, 2, KD, S])
        hT = p.sb("hT", [128, 2, NM, S])
        hs = p.sb("hs", [128, 2, S])
        hp = p.sb("hp", [128, 2, S])
        ys = p.sb("ys", [SUB, 2, NS, D])
        pt = p.ps("pt", [128, KD, 512])
        ph = p.ps("ph", [128, 2, 512])
        py = p.ps("py", [128, NY, 512])
        w_in = [p.sem(f"w_in{u}") for u in range(2)]
        x_in = [p.sem(f"x_in{u}") for u in range(2)]
        y_sent = K["tile_stored"]
        t_ready = p.sem("t_ready")
        t_out = p.sem("t_out")
        h_ready = p.sem("h_ready")
        h_half = p.sem("h_half")
        h_prod = p.sem("h_prod")
        h_out = p.sem("h_out")
        y_ready = p.sem("y_ready")
        y_out = p.sem("y_out")
        extra = [(t, src) for t, src in ((bu, b_up), (bg, b_gate)) if t is not None]
        n_w = 2 + two + len(extra) + (b_down is not None)

        def hb(j, u, m):
            return ph[:, m % 2, :]

        def yb(u, s):
            return s if NS > 1 else u

        def y_sent_before(j, u):
            return (j - u) // 2 * (16 * NS) if isinstance(j, int) else (j - u) * (8 * NS)

        stores = [16 * NS * ((NTL + 1 - u) // 2) for u in range(2)]

        with nc.Block() as block:

            @block.sync
            def _(sp):
                def body(j, u, i):
                    if R.capacity:
                        e = j
                    else:
                        e = sp.value_load(R.expert[0:1, bass.ds(j, 1)], min_val=0, max_val=NE - 1)
                    one = bass.ds(e, 1)
                    wait(sp, t_ready, j - 1)
                    for s, n in enumerate(R.sub):
                        sp.dma_start(xs[0:n, u, s, :], slots[bass.ds(j * S + s * SUB, n), :]).then_inc(x_in[u], 16)
                    wait(sp, y_ready, (j - 1) * NS)
                    for t, src in extra:
                        sp.dma_start(t[:, u, :], src[one].rearrange("e p m -> p (e m)")).then_inc(w_in[u], 16)
                    sp.dma_start(wu[:, u], w_up[one].rearrange("e (k p) n -> p (e k) n", p=128)).then_inc(w_in[u], 16)
                    if two:
                        sp.dma_start(wg[:, u], w_gate[one].rearrange("e (k p) n -> p (e k) n", p=128)).then_inc(w_in[u], 16)
                    sp.dma_start(wd[:, u], w_down[one].rearrange("e (k p) n -> p (e k) n", p=128)).then_inc(w_in[u], 16)
                    if bd is not None:
                        sp.dma_start(bd[:, u, :], b_down[one]).then_inc(w_in[u], 16)

                over_tiles(sp, NTL, body)

            @block.gpsimd
            def _(g):
                def body(j, u, i):
                    g.wait_ge(y_out, (j + 1) * NS)
                    for s, n in enumerate(R.sub):
                        g.dma_start(outs[bass.ds(j * S + s * SUB, n), :], ys[0:n, u, s, :]).then_inc(y_sent[u].sem, 16)

                over_tiles(g, NTL, body)
                for u in range(2):
                    g.wait_ge(y_sent[u].sem, y_sent[u].base + stores[u])

            @block.tensor
            def _(pe):
                def turn(j, u, i):
                    pe.wait_ge(x_in[u], i * (16 * NS) + 16 * NS)
                    wait(pe, t_out, j)
                    for k in range(KD):
                        for s, n in enumerate(R.sub):
                            last = pe.transpose(pt[:, k, s * SUB:s * SUB + n], xs[0:n, u, s, k * 128:(k + 1) * 128], ident[0:n, 0:n])
                    last.then_inc(t_ready, 1)

                def hidden(j, u, m):
                    wait(pe, h_out, j * NM + m - 1)
                    for c, w in enumerate((wu, wg)[0:1 + two]):
                        for k in range(KD):
                            last = pe.matmul(hb(j, u, m)[:, c * S:(c + 1) * S], w[:, u, k, m * 128:(m + 1) * 128], xT[:, u, k, :],
                                             start=k == 0, stop=k == KD - 1)
                    last.then_inc(h_ready, 1)

                def down(j, u):
                    pe.wait_ge(h_out, (j + 1) * NM)
                    for s, n in enumerate(R.sub):
                        wait(pe, y_out, (j - 1) * NS + s + 1 if NS > 1 else j - 1)
                        out = py[0:n, yb(u, s), 0:D]
                        for m in range(NM):
                            last = pe.matmul(out, hT[:, u, m, s * SUB:s * SUB + n], wd[:, u, m, :], start=m == 0,
                                             stop=m == NM - 1 and bd is None)
                        if bd is not None:
                            last = pe.matmul(out, ones[0:1, 0:n], bd[0:1, u, :], start=False, stop=True)
                        last.then_inc(y_ready, 1)

                def body(j, u, i):
                    turn(j, u, i)
                    if not (isinstance(j, int) and j == 0):
                        down(j - 1, 1 - u)
                    pe.wait_ge(t_out, j + 1)
                    pe.wait_ge(w_in[u], i * (16 * n_w) + 16 * n_w)
                    for m in range(NM):
                        hidden(j, u, m)

                over_tiles(pe, NTL, body)
                down(NTL - 1, (NTL - 1) % 2)

            @block.scalar
            def _(a):
                def body(j, u, i):
                    a.wait_ge(t_ready, j + 1)
                    for k in range(KD):
                        last = a.activation(xT[:, u, k, :], pt[:, k, 0:S], ACT.Copy)
                    last.then_inc(t_out, 1)
                    for m in range(NM):
                        up, gt = hb(j, u, m)[:, 0:S], hb(j, u, m)[:, S:2 * S] if two else None
                        a.wait_ge(h_ready, j * NM + m + 1)
                        if act == "relu":
                            a.activation(hT[:, u, m, :], up, ACT.Relu, bias=bu[:, u, m:m + 1]).then_inc(h_out, 1)
                        if act == "swiglu":
                            wait(a, h_out, j * NM + m - 1)
                            a.activation(hs[:, m % 2, :], gt, ACT.Silu).then_inc(h_half, 1)
                        if act == "silu_of_product":
                            wait(a, h_prod, j * NM + m - 1)
                            a.activation(hs[:, m % 2, :], gt, ACT.Identity, bias=bg[:, u, m:m + 1]).then_inc(h_half, 1)
                            a.wait_ge(h_prod, j * NM + m + 1)
                            a.activation(hT[:, u, m, :], hp[:, m % 2, :], ACT.Silu).then_inc(h_out, 1)

                over_tiles(a, NTL, body)

            @block.vector
            def _(v):
                def out(j, u):
                    if not (isinstance(j, int) and j < 2):
                        v.wait_ge(y_sent[u].sem, y_sent[u].base + y_sent_before(j, u))
                    for s, n in enumerate(R.sub):
                        v.wait_ge(y_ready, j * NS + s + 1)
                        v.tensor_copy(ys[0:n, u, s, :], py[0:n, yb(u, s), 0:D]).then_inc(y_out, 1)

                def body(j, u, i):
                    if not (isinstance(j, int) and j == 0):
                        out(j - 1, 1 - u)
                    for m in range(NM if two else 0):
                        up = hb(j, u, m)[:, 0:S]
                        v.wait_ge(h_half, j * NM + m + 1)
                        if act == "swiglu":
                            v.tensor_tensor(hT[:, u, m, :], up, hs[:, m % 2, :], ALU.mult).then_inc(h_out, 1)
                        if act == "silu_of_product":
                            wait(v, h_out, j * NM + m - 1)
                            v.scalar_tensor_tensor(hp[:, m % 2, :], up, bu[:, u, m:m + 1], hs[:, m % 2, :],
                                                   ALU.add, ALU.mult).then_inc(h_prod, 1)

                over_tiles(v, NTL, body)
                out(NTL - 1, (NTL - 1) % 2)

        for u in range(2):
            y_sent[u].base += stores[u]


def combine(nc, name, K, R, outs, acc, first):
    QB = 4
    with Phase(nc, name + "c") as p:
        y = p.sb("y", [T, NB, R.choices, D])
        got = K["rows_got"]
        step = p.sem("step")
        with nc.Block() as block:

            @block.gpsimd
            def _(g):
                for b in range(NB):
                    for k in range(R.choices):
                        g.indirect_dma_start(y[:, b, k, :], None, outs, bass.IndirectOffsetOnAxis(ap=R.get[:, k, b:b + 1], axis=0)).then_inc(got[b // QB].sem, 16)

            @block.vector
            def _(v):
                n = 0
                for b in range(NB):
                    if b % QB == 0:
                        got[b // QB].base += 16 * QB * R.choices
                        v.wait_ge(got[b // QB].sem, got[b // QB].base)
                    for k in range(R.choices):
                        w = R.wt[:, k, b:b + 1]
                        if k:
                            v.wait_ge(step, n)
                        n += 1
                        if first and k == 0:
                            v.tensor_scalar(acc[:, b, :], y[:, b, k, :], w, None, ALU.mult).then_inc(step, 1)
                        else:
                            v.scalar_tensor_tensor(acc[:, b, :], y[:, b, k, :], w, acc[:, b, :], ALU.mult, ALU.add).then_inc(step, 1)



CB = 4
NCH = NB // CB
CT = CB * T


def experts(nc, name, K, xnT_all, wts, acc, w_up, w_gate, w_down, b_up, b_gate, act, n_exp=NE):
    HID = w_up.shape[2]
    tiles = [min(128, HID - 128 * m) for m in range(-(-HID // 128))]
    NM = len(tiles)
    FULL = HID // 128
    two = w_gate is not None
    NHB = 2 if two else 1
    with Phase(nc, name + "e") as p:
        wu = p.sb("wu", [128, 2, KD, HID])
        wg = p.sb("wg", [128, 2, KD, HID]) if two else None
        wd = p.sb("wd", [128, 2, NM, D])
        bu = p.sb("bu", [128, 2, NM]) if b_up is not None else None
        bg = p.sb("bg", [128, 2, NM]) if b_gate is not None else None
        hT = p.sb("hT", [128, 2, NM, CT])
        hs = p.sb("hs", [128, 2, CT])
        hp = p.sb("hp", [128, 2, CT])
        ph = p.ps("ph", [128, 4, 512])
        py = p.ps("py", [128, 4, 512])
        HR = 2
        w_in = [p.sem(f"w_in{u}") for u in range(2)]
        h_ready = p.sem("h_ready")
        h_half = p.sem("h_half")
        h_prod = p.sem("h_prod")
        h_out = p.sem("h_out")
        y_ready = p.sem("y_ready")
        y_out = p.sem("y_out")
        n_w = 2 + two + (FULL < NM) + (b_up is not None) + (b_gate is not None)
        NPAIRE = max(1, n_exp // 2)

        def over_experts(eng, body):
            if n_exp == 1:
                for c in range(NCH):
                    body(0, 0, 0, c)
                return
            for u in range(2):
                for c in range(NCH):
                    body(u, u, 0, c)
            with eng.Fori(1, NPAIRE) as i:
                for u in range(2):
                    for c in range(NCH):
                        body(i * 2 + u, u, i, c)

        with nc.Block() as block:

            @block.sync
            def _(sp):
                def body(e, u, i, c):
                    if c:
                        return
                    wait(sp, y_ready, (e - 1) * NB)
                    one = bass.ds(e, 1)
                    for t, src in ((bu, b_up), (bg, b_gate)):
                        if t is not None:
                            sp.dma_start(t[:, u, :], src[one].rearrange("e p m -> p (e m)")).then_inc(w_in[u], 16)
                    sp.dma_start(wu[:, u], w_up[one].rearrange("e (k p) n -> p (e k) n", p=128)).then_inc(w_in[u], 16)
                    if two:
                        sp.dma_start(wg[:, u], w_gate[one].rearrange("e (k p) n -> p (e k) n", p=128)).then_inc(w_in[u], 16)
                    sp.dma_start(wd[:, u, 0:FULL, :], w_down[one, 0:FULL * 128, :].rearrange("e (k p) n -> p (e k) n", p=128)).then_inc(w_in[u], 16)
                    if FULL < NM:
                        sp.dma_start(wd[0:tiles[-1], u, FULL, :], w_down[one, FULL * 128:HID, :].rearrange("e p n -> p (e n)")).then_inc(w_in[u], 16)

                over_experts(sp, body)

            @block.tensor
            def _(pe):
                def hidden(e, u, i, c, m):
                    n = c * NM + m
                    wait(pe, h_out, reuse(e, n, NCH * NM, HR))
                    for w, k0 in ((wu, 0), (wg, 1))[0:NHB]:
                        bank = n % HR * 2 + k0
                        for k in range(KD):
                            last = pe.matmul(ph[0:tiles[m], bank, 0:CT], w[:, u, k, m * 128:m * 128 + tiles[m]],
                                             xnT_all[:, k, c * CT:(c + 1) * CT], start=k == 0, stop=k == KD - 1)
                    last.then_inc(h_ready, 1)

                def down(e, u, c, t):
                    n = c * CB + t
                    pe.wait_ge(h_out, e * (NCH * NM) + (c + 1) * NM)
                    wait(pe, y_out, reuse(e, n, NB, 4))
                    for m in range(NM):
                        last = pe.matmul(py[0:T, n % 4, 0:D], hT[0:tiles[m], c % 2, m, t * T:(t + 1) * T], wd[0:tiles[m], u, m, :],
                                         start=m == 0, stop=m == NM - 1)
                    last.then_inc(y_ready, 1)

                def body(e, u, i, c):
                    if c == 0:
                        pe.wait_ge(w_in[u], i * 16 * n_w + 16 * n_w)
                    for m in range(NM):
                        hidden(e, u, i, c, m)
                    if c:
                        for t in range(CB):
                            down(e, u, c - 1, t)
                    if c == NCH - 1:
                        for t in range(CB):
                            down(e, u, c, t)

                over_experts(pe, body)

            def bias(t, u, m):
                return t[0:tiles[m], u, m:m + 1]

            @block.scalar
            def _(a):
                def body(e, u, i, c):
                    for m in range(NM):
                        n, P = c * NM + m, tiles[m]
                        N = NCH * NM
                        up, gt = ph[0:P, n % HR * 2, 0:CT], ph[0:P, n % HR * 2 + 1, 0:CT]
                        a.wait_ge(h_ready, e * N + n + 1)
                        if m == 0:
                            wait(a, y_ready, reuse(e, c, NCH, 2) * CB)
                        if act == "relu":
                            a.activation(hT[0:P, c % 2, m, :], up, ACT.Relu, bias=bias(bu, u, m)).then_inc(h_out, 1)
                        if act == "swiglu":
                            wait(a, h_out, reuse(e, n, N, 2))
                            a.activation(hs[0:P, n % 2, :], gt, ACT.Silu).then_inc(h_half, 1)
                        if act == "silu_of_product":
                            wait(a, h_prod, reuse(e, n, N, 2))
                            a.activation(hs[0:P, n % 2, :], gt, ACT.Identity, bias=bias(bg, u, m)).then_inc(h_half, 1)
                            a.wait_ge(h_prod, e * N + n + 1)
                            a.activation(hT[0:P, c % 2, m, :], hp[0:P, n % 2, :], ACT.Silu).then_inc(h_out, 1)

                over_experts(a, body)

            @block.vector
            def _(v):
                N = NCH * NM

                def add(e, c, t):
                    n = c * CB + t
                    v.wait_ge(y_ready, e * NB + n + 1)
                    if wts is None:
                        v.tensor_tensor(batch(acc, n), batch(acc, n), py[0:T, n % 4, 0:D], ALU.add).then_inc(y_out, 1)
                    else:
                        v.scalar_tensor_tensor(batch(acc, n), py[0:T, n % 4, 0:D], wts[:, n, bass.ds(e, 1)],
                                               batch(acc, n), ALU.mult, ALU.add).then_inc(y_out, 1)

                def body(e, u, i, c):
                    for m in range(NM):
                        n, P = c * NM + m, tiles[m]
                        up = ph[0:P, n % HR * 2, 0:CT]
                        if act == "swiglu":
                            v.wait_ge(h_half, e * N + n + 1)
                            if m == 0:
                                wait(v, y_ready, reuse(e, c, NCH, 2) * CB)
                            v.tensor_tensor(hT[0:P, c % 2, m, :], up, hs[0:P, n % 2, :], ALU.mult).then_inc(h_out, 1)
                        if act == "silu_of_product":
                            v.wait_ge(h_half, e * N + n + 1)
                            wait(v, h_out, reuse(e, n, N, 2))
                            v.scalar_tensor_tensor(hp[0:P, n % 2, :], up, bias(bu, u, m), hs[0:P, n % 2, :],
                                                   ALU.add, ALU.mult).then_inc(h_prod, 1)
                    if c:
                        for t in range(CB):
                            add(e, c - 1, t)
                    if c == NCH - 1:
                        for t in range(CB):
                            add(e, c, t)

                over_experts(v, body)


def linear(nc, name, K, src, w, bias, dest):
    ident, ones = K["ident"], K["ones"]
    with Phase(nc, name) as p:
        w_sb, b_sb = p.sb("w", [128, KD, D]), p.sb("b", [1, D])
        w_hi, w_lo = p.sb("w_hi", [128, KD, D], F32R), p.sb("w_lo", [128, KD, D], F32R)
        st = p.sb("st", [T, 2, D])
        s_hi, s_lo = p.sb("s_hi", [128, 2, KD * T], F32R), p.sb("s_lo", [128, 2, KD * T], F32R)
        pt, py = p.ps("pt", [128, 2, 512]), p.ps("py", [128, 2, 512])
        loaded, w_steps, hi_ready, s_ready, t_ready, t_out, y_ready, y_out = (p.sem(s) for s in ("loaded", "w_steps", "hi_ready", "s_ready", "t_ready", "t_out", "y_ready", "y_out"))
        with nc.Block() as block:

            @block.sync
            def _(sp):
                sp.dma_start(w_sb[:], w.rearrange("(k p) n -> p k n", p=128)).then_inc(loaded, 16)
                sp.dma_start(b_sb[:], bias.rearrange("(a n) -> a n", a=1)).then_inc(loaded, 16)

            @block.tensor
            def _(pe):
                pe.wait_ge(loaded, 32)
                pe.wait_ge(w_steps, 2)

                def turn(b, u):
                    pe.wait_ge(s_ready, b + 1)
                    wait(pe, t_out, b - 1)
                    for k in range(KD):
                        last = pe.transpose(pt[:, u, k * T:(k + 1) * T], st[:, u, k * 128:(k + 1) * 128], ident[0:T, 0:T])
                    last.then_inc(t_ready, 1)

                def body(b, u, i):
                    if not is_static(b, NB - 1):
                        turn(b + 1, 1 - u)
                    pe.wait_ge(t_out, b + 1)
                    wait(pe, y_out, b - 1)
                    for k in range(KD):
                        cols = slice(k * T, (k + 1) * T)
                        for n, (a, b_) in enumerate(((s_hi, w_hi), (s_hi, w_lo), (s_lo, w_hi))):
                            pe.matmul(py[0:T, u, 0:D], a[:, u, cols], b_[:, k, :], start=k == 0 and n == 0, stop=False)
                    pe.matmul(py[0:T, u, 0:D], ones[0:1, 0:T], b_sb[0:1, :], start=False, stop=True).then_inc(y_ready, 1)

                turn(0, 0)
                over_batches_ahead(pe, body)

            @block.scalar
            def _(a):
                def body(b, u, i):
                    a.wait_ge(t_ready, b + 1)
                    wait(a, y_ready, b - 1)
                    a.activation(s_hi[:, u, :], pt[:, u, 0:KD * T], ACT.Copy).then_inc(hi_ready, 1)

                over_batches(a, body)

            @block.vector
            def _(v):
                def rows(b, u):
                    wait(v, t_ready, b - 1)
                    v.tensor_scalar(st[:, u, :], batch(src, b), 1.0, None, ALU.mult).then_inc(s_ready, 1)
                    v.wait_ge(hi_ready, b + 1)
                    wait(v, y_ready, b - 1)
                    v.tensor_tensor(s_lo[:, u, :], pt[:, u, 0:KD * T], s_hi[:, u, :].bitcast(F32), ALU.subtract).then_inc(t_out, 1)

                def body(b, u, i):
                    if not is_static(b, NB - 1):
                        rows(b + 1, 1 - u)
                    v.wait_ge(y_ready, b + 1)
                    v.tensor_tensor(batch(dest, b), batch(dest, b), py[0:T, u, 0:D], ALU.add).then_inc(y_out, 1)

                v.wait_ge(loaded, 32)
                v.tensor_copy(w_hi[:], w_sb[:]).then_inc(w_steps, 1)
                v.wait_ge(w_steps, 1)
                v.tensor_tensor(w_lo[:], w_sb[:], w_hi[:].bitcast(F32), ALU.subtract).then_inc(w_steps, 1)
                rows(0, 0)
                over_batches_ahead(v, body)


def add_all(nc, name, dest, src):
    with Phase(nc, name) as p:
        done = p.sem("done")
        with nc.Block() as block:

            @block.vector
            def _(v):
                v.tensor_tensor(dest[:], dest[:], src[:], ALU.add).then_inc(done, 1)



def constants(nc, x, x_dram, K, masks, slots):
    with Phase(nc, "init") as p:
        m1, m2 = p.sb("m1", [1, NB * SK], I32), p.sb("m2", [1, NB * SK], U8)
        fs = p.sb("fs", [1, NB * SK])
        zeros = p.sb("zeros", [128, D])
        half_done = p.sem("half_done")
        x_in, set_done, m_in, ready, ind, mk, z_set, z_out = (
            p.sem(s) for s in ("x_in", "set_done", "m_in", "ready", "ind", "mk", "z_set", "z_out"))
        if1, bk0, fside = masks
        with nc.Block() as block:

            @block.sync
            def _(sp):
                sp.dma_start(x[:], x_dram.rearrange("b t d -> t b d")).then_inc(x_in, 16)
                sp.dma_start(m1[:], if1.rearrange("b s -> (b s)").rearrange("(a n) -> a n", a=1)).then_inc(m_in, 16)
                sp.dma_start(m2[:], bk0.rearrange("b s -> (b s)").rearrange("(a n) -> a n", a=1)).then_inc(m_in, 16)
                sp.dma_start(fs[:], fside.rearrange("b s -> (b s)").rearrange("(a n) -> a n", a=1)).then_inc(m_in, 16)
                sp.wait_ge(z_set, 1)
                n = slots.shape[0] // 128
                sp.dma_start(slots.rearrange("(p n) d -> p n d", p=128), zeros[:].unsqueeze(1).broadcast_to([128, n, D])).then_inc(z_out, 16)
                sp.wait_ge(x_in, 16)
                sp.wait_ge(z_out, 16)

            @block.gpsimd
            def _(g):
                g.memset(K["ident"][:], 0.0).then_inc(set_done, 1)
                g.memset(K["upto"][:], 1.0).then_inc(set_done, 1)
                for name in ("sel", "sel_masked"):
                    g.memset(K[name][:], 1.0).then_inc(set_done, 1)
                g.wait_ge(set_done, 4)
                for name, groups in (("sel", GROUPS), ("sel_masked", MASKED_GROUPS)):
                    for h0, m in groups:
                        t = K[name][:, h0:h0 + m]
                        g.affine_select(out=t, in_=t, compare_op=ALU.is_ge, fill=0.0, base=0, pattern=[[-16, m]],
                                        channel_multiplier=1).then_inc(half_done, 1)
                g.wait_ge(half_done, len(GROUPS) + len(MASKED_GROUPS))
                for name, groups in (("sel", GROUPS), ("sel_masked", MASKED_GROUPS)):
                    for h0, m in groups:
                        t = K[name][:, h0:h0 + m]
                        g.affine_select(out=t, in_=t, compare_op=ALU.is_ge, fill=0.0, base=15, pattern=[[16, m]],
                                        channel_multiplier=-1).then_inc(ready, 1)
                g.affine_select(out=K["ident"][:], in_=K["ident"][:], compare_op=ALU.not_equal, fill=1.0, base=0,
                                pattern=[[-1, 128]], channel_multiplier=1).then_inc(ready, 1)
                g.affine_select(out=K["upto"][:], in_=K["upto"][:], compare_op=ALU.is_ge, fill=0.0, base=0,
                                pattern=[[1, 128]], channel_multiplier=-1).then_inc(ready, 1)

            @block.vector
            def _(v):
                v.memset(zeros[:], 0.0).then_inc(z_set, 1)
                v.memset(K["ones"][:], 1.0).then_inc(ind, 1)
                v.wait_ge(m_in, 48)
                v.tensor_scalar(K["mask_if1"][:], m1[:], 0.0, MASKED, ALU.is_equal, ALU.mult).then_inc(mk, 1)
                v.tensor_scalar(K["mask_bk0"][:], m2[:], 0.0, MASKED, ALU.is_equal, ALU.mult).then_inc(mk, 1)
                v.wait_ge(mk, 2)
                v.tensor_tensor(K["mask_bk0"][:], K["mask_bk0"][:], fs[:], ALU.add).then_inc(mk, 1)


def decoder(nc, A, out, last_stage=12):
    with ExitStack() as ctx:
        def sb(name, shape, dt=F32):
            return ctx.enter_context(nc.sbuf_tensor(name, shape, dt))

        x = sb("x", [T, NB, D])
        K = {"ident": sb("ident", [128, 128]), "upto": sb("upto", [128, 128]), "ones": sb("ones", [128, 128]),
             "sel": sb("sel", [128, 16]), "sel_masked": sb("sel_masked", [128, 16])}
        with ExitStack() as mctx:
            K["mask_if1"] = sb("mask_if1", [1, NB * SK])
            K["mask_bk0"] = sb("mask_bk0", [1, NB * SK])
        K["rows_sent"] = Kept(ctx, nc, "rows_sent")
        K["tile_stored"] = [Kept(ctx, nc, f"tile_stored{u}") for u in range(2)]
        K["rows_got"] = [Kept(ctx, nc, f"rows_got{q}") for q in range(4)]
        rows = (2 * NB * T + NE * (MOE_TILE - 1)) // MOE_TILE * MOE_TILE
        slots = nc.dram_tensor("slots", [rows, D], F32, kind="Internal").ap()
        outs = nc.dram_tensor("outs", [rows, D], F32, kind="Internal").ap()
        constants(nc, x, A["x"], K, (A["mask_BxS2_if1"], A["mask_BxS2_bk0"], A["fside_BxS2_0"]), slots)
        ctxT = A["ctxT"]

        def ffn(name, choices, S, capacity, first_wins, wg, bg, w_up, w_gate, w_down, b_up, b_gate, b_down, act, acc, first=False):
            with ExitStack() as c:
                R = Route(c, nc, name, choices, S, capacity)
                route(nc, name, x, K, R, first_wins, wg, bg, slots)
                routed_experts(nc, name, K, R, slots, outs, w_up, w_gate, w_down, b_up, b_gate, b_down, act)
                combine(nc, name, K, R, outs, acc, first)

        def stages():
            channel_attention(nc, x, K, A["L0_attn_w_qkv"], A["L0_attn_w_out"])
            yield
            attention(nc, "l0x", x, K, heads=16, dh=64, dv=64, wq=A["L0_xattn_Wq"], wk=A["L0_xattn_Wk"], wv=A["L0_xattn_Wv"],
                      scale=64 ** -0.5, ctxT=ctxT, wo=A["L0_xattn_Wo"], bo=A["L0_xattn_bo"])
            yield
            with nc.sbuf_tensor("mixed", [T, NB, D], F32) as y:
                ffn("l0f", 2, MOE_TILE, False, False, A["L0_ffn_Wg"], A["L0_ffn_bg"], A["L0_ffn_W1"], A["L0_ffn_W3"], A["L0_ffn_W2"],
                    A["L0_ffn_b1"], A["L0_ffn_b3"], A["L0_ffn_b2"], "silu_of_product", y, first=True)
                linear(nc, "l0w", K, y, A["L0_ffn_Wf"], A["L0_ffn_bf"], x)
            yield
            with nc.sbuf_tensor("inner", [T, NB, D], F32) as y:
                with nc.sbuf_tensor("offbias", [T, 16, T], F32) as bias:
                    scratch = nc.dram_tensor("bias_rows", [16, T, RELS], F32, kind="Internal").ap()
                    offset_bias(nc, bias, K, A["L1_attn_pos_bias"], A["L1_attn_offsets"], scratch)
                    attention(nc, "l1a", x, K, heads=16, dh=16, dv=16, wq=A["L1_q"], wk=A["L1_k"], wv=A["L1_v"], scale=0.25,
                              wo=A["L1_attn_w_out"], addend=bias, gate=(A["L1_attn_w_gate"], A["L1_attn_b_gate"]),
                              norm="ln_rms", norm_scale=A["L1_attn_norm1_scale"], y=y)
                with nc.sbuf_tensor("l1af_xT", [128, KD, NB * T], F32) as xnT_all:
                    normed_transposed(nc, "l1af", y, K, xnT_all, A["L1_attn_norm2_scale"])
                    experts(nc, "l1af", K, xnT_all, None, y, A["L1_up"], A["L1_gate"], A["L1_down"], None, None, "swiglu", n_exp=1)
                add_all(nc, "l1add", x, y)
            yield
            attention(nc, "l1x", x, K, heads=1, dh=256, dv=256, wq=A["L1_xattn_Wq"], wk=A["L1_xattn_Wk"], wv=A["L1_xattn_Wv"],
                      scale=D ** -0.5, ctxT=ctxT, bq=A["L1_xattn_bq"], bk=A["L1_xattn_bk"], bv=A["L1_xattn_bv"])
            yield
            ffn("l1f", 1, CAPACITY, True, True, A["L1_ffn_gate_w"], A["L1_ffn_gate_b"], A["L1_ffn_w1"], None, A["L1_ffn_w2"],
                A["L1_ffn_b1"], None, A["L1_ffn_b2"], "relu", x)
            yield
            scratch = nc.dram_tensor("rel_rows", [NB * 16, T, RELS], F32, kind="Internal").ap()
            relative_positions(nc, x, K, A["L2_q"], A["L2_bq"], A["L2_attn_Wr"], A["L2_attn_br"], scratch)
            attention(nc, "l2a", x, K, heads=16, dh=16, dv=16, wq=A["L2_q"], wk=A["L2_k"], wv=A["L2_v"], scale=0.25,
                      bq=A["L2_bq"], bk=A["L2_bk"], bv=A["L2_bv"], pos_dram=lambda b: skewed(scratch, b, 16))
            yield
            attention(nc, "l2x", x, K, heads=16, dh=16, dv=16, wq=A["L2_xattn_Wq"], wk=A["L2_xattn_Wk"], wv=A["L2_xattn_Wv"],
                      scale=0.25, ctxT=ctxT, bq=A["L2_xattn_bq"], bk=A["L2_xattn_bk"], bv=A["L2_xattn_bv"],
                      wo=A["L2_xattn_Wo"], bo=A["L2_xattn_bo"], maskrow=K["mask_if1"])
            yield
            ffn("l2f", 1, 128, False, True, A["L2_ffn_Wr"], A["L2_ffn_br"], A["L2_ffn_W1"], None, A["L2_ffn_W2"],
                A["L2_ffn_b1"], None, A["L2_ffn_b2"], "relu", x)
            yield
            attention(nc, "l3a", x, K, heads=1, dh=256, dv=256, wq=A["L3_attn_Wq"], wk=A["L3_attn_Wk"], wv=A["L3_attn_Wv"],
                      scale=D ** -0.5)
            yield
            attention(nc, "l3x", x, K, heads=16, dh=16, dv=16, wq=A["L3_q"], wk=A["L3_k"], wv=A["L3_v"], scale=0.25, ctxT=ctxT,
                      bq=A["L3_bq"], bk=A["L3_bk"], bv=A["L3_bv"], wo=A["L3_xattn_out_w"], bo=A["L3_xattn_out_b"],
                      maskrow=K["mask_bk0"])
            yield
            ffn("l3f", 2, MOE_TILE, False, True, A["L3_ffn_router_w"], None, A["L3_up"], A["L3_gate"], A["L3_ffn_w2"],
                None, None, None, "swiglu", x)
            yield

        for n, _ in enumerate(stages()):
            if n + 1 == last_stage:
                break

        with Phase(nc, "end") as p:
            stored = p.sem("stored")
            with nc.Block() as block:

                @block.sync
                def _(sp):
                    sp.dma_start(out.rearrange("b t d -> t b d"), x[:]).then_inc(stored, 16)
                    sp.wait_ge(stored, 16)



def layout(I):
    import numpy as np

    def c(a):
        return np.ascontiguousarray(a)

    def tile_bias(b):
        return c(b.reshape(b.shape[0], -1, 128).transpose(0, 2, 1))

    A = {k: I[k] for k in ("x", "fside_BxS2_0", "mask_BxS2_if1", "L0_xattn_bo", "L0_ffn_W1", "L0_ffn_W3", "L0_ffn_W2", "L0_ffn_b2",
                           "L0_ffn_Wg", "L0_ffn_bg", "L0_ffn_Wf", "L0_ffn_bf", "L1_attn_norm1_scale", "L1_attn_norm2_scale",
                           "L1_attn_w_out", "L1_attn_w_gate", "L1_attn_b_gate", "L1_attn_offsets", "L1_xattn_Wq", "L1_xattn_Wk",
                           "L1_xattn_Wv", "L1_xattn_bq", "L1_xattn_bk", "L1_xattn_bv", "L1_ffn_gate_b", "L1_ffn_w1", "L1_ffn_w2", "L1_ffn_b2", "L2_attn_br",
                           "L2_xattn_Wq", "L2_xattn_bq", "L2_xattn_Wk", "L2_xattn_bk", "L2_xattn_Wv", "L2_xattn_bv", "L2_xattn_Wo", "L2_xattn_bo", "L2_ffn_Wr", "L2_ffn_br", "L2_ffn_W1",
                           "L2_ffn_W2", "L2_ffn_b2", "L3_xattn_out_b")}
    A["mask_BxS2_bk0"] = I["mask_BxS2_bk0"]
    A["ctxT"] = c(I["ctx_1024"].transpose(0, 2, 1))
    for k in ("L0_attn_w_qkv", "L0_attn_w_out", "L0_xattn_Wq", "L0_xattn_Wk", "L0_xattn_Wv", "L0_xattn_Wo", "L1_attn_pos_bias",
              "L1_ffn_gate_w", "L2_attn_Wr", "L3_attn_Wq", "L3_attn_Wk", "L3_attn_Wv", "L3_xattn_out_w", "L3_ffn_router_w"):
        A[k] = c(I[k].T)
    for k in ("L0_ffn_b1", "L0_ffn_b3", "L1_ffn_b1", "L2_ffn_b1"):
        A[k] = tile_bias(I[k])
    w = I["L1_attn_w_qkv"]
    A["L1_q"], A["L1_k"], A["L1_v"] = w[:, :256], w[:, 256:512], w[:, 512:]
    A["L1_gate"], A["L1_up"], A["L1_down"] = I["L1_attn_w_ffn_gate"][None], I["L1_attn_w_ffn_up"][None], I["L1_attn_w_ffn_down"][None]
    w = I["L2_attn_Wqkv"].reshape(16, 3, 16, 256).transpose(1, 3, 0, 2).reshape(3, 256, 256)
    b = I["L2_attn_bqkv"].reshape(16, 3, 16).transpose(1, 0, 2).reshape(3, 256)
    A["L2_q"], A["L2_k"], A["L2_v"] = w
    A["L2_bq"], A["L2_bk"], A["L2_bv"] = b
    wkv, bkv = I["L3_xattn_Wkv_w"], I["L3_xattn_Wkv_b"]
    A["L3_q"], A["L3_k"], A["L3_v"] = I["L3_xattn_Wq_w"].T, wkv[:256].T, wkv[256:].T
    A["L3_bq"], A["L3_bk"], A["L3_bv"] = I["L3_xattn_Wq_b"], bkv[:256], bkv[256:]
    w = I["L3_ffn_w1"].transpose(0, 2, 1)
    A["L3_gate"], A["L3_up"] = c(w[:, :, :512]), c(w[:, :, 512:])
    A["L3_ffn_w2"] = c(I["L3_ffn_w2"].transpose(0, 2, 1))
    return {k: c(a) for k, a in A.items()}


def kernel(**inputs):
    import numpy as _np
    import concourse.bacc as _bacc
    from concourse import mybir as _mybir
    from concourse.bass_utils import run_bass_kernel_spmd as _run

    arrays = {f"in_{k}": a for k, a in layout({k: _np.asarray(v) for k, v in inputs.items()}).items()}
    nc = _bacc.Bacc("TRN2", target_bir_lowering=False, num_devices=1)
    A = {k[3:]: nc.dram_tensor(k, a.shape, _mybir.dt.from_np(a.dtype), kind="ExternalInput").ap() for k, a in arrays.items()}
    out = nc.dram_tensor("out_dram", (NB, T, D), F32, kind="ExternalOutput").ap()
    decoder(nc, A, out)
    r = _run(nc, [arrays], core_ids=[0])
    return r.results[0]["out_dram"]
```
